# Optimizing a Trainium2 kernel written in Bass

```python
import numpy as np
import jax
import jax.numpy as jnp

def _softmax(x, axis=-1):
    return jax.nn.softmax(x, axis=axis)

def _gelu(x):
    return jax.nn.gelu(x, approximate=True)

def _silu(x):
    return jax.nn.silu(x)

def _sigmoid(x):
    return jax.nn.sigmoid(x)

def _layernorm(x, axis=-1, eps=1e-05):
    m = jnp.mean(x, axis=axis, keepdims=True)
    v = jnp.var(x, axis=axis, keepdims=True)
    return (x - m) / jnp.sqrt(v + eps)

def _scatter_add(tgt, idx, src, axis=0):
    return tgt.at[idx].add(src)

def _segment_sum(src, seg, n):
    return jax.ops.segment_sum(src, seg, n)
kernel_name = 'mk_sandwich_d1_jaxref_r4_a33b64'

def setup_inputs(seed: int=0):
    np.random.seed(seed)
    _w = jnp.asarray

    def _L0_attn_setup():
        import jax, jax.numpy as jnp
        import numpy as np
        CHUNK = 64
        L2_EPS = 1e-06
        RMS_EPS = 1e-05

        def _silu(x):
            return x * jax.nn.sigmoid(x)

        def _causal_shared_conv(x, w):
            K = w.shape[0]
            T = x.shape[1]
            xp = jnp.pad(x, ((0, 0), (K - 1, 0), (0, 0)))
            out = w[0] * xp[:, 0:T, :]
            for j in range(1, K):
                out = out + w[j] * xp[:, j:j + T, :]
            return out

        def _l2norm(x):
            return x * jax.lax.rsqrt(jnp.sum(x * x, axis=-1, keepdims=True) + L2_EPS)

        def _delta_rule_chunk(q, k, v, beta, chunk=CHUNK):
            B, H, T, dk = q.shape
            dv = v.shape[-1]
            q = q * dk ** (-0.5)
            nC = T // chunk
            q = q.reshape(B, H, nC, chunk, dk)
            k = k.reshape(B, H, nC, chunk, dk)
            v = v.reshape(B, H, nC, chunk, dv)
            beta = beta.reshape(B, H, nC, chunk)
            k_beta = k * beta[..., None]
            v_beta = v * beta[..., None]
            A = jnp.einsum('bhncd,bhnmd->bhncm', k_beta, k)
            stril = jnp.tril(jnp.ones((chunk, chunk), bool), -1)
            M = jnp.where(stril, A, 0.0) + jnp.eye(chunk, dtype=q.dtype)
            u = jax.scipy.linalg.solve_triangular(M, v_beta, lower=True)
            w = jax.scipy.linalg.solve_triangular(M, k_beta, lower=True)
            tril_incl = jnp.tril(jnp.ones((chunk, chunk), bool))

            def step(S, inp):
                q_i, k_i, u_i, w_i = inp
                u_i = u_i - jnp.einsum('bhcd,bhde->bhce', w_i, S)
                attn = jnp.where(tril_incl, jnp.einsum('bhcd,bhmd->bhcm', q_i, k_i), 0.0)
                o_i = jnp.einsum('bhcd,bhde->bhce', q_i, S) + jnp.einsum('bhcm,bhme->bhce', attn, u_i)
                S = S + jnp.einsum('bhcd,bhce->bhde', k_i, u_i)
                return (S, o_i)
            xs = tuple((jnp.moveaxis(t, 2, 0) for t in (q, k, u, w)))
            S0 = jnp.zeros((B, H, dk, dv), q.dtype)
            _, o = jax.lax.scan(step, S0, xs)
            return jnp.moveaxis(o, 0, 2).reshape(B, H, T, dv)
        key = jax.random.key(seed)
        ks = jax.random.split(key, 10)
        B, T, D, H = (2, 1024, 512, 16)
        sc = 0.02
        return {'x': jax.random.normal(ks[0], (B, T, D), jnp.float32), 'Wq': jax.random.normal(ks[1], (D, D), jnp.float32) * sc, 'Wk': jax.random.normal(ks[2], (D, D), jnp.float32) * sc, 'Wv': jax.random.normal(ks[3], (D, D), jnp.float32) * sc, 'Wb': jax.random.normal(ks[4], (D, H), jnp.float32) * sc, 'Wo': jax.random.normal(ks[5], (D, D), jnp.float32) * sc, 'conv_q': jax.random.normal(ks[6], (4,), jnp.float32) * 0.5, 'conv_k': jax.random.normal(ks[7], (4,), jnp.float32) * 0.5, 'conv_v': jax.random.normal(ks[8], (4,), jnp.float32) * 0.5, 'onorm_w': jnp.ones((D // H,), jnp.float32)}
    _L0_attn_in = _L0_attn_setup()

    def _L0_ffn_setup():
        import math
        import jax, jax.numpy as jnp
        import numpy as np
        from jax import lax
        D = 512
        I = 256
        E = 32
        K = 4
        NG = 8
        TKG = 3
        NSH = 2
        SCALE = 2.5
        CF = 1.25
        B, S = (2, 512)

        def _router(x, router_w, e_bias):
            scores = jax.nn.sigmoid(x @ router_w.T)
            sc = scores + e_bias[None, :]
            T = x.shape[0]
            gs = sc.reshape(T, NG, E // NG)
            group_scores = lax.top_k(gs, 2)[0].sum(-1)
            _, gidx = lax.top_k(group_scores, TKG)
            gmask = jnp.zeros((T, NG), sc.dtype).at[jnp.arange(T)[:, None], gidx].set(1.0)
            smask = jnp.repeat(gmask, E // NG, axis=1)
            masked = jnp.where(smask > 0, sc, 0.0)
            _, topk_idx = lax.top_k(masked, K)
            topk_w = jnp.take_along_axis(scores, topk_idx, axis=1)
            topk_w = topk_w / (topk_w.sum(-1, keepdims=True) + 1e-20)
            topk_w = topk_w * SCALE
            return (topk_idx.astype(jnp.int32), topk_w)

        def _moe_forward(hidden_states, router_w, e_bias, W_gate, W_up, W_down, shared_gate, shared_up, shared_down):
            b, s, d = hidden_states.shape
            T = b * s
            C = int(math.ceil(CF * T / E))
            EC = E * C
            x = hidden_states.reshape(T, d)
            topk_idx, topk_w = _router(x, router_w, e_bias)
            expert_flat = topk_idx.reshape(-1)
            w_flat = topk_w.reshape(-1)
            tok_flat = jnp.repeat(jnp.arange(T, dtype=jnp.int32), K)
            sort_ix = jnp.argsort(expert_flat)
            e_sorted = expert_flat[sort_ix]
            tok_s = tok_flat[sort_ix]
            w_s = w_flat[sort_ix]
            counts = jnp.zeros(E, jnp.int32).at[e_sorted].add(1)
            group_start = jnp.concatenate([jnp.zeros(1, jnp.int32), jnp.cumsum(counts)[:-1].astype(jnp.int32)])
            pos = jnp.arange(T * K, dtype=jnp.int32) - group_start[e_sorted]
            valid = pos < C
            dest = e_sorted * C + jnp.where(valid, pos, 0)
            slots_token = jnp.zeros(EC, jnp.int32).at[dest].add(jnp.where(valid, tok_s, 0))
            slots_w = jnp.zeros(EC, w_s.dtype).at[dest].add(jnp.where(valid, w_s, 0.0))
            Xp = x[slots_token].reshape(E, C, d)
            G = jnp.einsum('ecd,edi->eci', Xp, W_gate)
            U = jnp.einsum('ecd,edi->eci', Xp, W_up)
            Y = jnp.einsum('eci,eid->ecd', jax.nn.silu(G) * U, W_down)
            Yf = Y.reshape(EC, d) * slots_w[:, None]
            out = jnp.zeros((T, d), x.dtype).at[slots_token].add(Yf)
            shared = jax.nn.silu(x @ shared_gate.T) * (x @ shared_up.T) @ shared_down.T
            return (out + shared).reshape(b, s, d)
        key = jax.random.key(seed)
        ks = jax.random.split(key, 8)

        def rn(k, shape, scale=0.02):
            return jax.random.normal(k, shape, jnp.float32) * scale
        return {'hidden_states': jax.random.normal(ks[0], (B, S, D), jnp.float32), 'router_w': rn(ks[1], (E, D)), 'e_bias': jnp.zeros((E,), jnp.float32), 'W_gate': rn(ks[2], (E, D, I)), 'W_up': rn(ks[3], (E, D, I)), 'W_down': rn(ks[4], (E, I, D)), 'shared_gate': rn(ks[5], (I * NSH, D)), 'shared_up': rn(ks[6], (I * NSH, D)), 'shared_down': rn(ks[7], (D, I * NSH))}
    _L0_ffn_in = _L0_ffn_setup()
    _d = {'L0_attn_x': _L0_attn_in['x'], 'L0_attn_Wq': _L0_attn_in['Wq'], 'L0_attn_Wk': _L0_attn_in['Wk'], 'L0_attn_Wv': _L0_attn_in['Wv'], 'L0_attn_Wb': _L0_attn_in['Wb'], 'L0_attn_Wo': _L0_attn_in['Wo'], 'L0_attn_conv_q': _L0_attn_in['conv_q'], 'L0_attn_conv_k': _L0_attn_in['conv_k'], 'L0_attn_conv_v': _L0_attn_in['conv_v'], 'L0_attn_onorm_w': _L0_attn_in['onorm_w'], 'L0_ffn_router_w': _L0_ffn_in['router_w'], 'L0_ffn_e_bias': _L0_ffn_in['e_bias'], 'L0_ffn_W_gate': _L0_ffn_in['W_gate'], 'L0_ffn_W_up': _L0_ffn_in['W_up'], 'L0_ffn_W_down': _L0_ffn_in['W_down'], 'L0_ffn_shared_gate': _L0_ffn_in['shared_gate'], 'L0_ffn_shared_up': _L0_ffn_in['shared_up'], 'L0_ffn_shared_down': _L0_ffn_in['shared_down']}
    _x0 = _d['L0_attn_x']
    _d['L0_attn_x'] = jax.random.normal(jax.random.fold_in(jax.random.key(seed), 1), (2, 1024, 512), dtype=_x0.dtype)
    del _x0
    return _d

def reference(L0_attn_x, L0_attn_Wq, L0_attn_Wk, L0_attn_Wv, L0_attn_Wb, L0_attn_Wo, L0_attn_conv_q, L0_attn_conv_k, L0_attn_conv_v, L0_attn_onorm_w, L0_ffn_router_w, L0_ffn_e_bias, L0_ffn_W_gate, L0_ffn_W_up, L0_ffn_W_down, L0_ffn_shared_gate, L0_ffn_shared_up, L0_ffn_shared_down):

    def _L0_attn_ref(x, Wq, Wk, Wv, Wb, Wo, conv_q, conv_k, conv_v, onorm_w):
        import jax, jax.numpy as jnp
        import numpy as np
        CHUNK = 64
        L2_EPS = 1e-06
        RMS_EPS = 1e-05

        def _silu(x):
            return x * jax.nn.sigmoid(x)

        def _causal_shared_conv(x, w):
            K = w.shape[0]
            T = x.shape[1]
            xp = jnp.pad(x, ((0, 0), (K - 1, 0), (0, 0)))
            out = w[0] * xp[:, 0:T, :]
            for j in range(1, K):
                out = out + w[j] * xp[:, j:j + T, :]
            return out

        def _l2norm(x):
            return x * jax.lax.rsqrt(jnp.sum(x * x, axis=-1, keepdims=True) + L2_EPS)

        def _delta_rule_chunk(q, k, v, beta, chunk=CHUNK):
            B, H, T, dk = q.shape
            dv = v.shape[-1]
            q = q * dk ** (-0.5)
            nC = T // chunk
            q = q.reshape(B, H, nC, chunk, dk)
            k = k.reshape(B, H, nC, chunk, dk)
            v = v.reshape(B, H, nC, chunk, dv)
            beta = beta.reshape(B, H, nC, chunk)
            k_beta = k * beta[..., None]
            v_beta = v * beta[..., None]
            A = jnp.einsum('bhncd,bhnmd->bhncm', k_beta, k)
            stril = jnp.tril(jnp.ones((chunk, chunk), bool), -1)
            M = jnp.where(stril, A, 0.0) + jnp.eye(chunk, dtype=q.dtype)
            u = jax.scipy.linalg.solve_triangular(M, v_beta, lower=True)
            w = jax.scipy.linalg.solve_triangular(M, k_beta, lower=True)
            tril_incl = jnp.tril(jnp.ones((chunk, chunk), bool))

            def step(S, inp):
                q_i, k_i, u_i, w_i = inp
                u_i = u_i - jnp.einsum('bhcd,bhde->bhce', w_i, S)
                attn = jnp.where(tril_incl, jnp.einsum('bhcd,bhmd->bhcm', q_i, k_i), 0.0)
                o_i = jnp.einsum('bhcd,bhde->bhce', q_i, S) + jnp.einsum('bhcm,bhme->bhce', attn, u_i)
                S = S + jnp.einsum('bhcd,bhce->bhde', k_i, u_i)
                return (S, o_i)
            xs = tuple((jnp.moveaxis(t, 2, 0) for t in (q, k, u, w)))
            S0 = jnp.zeros((B, H, dk, dv), q.dtype)
            _, o = jax.lax.scan(step, S0, xs)
            return jnp.moveaxis(o, 0, 2).reshape(B, H, T, dv)
        B, T, D = x.shape
        H = Wb.shape[1]
        dk = Wq.shape[1] // H
        dv = Wv.shape[1] // H
        q = _silu(_causal_shared_conv(x @ Wq, conv_q))
        k = _silu(_causal_shared_conv(x @ Wk, conv_k))
        v = _silu(_causal_shared_conv(x @ Wv, conv_v))
        beta = jax.nn.sigmoid(x @ Wb)
        qh = _l2norm(q.reshape(B, T, H, dk)).transpose(0, 2, 1, 3)
        kh = _l2norm(k.reshape(B, T, H, dk)).transpose(0, 2, 1, 3)
        vh = v.reshape(B, T, H, dv).transpose(0, 2, 1, 3)
        o = _delta_rule_chunk(qh, kh, vh, beta.transpose(0, 2, 1))
        o = o.transpose(0, 2, 1, 3)
        o = o * jax.lax.rsqrt(jnp.mean(o * o, axis=-1, keepdims=True) + RMS_EPS) * onorm_w
        return o.reshape(B, T, H * dv) @ Wo

    def _L0_ffn_ref(hidden_states, router_w, e_bias, W_gate, W_up, W_down, shared_gate, shared_up, shared_down):
        import math
        import jax, jax.numpy as jnp
        import numpy as np
        from jax import lax
        D = 512
        I = 256
        E = 32
        K = 4
        NG = 8
        TKG = 3
        NSH = 2
        SCALE = 2.5
        CF = 1.25
        B, S = (2, 512)

        def _router(x, router_w, e_bias):
            scores = jax.nn.sigmoid(x @ router_w.T)
            sc = scores + e_bias[None, :]
            T = x.shape[0]
            gs = sc.reshape(T, NG, E // NG)
            group_scores = lax.top_k(gs, 2)[0].sum(-1)
            _, gidx = lax.top_k(group_scores, TKG)
            gmask = jnp.zeros((T, NG), sc.dtype).at[jnp.arange(T)[:, None], gidx].set(1.0)
            smask = jnp.repeat(gmask, E // NG, axis=1)
            masked = jnp.where(smask > 0, sc, 0.0)
            _, topk_idx = lax.top_k(masked, K)
            topk_w = jnp.take_along_axis(scores, topk_idx, axis=1)
            topk_w = topk_w / (topk_w.sum(-1, keepdims=True) + 1e-20)
            topk_w = topk_w * SCALE
            return (topk_idx.astype(jnp.int32), topk_w)

        def _moe_forward(hidden_states, router_w, e_bias, W_gate, W_up, W_down, shared_gate, shared_up, shared_down):
            b, s, d = hidden_states.shape
            T = b * s
            C = int(math.ceil(CF * T / E))
            EC = E * C
            x = hidden_states.reshape(T, d)
            topk_idx, topk_w = _router(x, router_w, e_bias)
            expert_flat = topk_idx.reshape(-1)
            w_flat = topk_w.reshape(-1)
            tok_flat = jnp.repeat(jnp.arange(T, dtype=jnp.int32), K)
            sort_ix = jnp.argsort(expert_flat)
            e_sorted = expert_flat[sort_ix]
            tok_s = tok_flat[sort_ix]
            w_s = w_flat[sort_ix]
            counts = jnp.zeros(E, jnp.int32).at[e_sorted].add(1)
            group_start = jnp.concatenate([jnp.zeros(1, jnp.int32), jnp.cumsum(counts)[:-1].astype(jnp.int32)])
            pos = jnp.arange(T * K, dtype=jnp.int32) - group_start[e_sorted]
            valid = pos < C
            dest = e_sorted * C + jnp.where(valid, pos, 0)
            slots_token = jnp.zeros(EC, jnp.int32).at[dest].add(jnp.where(valid, tok_s, 0))
            slots_w = jnp.zeros(EC, w_s.dtype).at[dest].add(jnp.where(valid, w_s, 0.0))
            Xp = x[slots_token].reshape(E, C, d)
            G = jnp.einsum('ecd,edi->eci', Xp, W_gate)
            U = jnp.einsum('ecd,edi->eci', Xp, W_up)
            Y = jnp.einsum('eci,eid->ecd', jax.nn.silu(G) * U, W_down)
            Yf = Y.reshape(EC, d) * slots_w[:, None]
            out = jnp.zeros((T, d), x.dtype).at[slots_token].add(Yf)
            shared = jax.nn.silu(x @ shared_gate.T) * (x @ shared_up.T) @ shared_down.T
            return (out + shared).reshape(b, s, d)
        return _moe_forward(hidden_states, router_w, e_bias, W_gate, W_up, W_down, shared_gate, shared_up, shared_down)
    x = L0_attn_x
    x = x + _layernorm(_L0_attn_ref(_layernorm(x, axis=-1), L0_attn_Wq, L0_attn_Wk, L0_attn_Wv, L0_attn_Wb, L0_attn_Wo, L0_attn_conv_q, L0_attn_conv_k, L0_attn_conv_v, L0_attn_onorm_w), axis=-1)
    x = x + _layernorm(_L0_ffn_ref(_layernorm(x, axis=-1), L0_ffn_router_w, L0_ffn_e_bias, L0_ffn_W_gate, L0_ffn_W_up, L0_ffn_W_down, L0_ffn_shared_gate, L0_ffn_shared_up, L0_ffn_shared_down), axis=-1)
    return x

_drawn_inputs = setup_inputs


def setup_inputs(seed=0):
    import zlib

    import numpy as np

    out = dict(_drawn_inputs(seed))
    spreads = {'L0_attn_onorm_w': (1.0, 0.2), 'L0_ffn_e_bias': (0.0, 0.1)}
    factors = {}
    for name, (base, spread) in spreads.items():
        noise = np.random.default_rng([zlib.crc32(name.encode()), seed]).standard_normal(out[name].shape)
        drawn = base * np.exp(spread * noise) if base else spread * noise
        out[name] = jnp.asarray(drawn.astype(out[name].dtype))
    for name, factor in factors.items():
        out[name] = (out[name] * factor).astype(out[name].dtype)
    return out
```

```python
from contextlib import ExitStack

import concourse.bass as bass
from concourse import mybir

F32 = mybir.dt.float32
BF16 = mybir.dt.bfloat16
I32 = mybir.dt.int32
U32 = mybir.dt.uint32
ALU = mybir.AluOpType
ACT = mybir.ActivationFunctionType
AX_X = mybir.AxisListType.X

P = 128
B, SEQ, D = 2, 1024, 512
H, DK = 16, 32
TT = 128
STEPS = SEQ // TT
KT = D // P
CT = H * DK // P
HT = P // DK
CH = 32
J = TT // CH
COLS = B * TT
I8 = CT * B
G = I8 * J
TAPS = 4
HALO = TAPS - 1
NE, EI = 32, 256
NG, EG = 8, 4
TOPG, TOPK = 3, 4
SCALE = 2.5
NT = B * STEPS
NTOK = B * SEQ
CAP = -(-5 * NTOK // (4 * NE))
FF = 512
FT = FF // P
LN_EPS, L2_EPS, RMS_EPS = 1e-5, 1e-6, 1e-5

SMALL = 1 + 1 + HT + 3 + 4
RING = 6
JOBS_F, JOBS_C, JOBS_W, JOBS_T = 19, 6, 2, 9
JOBS = JOBS_F + JOBS_C + JOBS_W + JOBS_T
assert JOBS % RING == 0
TURNS = JOBS // RING


class Ring:

    def __init__(self, banks, filled, freed):
        self.banks, self.filled, self.freed = banks, filled, freed

    def bank(self, first, n):
        return self.banks[(first + n) % RING]

    def wait_free(self, pe, first, step, n):
        turn = (first + n) // RING
        if isinstance(step, int) and turn + TURNS * step == 0:
            return
        pe.wait_ge(self.freed[(first + n) % RING], step * TURNS + turn)

    def wait_full(self, eng, first, step, n):
        eng.wait_ge(self.filled[(first + n) % RING], step * TURNS + (first + n) // RING + 1)

    def full(self, first, n):
        return self.filled[(first + n) % RING]

    def free(self, first, n):
        return self.freed[(first + n) % RING]


def where(section, step, tail):
    if section == "F":
        return (0, 0) if isinstance(step, int) else (JOBS_C + JOBS_W + JOBS_F - JOBS, step)
    first = {"C": JOBS_F, "W": JOBS_F + JOBS_C, "T": JOBS_F + JOBS_C + JOBS_W + (0 if tail else JOBS_F)}[section]
    return first, step


def step_part(nc, ctx, dram, wring, route_m, route_w):
    def sb(name, shape, dt=F32):
        return ctx.enter_context(nc.sbuf_tensor(name, shape, dt))

    def sem(name):
        return ctx.enter_context(nc.semaphore(name))

    (x, Wq, Wk, Wv, Wb, Wo, conv_q, conv_k, conv_v, onorm_w, router_w, e_bias, W_gate, W_up, W_down,
     s_gate, s_up, s_down, x2_d, h_d, acc_d) = dram

    wqkv = wring[:, :].rearrange("p (s k n) -> p s k n", s=3, k=KT)
    wb = sb("wb", [P, KT, H])
    wo = sb("wo", [P, CT, D])
    wr = sb("wr", [P, KT, 4 * NE])
    sg_w = sb("sg_w", [P, KT, FF])
    su_w = sb("su_w", [P, KT, FF])
    sd_w = sb("sd_w", [P, FT, D])
    taps = sb("taps", [P, 3, TAPS])
    onw = sb("onw", [P, 1])
    ebias = sb("ebias", [P, NE])

    ident = sb("ident", [P, P])
    heads1 = sb("heads1", [P, P])
    headsm = sb("headsm", [P, P])
    spread = sb("spread", [H, CT, P])
    below = sb("below", [P, CH])
    upto = sb("upto", [P, CH])
    eps_ln = sb("eps_ln", [P, 1])
    eps_l2 = sb("eps_l2", [P, 1])
    eps_q = sb("eps_q", [P, 1])
    eps_rms = sb("eps_rms", [P, 1])
    iota_g = sb("iota_g", [P, NG])
    iota_e = sb("iota_e", [P, NE])

    x_in = sb("x_in", [P, B, D])
    x_res = sb("x_res", [P, B, D])
    stats = sb("stats", [P, B, 6])
    mv = sb("mv", [P, 3, B, 2])
    rs = sb("rs", [P, 3, B])
    xn = sb("xn", [P, B, D])
    xnT = sb("xnT", [P, KT, COLS])
    pre = sb("pre", [P, 3, I8, HALO + TT])
    cv = sb("cv", [P, 3, I8, TT])
    sig = sb("sig", [P, 3, I8 * TT])
    b16 = sb("b16", [H, COLS])
    kq = sb("kq", [P, G, 2, CH])
    beta = sb("beta", [P, G, CH])
    mbeta = sb("mbeta", [P, G, CH])
    k_tok = sb("k_tok", [P, G, DK])
    vk = sb("vk", [P, G, 2, DK])
    low = sig[:, 1, :].rearrange("p (g c) -> p g c", g=G)
    prod = sig[:, 0, :]
    lowp = sb("lowp", [P, CH, CH])
    inv = sb("inv", [P, CH, CH])
    invT = sb("invT", [P, G, CH])
    attnT = sb("attnT", [P, G, CH])
    uw = sb("uw", [P, J, I8, 2, DK])
    wT = sb("wT", [P, J, I8, CH])
    unew = sb("unew", [P, I8, DK])
    state = [sb(f"state{n}", [P, I8, DK]) for n in range(2)]
    o_ch = sb("o_ch", [P, I8, TT])
    o_r = sb("o_r", [P, I8 * TT])
    x2 = sb("x2", [P, B, D])
    h = sb("h", [P, B, D])
    hT = sb("hT", [P, KT, COLS])
    sh_g = cv[:, 0, :, :].rearrange("p i t -> p (i t)").rearrange("p (f c) -> p f c", f=FT)
    sh_u = cv[:, 1, :, :].rearrange("p i t -> p (i t)").rearrange("p (f c) -> p f c", f=FT)
    sh_s = cv[:, 2, :, :].rearrange("p i t -> p (i t)").rearrange("p (f c) -> p f c", f=FT)
    acc_sb = sb("acc_sb", [P, B, D])
    score = sb("score", [P, B, NE])
    sc = sb("sc", [P, B, NE])
    grp = sb("grp", [P, 4, B, NG, 2])
    gs = sb("gs", [P, B, NG])
    top = sb("top", [P, B, 2, 8])
    topi = sb("topi", [P, B, 2, 8], U32)
    topf = sb("topf", [P, B, 2, 8])
    gmask = sb("gmask", [P, B, NG])
    masked = sb("masked", [P, B, NE])
    picked = sb("picked", [P, B, NE])
    weigh = sb("weigh", [P, B, NE])
    wsum = sb("wsum", [P, B])

    banks = [ctx.enter_context(nc.psum_tensor(f"bank{n}", [P, 512], F32)) for n in range(8)]
    ring = Ring(banks[:RING], [sem(f"filled{n}") for n in range(RING)], [sem(f"freed{n}") for n in range(RING)])
    ps_ws, ps_o = banks[6], banks[7]

    consts = sem("consts")
    consts_go = sem("consts_go")
    proj_in = sem("proj_in")
    weights_in = sem("weights_in")
    small_in = sem("small_in")
    wo_scaled = sem("wo_scaled")
    x_loaded = sem("x_loaded")
    xres_loaded = sem("xres_loaded")
    x_used = sem("x_used")
    xres_used = sem("xres_used")
    stats_ready = [sem(f"stats_ready{n}") for n in range(3)]
    rs_ready = [sem(f"rs_ready{n}") for n in range(3)]
    xn_ready = sem("xn_ready")
    xnT_ready = sem("xnT_ready")
    beta_ready = sem("beta_ready")
    pre_ready = [sem(f"pre_ready{n}") for n in range(3)]
    conv_done = [sem(f"conv_done{n}") for n in range(3)]
    sig_ready = [sem(f"sig_ready{n}") for n in range(3)]
    act_ready = [sem(f"act_ready{n}") for n in range(3)]
    sq_ready = [sem(f"sq_ready{n}") for n in range(2)]
    norm_ready = [sem(f"norm_ready{n}") for n in range(2)]
    halo_done = sem("halo_done")
    kq_ready = sem("kq_ready")
    betaT_ready = sem("betaT_ready")
    mbeta_ready = sem("mbeta_ready")
    tok_ready = sem("tok_ready")
    vk_ready = sem("vk_ready")
    gram_read = sem("gram_read")
    inv_ready = sem("inv_ready")
    uw_ready = sem("uw_ready")
    wT_ready = sem("wT_ready")
    ws_done = sem("ws_done")
    unew_ready = sem("unew_ready")
    ds_done = sem("ds_done")
    state_ready = sem("state_ready")
    o_done = sem("o_done")
    o_out = sem("o_out")
    osq_ready = sem("osq_ready")
    onorm_ready = sem("onorm_ready")
    on_ready = sem("on_ready")
    h_ready = sem("h_ready")
    rows_out = sem("rows_out")
    hT_ready = sem("hT_ready")
    gate_sig = sem("gate_sig")
    up_out = sem("up_out")
    hid_ready = sem("hid_ready")
    acc_ready = sem("acc_ready")
    acc_out = sem("acc_out")
    score_ready = sem("score_ready")
    score_used = sem("score_used")
    dve_step = sem("dve_step")
    act_step = sem("act_step")
    pool_step = sem("pool_step")
    pe_passed = sem("pe_passed")
    zeros_out = sem("zeros_out")
    moe_in = sem("moe_in")

    def quad(n):
        return slice(DK * n, DK * n + DK)

    block = ctx.enter_context(nc.Block())

    @block.sync
    def _(sp):
        sp.dma_start(x_in[:, :, :], x[:, 0:TT, :].rearrange("b p d -> p b d")).then_inc(x_loaded, 16)
        small = [(wb[:, :, :], Wb.rearrange("(k p) n -> p k n", p=P)),
                 (ebias[:, :], e_bias.rearrange("(o n) -> o n", o=1).to_broadcast([P, NE]))]
        for n in range(HT):
            small.append((onw[quad(n), :], onorm_w.rearrange("(n o) -> n o", o=1)))
        for n, w in enumerate((conv_q, conv_k, conv_v)):
            small.append((taps[:, n, :], w.rearrange("(o n) -> o n", o=1).to_broadcast([P, TAPS])))
        for n in range(4):
            small.append((wr[:, :, NE * n:NE * n + NE], router_w.rearrange("(k p) e -> p k e", p=P)))
        for n, w in enumerate((Wk, Wq, Wv)):
            s = (1, 0, 2)[n]
            sp.dma_start(wqkv[:, s, :, :], w.rearrange("(k p) n -> p k n", p=P)).then_inc(proj_in, 16)
        for dst, src in small:
            sp.dma_start(dst, src).then_inc(small_in, 16)
        for dst, src in ((wo, Wo), (sg_w, s_gate), (su_w, s_up), (sd_w, s_down)):
            sp.dma_start(dst[:, :, :], src.rearrange("(k p) n -> p k n", p=P)).then_inc(weights_in, 16)
        assert len(small) == SMALL

        def load_x(s):
            sp.wait_ge(x_used, s)
            sp.dma_start(x_in[:, :, :], x.rearrange("b (t p) d -> t p b d", p=TT)[s]).then_inc(x_loaded, 16)

        def rows(s):
            if not (isinstance(s, int) and s == 0):
                sp.wait_ge(xres_used, s)
            sp.dma_start(x_res[:, :, :], x.rearrange("b (t p) d -> t p b d", p=TT)[s]).then_inc(xres_loaded, 16)
            sp.wait_ge(h_ready, s + 1)
            sp.dma_start(x2_d.rearrange("(b t p) d -> t p b d", p=TT, b=B)[s], x2[:, :, :]).then_inc(rows_out, 16)
            sp.dma_start(h_d[0:NTOK, :].rearrange("(b t p) d -> t p b d", p=TT, b=B)[s], h[:, :, :]).then_inc(rows_out, 16)

        def shared_out(s):
            sp.wait_ge(acc_ready, s + 1)
            sp.dma_start(acc_d[0:NTOK, :].rearrange("(b t p) d -> t p b d", p=TT, b=B)[s], acc_sb[:, :, :]).then_inc(acc_out, 16)

        load_x(1)
        with sp.Fori(1, STEPS - 1) as s:
            rows(s - 1)
            load_x(s + 1)
            shared_out(s - 1)
        rows(STEPS - 2)
        shared_out(STEPS - 2)
        rows(STEPS - 1)
        shared_out(STEPS - 1)
        sp.wait_ge(rows_out, 32 * STEPS)
        sp.wait_ge(acc_out, 16 * STEPS)
        sp.wait_ge(zeros_out, 32)

    @block.gpsimd
    def _(pool):
        g = nc.gpsimd
        g.memset(ident[:, :], 0.0)
        g.memset(heads1[:, :], 0.0)
        g.memset(headsm[:, :], 0.0)
        g.memset(spread[:, :, :], 1.0)
        g.memset(below[:, :], -1.0)
        g.memset(upto[:, :], 1.0)
        g.memset(inv[:, :, :], 0.0)
        g.memset(pre[:, :, :, 0:HALO], 0.0)
        g.memset(state[0][:, :, :], 0.0)
        g.memset(eps_ln[:, :], LN_EPS)
        g.memset(eps_l2[:, :], L2_EPS)
        g.memset(eps_q[:, :], L2_EPS * DK)
        g.memset(eps_rms[:, :], RMS_EPS)
        g.iota(iota_g[:, :], pattern=[[1, NG]], base=0, channel_multiplier=0, allow_small_or_imprecise_dtypes=True)
        g.iota(iota_e[:, :], pattern=[[1, NE]], base=0, channel_multiplier=0, allow_small_or_imprecise_dtypes=True)
        g.memset(acc_sb[:, :, :], 0.0).then_inc(consts_go, 1)
        pool.wait_ge(consts_go, 1)
        made = [1]

        def alone(ins):
            made[0] += 1
            ins.then_inc(consts_go, 1)
            pool.wait_ge(consts_go, made[0])

        for n in range(HT):
            alone(g.memset(heads1[quad(n), quad(n)], 1.0))
            alone(g.memset(headsm[quad(n), quad(n)], 1.0 / DK))
            alone(g.affine_select(out=below[quad(n), :], in_=below[quad(n), :], compare_op=ALU.is_gt, fill=0.0,
                                  base=0, pattern=[[-1, CH]], channel_multiplier=1))
            alone(g.affine_select(out=upto[quad(n), :], in_=upto[quad(n), :], compare_op=ALU.is_ge, fill=0.0,
                                  base=0, pattern=[[1, CH]], channel_multiplier=-1))
        g.affine_select(out=ident[:, :], in_=ident[:, :], compare_op=ALU.not_equal, fill=1.0,
                        base=0, pattern=[[-1, P]], channel_multiplier=1)
        g.affine_select(out=inv[:, :, :], in_=inv[:, :, :], compare_op=ALU.not_equal, fill=1.0,
                        base=0, pattern=[[1, CH], [-1, CH]], channel_multiplier=0)
        g.affine_select(out=spread[:, :, :].rearrange("h c (a d) -> h c a d", a=HT),
                        in_=spread[:, :, :].rearrange("h c (a d) -> h c a d", a=HT), compare_op=ALU.is_equal, fill=0.0,
                        base=0, pattern=[[-HT, CT], [-1, HT], [0, DK]], channel_multiplier=1).then_inc(consts, 1)
        pool.wait_ge(consts, 1)
        pool.dma_start(h_d[NTOK:NTOK + CAP, :], acc_sb[0:CAP, 0, :]).then_inc(zeros_out, 16)
        pool.dma_start(acc_d[NTOK:NTOK + CAP, :], acc_sb[0:CAP, 0, :]).then_inc(zeros_out, 16)

        def front(s):
            pool.wait_ge(betaT_ready, s + 1)
            if not (isinstance(s, int) and s == 0):
                pool.wait_ge(gram_read, s)
            g.tensor_tensor(mbeta[:, :, :], beta[:, :, :], below[:, :].rearrange("p (o c) -> p o c", o=1).to_broadcast([P, G, CH]), ALU.mult).then_inc(mbeta_ready, 1)
            pool.wait_ge(tok_ready, s + 1)
            g.tensor_tensor(vk[:, :, 0, :], vk[:, :, 0, :], beta[:, :, :], ALU.mult)
            g.tensor_tensor(vk[:, :, 1, :], k_tok[:, :, :], beta[:, :, :], ALU.mult).then_inc(vk_ready, 1)

        def shared(s):
            pool.wait_ge(gate_sig, s + 1)
            g.tensor_tensor(sh_g, sh_g, sh_s, ALU.mult).then_inc(pool_step, 1)
            pool.wait_ge(pool_step, 1)
            pool.wait_ge(up_out, s + 1)
            g.tensor_tensor(sh_g, sh_g, sh_u, ALU.mult).then_inc(hid_ready, 1)
            pool.sem_clear(pool_step)

        front(0)
        with pool.Fori(1, STEPS) as s:
            front(s)
            shared(s - 1)
        shared(STEPS - 1)

    @block.tensor
    def _(pe):
        te = nc.tensor

        def front(s, tail=False):
            first, st = where("F", s, tail)

            def start(n):
                ring.wait_free(pe, first, st, n)
                return ring.bank(first, n)

            pe.wait_ge(xn_ready, s + 1)
            pe.wait_ge(consts, 1)
            for n in range(2):
                bank = start(n)
                pe.sem_inc(pe_passed, 1)
                for k in range(2):
                    for b in range(B):
                        kt = 2 * n + k
                        m = te.transpose(bank[:, k * COLS + b * TT:k * COLS + (b + 1) * TT], xn[:, b, kt * P:(kt + 1) * P], ident[:, :])
                m.then_inc(ring.full(first, n), 1)
            pe.wait_ge(proj_in, 48)
            pe.wait_ge(small_in, 16 * SMALL)
            pe.wait_ge(xnT_ready, 2 * (s + 1))
            bank = start(2)
            for kt in range(KT):
                m = te.matmul(bank[0:H, 0:COLS], wb[:, kt, :], xnT[:, kt, :], start=(kt == 0), stop=(kt == KT - 1))
            m.then_inc(ring.full(first, 2), 1)
            for a, w in enumerate((1, 0, 2)):
                for half in range(2):
                    n = 3 + 2 * a + half
                    bank = start(n)
                    for c in range(2):
                        ct = 2 * half + c
                        for kt in range(KT):
                            m = te.matmul(bank[:, c * COLS:(c + 1) * COLS], wqkv[:, w, kt, ct * P:(ct + 1) * P], xnT[:, kt, :],
                                          start=(kt == 0), stop=(kt == KT - 1))
                    m.then_inc(ring.full(first, n), 1)
                if a == 1:
                    beta_spread(s, first, st)
            for a in range(2):
                pe.wait_ge(sq_ready[a], s + 1)
                for half in range(2):
                    n = 11 + 2 * a + half
                    bank = start(n)
                    for c in range(2):
                        m = te.matmul(bank[:, c * COLS:(c + 1) * COLS], heads1[:, :], sig[:, a, (2 * half + c) * COLS:(2 * half + c + 1) * COLS],
                                      start=True, stop=True)
                    m.then_inc(ring.full(first, n), 1)
            pe.wait_ge(kq_ready, 2 * (s + 1))
            for j in range(J):
                n = 15 + j
                bank = start(n)
                pe.sem_inc(pe_passed, 1)
                for i in range(I8):
                    for hh in range(HT):
                        m = te.matmul(bank[quad(hh), i * 64:(i + 1) * 64], kq[quad(hh), i * J + j, 0, :], kq[quad(hh), i * J + j, :, :].rearrange("p a c -> p (a c)"),
                                      start=True, stop=True)
                m.then_inc(ring.full(first, n), 1)

        def beta_spread(s, first, st):
            pe.wait_ge(beta_ready, s + 1)
            for half in range(2):
                n = 9 + half
                ring.wait_free(pe, first, st, n)
                bank = ring.bank(first, n)
                for c in range(2):
                    m = te.matmul(bank[:, c * COLS:(c + 1) * COLS], spread[:, 2 * half + c, :], b16[:, :], start=True, stop=True)
                m.then_inc(ring.full(first, n), 1)

        def core(s):
            first, st = where("C", s, False)
            pe.wait_ge(inv_ready, s + 1)
            pe.wait_ge(vk_ready, s + 1)
            for j in range(J):
                ring.wait_free(pe, first, st, j)
                bank = ring.bank(first, j)
                pe.sem_inc(pe_passed, 1)
                for i in range(I8):
                    for hh in range(HT):
                        m = te.matmul(bank[quad(hh), i * 64:(i + 1) * 64], invT[quad(hh), i * J + j, :], vk[quad(hh), i * J + j, :, :].rearrange("p a c -> p (a c)"),
                                      start=True, stop=True)
                m.then_inc(ring.full(first, j), 1)
            for j in range(J):
                now = state[j % 2]
                pe.wait_ge(wT_ready, J * s + j + 1)
                if not (isinstance(s, int) and s == 0 and j == 0):
                    pe.wait_ge(state_ready, J * s + j)
                pe.sem_inc(pe_passed, 1)
                for i in range(I8):
                    for hh in range(HT):
                        m = te.matmul(ps_ws[quad(hh), i * DK:(i + 1) * DK], wT[quad(hh), j, i, :], now[quad(hh), i, :], start=True, stop=True)
                m.then_inc(ws_done, 1)
                if not (isinstance(s, int) and s == 0 and j == 0):
                    pe.wait_ge(o_out, J * s + j)
                pe.sem_inc(pe_passed, 1)
                for i in range(I8):
                    for hh in range(HT):
                        te.matmul(ps_o[quad(hh), i * CH:(i + 1) * CH], now[quad(hh), i, :], kq[quad(hh), i * J + j, 1, :],
                                  start=(i == 0), stop=False, skip_group_check=True)
                pe.wait_ge(unew_ready, J * s + j + 1)
                pe.sem_inc(pe_passed, 1)
                for i in range(I8):
                    for hh in range(HT):
                        m = te.matmul(ps_ws[quad(hh), 256 + i * DK:256 + (i + 1) * DK], k_tok[quad(hh), i * J + j, :], unew[quad(hh), i, :], start=True, stop=True,
                                      skip_group_check=True)
                m.then_inc(ds_done, 1)
                for i in range(I8):
                    for hh in range(HT):
                        m = te.matmul(ps_o[quad(hh), i * CH:(i + 1) * CH], unew[quad(hh), i, :], attnT[quad(hh), i * J + j, :],
                                      start=False, stop=(i == I8 - 1), skip_group_check=True)
                m.then_inc(o_done, 1)
            pe.wait_ge(osq_ready, s + 1)
            for half in range(2):
                ring.wait_free(pe, first, st, J + half)
                bank = ring.bank(first, J + half)
                for c in range(2):
                    m = te.matmul(bank[:, c * COLS:(c + 1) * COLS], headsm[:, :], o_r[:, (2 * half + c) * COLS:(2 * half + c + 1) * COLS], start=True, stop=True)
                m.then_inc(ring.full(first, J + half), 1)

        def out_proj(s):
            first, st = where("W", s, False)
            pe.wait_ge(on_ready, s + 1)
            pe.wait_ge(wo_scaled, 1)
            for b in range(B):
                ring.wait_free(pe, first, st, b)
                bank = ring.bank(first, b)
                for ct in range(CT):
                    m = te.matmul(bank[:, :], o_ch[:, ct * B + b, :], wo[:, ct, :], start=(ct == 0), stop=(ct == CT - 1))
                m.then_inc(ring.full(first, b), 1)

        def tail_part(s, tail):
            first, st = where("T", s, tail)
            pe.wait_ge(h_ready, s + 1)
            for n in range(2):
                ring.wait_free(pe, first, st, n)
                bank = ring.bank(first, n)
                for k in range(2):
                    for b in range(B):
                        kt = 2 * n + k
                        m = te.transpose(bank[:, k * COLS + b * TT:k * COLS + (b + 1) * TT], h[:, b, kt * P:(kt + 1) * P], ident[:, :])
                m.then_inc(ring.full(first, n), 1)
            pe.wait_ge(hT_ready, 2 * (s + 1))
            ring.wait_free(pe, first, st, 2)
            bank = ring.bank(first, 2)
            for b in range(B):
                for kt in range(KT):
                    m = te.matmul(bank[:, b * P:(b + 1) * P], hT[:, kt, b * TT:(b + 1) * TT], wr[:, kt, :], start=(kt == 0), stop=(kt == KT - 1))
            m.then_inc(ring.full(first, 2), 1)
            pe.wait_ge(weights_in, 16 * 4)
            for a, w in enumerate((sg_w, su_w)):
                for half in range(2):
                    n = 3 + 2 * a + half
                    ring.wait_free(pe, first, st, n)
                    bank = ring.bank(first, n)
                    for c in range(2):
                        ft = 2 * half + c
                        for kt in range(KT):
                            m = te.matmul(bank[:, c * COLS:(c + 1) * COLS], w[:, kt, ft * P:(ft + 1) * P], hT[:, kt, :], start=(kt == 0), stop=(kt == KT - 1))
                    m.then_inc(ring.full(first, n), 1)
            pe.wait_ge(hid_ready, s + 1)
            for b in range(B):
                ring.wait_free(pe, first, st, 7 + b)
                bank = ring.bank(first, 7 + b)
                for ft in range(FT):
                    m = te.matmul(bank[:, :], sh_g[:, ft, b * TT:(b + 1) * TT], sd_w[:, ft, :], start=(ft == 0), stop=(ft == FT - 1))
                m.then_inc(ring.full(first, 7 + b), 1)

        front(0)
        with pe.Fori(1, STEPS) as s:
            core(s - 1)
            out_proj(s - 1)
            front(s)
            tail_part(s - 1, False)
        core(STEPS - 1)
        out_proj(STEPS - 1)
        tail_part(STEPS - 1, True)

    @block.scalar
    def _(act):
        sc_e = nc.scalar

        class Steps:
            count = 0

        def link(ins):
            Steps.count += 1
            ins.then_inc(act_step, 1)
            act.wait_ge(act_step, Steps.count)

        def end_steps():
            act.sem_clear(act_step)
            Steps.count = 0

        def rstd(n, s):
            act.wait_ge(stats_ready[n], s + 1)
            link(sc_e.activation(rs[:, n, :], mv[:, n, :, 1], ACT.Ln, bias=eps_ln[:, 0:1]))
            sc_e.activation(rs[:, n, :], rs[:, n, :], ACT.Exp, scale=-0.5).then_inc(rs_ready[n], 1)

        def sigmoid(dst, src, done=None):
            link(sc_e.activation(dst, src, ACT.Exp, scale=-1.0))
            link(sc_e.activation(dst, dst, ACT.Ln, bias=1.0))
            return sc_e.activation(dst, dst, ACT.Exp, scale=-1.0)

        def front(s):
            first, st = where("F", s, False)
            for n in range(2):
                ring.wait_full(act, first, st, n)
                link(sc_e.activation(xnT[:, 2 * n:2 * n + 2, :], ring.bank(first, n)[:, :].rearrange("p (k c) -> p k c", k=2), ACT.Copy))
                act.sem_inc(ring.free(first, n), 1)
                act.sem_inc(xnT_ready, 1)
            ring.wait_full(act, first, st, 2)
            link(sc_e.activation(b16[:, :], ring.bank(first, 2)[0:H, 0:COLS], ACT.Exp, scale=-1.0))
            act.sem_inc(ring.free(first, 2), 1)
            link(sc_e.activation(b16[:, :], b16[:, :], ACT.Ln, bias=1.0))
            sc_e.activation(b16[:, :], b16[:, :], ACT.Exp, scale=-1.0).then_inc(beta_ready, 1)

            def evacuate(a, w):
                if not (isinstance(s, int) and s == 0):
                    act.wait_ge(halo_done, 3 * (s - 1) + a + 1)
                for half in range(2):
                    n = 3 + 2 * a + half
                    ring.wait_full(act, first, st, n)
                    link(sc_e.activation(pre[:, w, 4 * half:4 * half + 4, HALO:], ring.bank(first, n)[:, :].rearrange("p (i t) -> p i t", t=TT), ACT.Copy))
                    act.sem_inc(ring.free(first, n), 1)
                act.sem_inc(pre_ready[w], 1)

            def silu_factor(a, w):
                act.wait_ge(conv_done[w], s + 1)
                slot = (1, 0, 2)[w]
                sigmoid(sig[:, slot, :], cv[:, w, :, :].rearrange("p i t -> p (i t)")).then_inc(sig_ready[w], 1)

            def square(a, w):
                act.wait_ge(act_ready[w], s + 1)
                sc_e.activation(sig[:, a, :], cv[:, w, :, :].rearrange("p i t -> p (i t)"), ACT.Square).then_inc(sq_ready[a], 1)

            def norms(a):
                for half in range(2):
                    n = 11 + 2 * a + half
                    part = sig[:, a, half * 512:(half + 1) * 512]
                    ring.wait_full(act, first, st, n)
                    link(sc_e.activation(part, ring.bank(first, n)[:, :], ACT.Ln, bias=(eps_l2, eps_q)[a][:, 0:1], scale=(1.0, float(DK))[a]))
                    act.sem_inc(ring.free(first, n), 1)
                    link(sc_e.activation(part, part, ACT.Exp, scale=-0.5))
                act.sem_inc(norm_ready[a], 1)

            evacuate(0, 1)
            evacuate(1, 0)
            silu_factor(0, 1)
            square(0, 1)
            evacuate(2, 2)
            silu_factor(1, 0)
            square(1, 0)
            norms(0)
            silu_factor(2, 2)
            norms(1)
            end_steps()

        def core(s):
            first, st = where("C", s, False)
            for j in range(J):
                ring.wait_full(act, first, st, j)
                m = sc_e.activation(uw[:, j, :, :, :].rearrange("p i a d -> p (i a d)"), ring.bank(first, j)[:, :], ACT.Copy)
                link(m)
                act.sem_inc(ring.free(first, j), 1)
                act.sem_inc(uw_ready, 1)
            for j in range(J):
                act.wait_ge(o_done, J * s + j + 1)
                link(sc_e.activation(o_ch[:, :, j * CH:(j + 1) * CH], ps_o[:, 0:I8 * CH].rearrange("p (i c) -> p i c", c=CH), ACT.Copy))
                act.sem_inc(o_out, 1)
            sc_e.activation(o_r[:, :], o_ch[:, :, :].rearrange("p i t -> p (i t)"), ACT.Square).then_inc(osq_ready, 1)
            for half in range(2):
                n = J + half
                part = o_r[:, half * 512:(half + 1) * 512]
                ring.wait_full(act, first, st, n)
                if half == 0:
                    ring.wait_full(act, first, st, n + 1)
                link(sc_e.activation(part, ring.bank(first, n)[:, :], ACT.Ln, bias=eps_rms[:, 0:1]))
                act.sem_inc(ring.free(first, n), 1)
                link(sc_e.activation(part, part, ACT.Exp, scale=-0.5))
            act.sem_inc(onorm_ready, 1)
            end_steps()

        def rows(s):
            rstd(1, s)
            rstd(2, s)
            end_steps()

        def tail_part(s, tail):
            first, st = where("T", s, tail)
            for n in range(2):
                ring.wait_full(act, first, st, n)
                link(sc_e.activation(hT[:, 2 * n:2 * n + 2, :], ring.bank(first, n)[:, :].rearrange("p (k c) -> p k c", k=2), ACT.Copy))
                act.sem_inc(ring.free(first, n), 1)
                act.sem_inc(hT_ready, 1)
            ring.wait_full(act, first, st, 2)
            if not (isinstance(s, int) and s == 0):
                act.wait_ge(score_used, s)
            link(sc_e.activation(score[:, :, :], ring.bank(first, 2)[:, 0:B * P].rearrange("p (b e) -> p b e", b=B)[:, :, 0:NE], ACT.Exp, scale=-1.0))
            act.sem_inc(ring.free(first, 2), 1)
            link(sc_e.activation(score[:, :, :], score[:, :, :], ACT.Ln, bias=1.0))
            sc_e.activation(score[:, :, :], score[:, :, :], ACT.Exp, scale=-1.0).then_inc(score_ready, 1)
            act.wait_ge(tok_ready, s + (1 if tail else 2))
            for half in range(2):
                n = 3 + half
                ring.wait_full(act, first, st, n)
                src = ring.bank(first, n)[:, :].rearrange("p (f c) -> p f c", f=2)
                sc_e.activation(sh_g[:, 2 * half:2 * half + 2, :], src, ACT.Copy)
                link(sc_e.activation(sh_s[:, 2 * half:2 * half + 2, :], src, ACT.Exp, scale=-1.0))
                act.sem_inc(ring.free(first, n), 1)
            link(sc_e.activation(sh_s, sh_s, ACT.Ln, bias=1.0))
            sc_e.activation(sh_s, sh_s, ACT.Exp, scale=-1.0).then_inc(gate_sig, 1)
            for half in range(2):
                n = 5 + half
                ring.wait_full(act, first, st, n)
                link(sc_e.activation(sh_u[:, 2 * half:2 * half + 2, :], ring.bank(first, n)[:, :].rearrange("p (f c) -> p f c", f=2), ACT.Copy))
                act.sem_inc(ring.free(first, n), 1)
            act.sem_inc(up_out, 1)
            if isinstance(s, int) and s == 0:
                act.wait_ge(zeros_out, 32)
            else:
                act.wait_ge(acc_out, 16 * s)
                act.wait_ge(zeros_out, 32)
            for b in range(B):
                n = 7 + b
                ring.wait_full(act, first, st, n)
                link(sc_e.activation(acc_sb[:, b, :], ring.bank(first, n)[:, :], ACT.Copy))
                act.sem_inc(ring.free(first, n), 1)
            act.sem_inc(acc_ready, 1)
            end_steps()

        act.wait_ge(consts, 1)
        rstd(0, 0)
        front(0)
        with act.Fori(1, STEPS) as s:
            rstd(0, s)
            core(s - 1)
            rows(s - 1)
            front(s)
            tail_part(s - 1, False)
        core(STEPS - 1)
        rows(STEPS - 1)
        tail_part(STEPS - 1, True)

    @block.vector
    def _(dve):
        v = nc.vector

        class Steps:
            count = 0

        def link(ins):
            Steps.count += 1
            ins.then_inc(dve_step, 1)
            dve.wait_ge(dve_step, Steps.count)

        def end_steps():
            dve.sem_clear(dve_step)
            Steps.count = 0

        def flat(ap):
            return ap.rearrange("p i t -> p (i t)")

        def moments(n, s, srcs):
            for b in range(B):
                last = v.bn_stats(stats[:, b, :], srcs[b])
            link(last)
            for b in range(B):
                last = v.bn_aggr(mv[:, n, b, :], stats[:, b, :])
            last.then_inc(stats_ready[n], 1)

        def first_norm(s):
            dve.wait_ge(x_loaded, 16 * (s + 1))
            if not (isinstance(s, int) and s == 0):
                dve.wait_ge(xnT_ready, 2 * s)
            moments(0, s, [x_in[:, b, :] for b in range(B)])
            dve.wait_ge(rs_ready[0], s + 1)
            for b in range(B):
                last = v.tensor_scalar(xn[:, b, :], x_in[:, b, :], mv[:, 0, b, 0:1], rs[:, 0, b:b + 1], ALU.subtract, ALU.mult)
            link(last)
            dve.sem_inc(xn_ready, 1)
            dve.sem_inc(x_used, 1)

        def conv(a, w, s):
            dve.wait_ge(pre_ready[w], s + 1)
            out = cv[:, w, :, :]
            link(v.tensor_scalar(out, pre[:, w, :, 0:TT], taps[:, w, 0:1], None, ALU.mult))
            for n in range(1, TAPS):
                link(v.scalar_tensor_tensor(out=out, in0=pre[:, w, :, n:n + TT], scalar=taps[:, w, n:n + 1], in1=out, op0=ALU.mult, op1=ALU.add))
            dve.sem_inc(conv_done[w], 1)
            link(v.tensor_copy(pre[:, w, :, 0:HALO], pre[:, w, :, TT:TT + HALO]))
            dve.sem_inc(halo_done, 1)

        def silu(w, s):
            slot = (1, 0, 2)[w]
            dve.wait_ge(sig_ready[w], s + 1)
            link(v.tensor_tensor(flat(cv[:, w, :, :]), flat(cv[:, w, :, :]), sig[:, slot, :], ALU.mult))
            dve.sem_inc(act_ready[w], 1)

        def normalise(a, w, s):
            dve.wait_ge(norm_ready[a], s + 1)
            link(v.tensor_tensor(kq[:, :, a, :], flat(cv[:, w, :, :]).rearrange("p (g c) -> p g c", c=CH), sig[:, a, :].rearrange("p (g c) -> p g c", c=CH), ALU.mult))
            dve.sem_inc(kq_ready, 1)

        def front(s):
            first, st = where("F", s, False)
            if isinstance(s, int) and s == 0:
                dve.wait_ge(small_in, 16 * SMALL)
            if not (isinstance(s, int) and s == 0):
                ok = s - 1
                if not isinstance(ok, int) or ok > 0:
                    dve.wait_ge(acc_ready, ok)
            conv(0, 1, s)
            conv(1, 0, s)
            silu(1, s)
            for half in range(2):
                n = 9 + half
                ring.wait_full(dve, first, st, n)
                link(v.transpose(beta[:, half * 16:(half + 1) * 16, :].rearrange("p g c -> p (g c)"), ring.bank(first, n)[:, :]))
                dve.sem_inc(ring.free(first, n), 1)
            dve.sem_inc(betaT_ready, 1)
            silu(0, s)
            normalise(0, 1, s)
            link(v.transpose(k_tok[:, :, :], kq[:, :, 0, :]))
            conv(2, 2, s)
            normalise(1, 0, s)
            silu(2, s)
            link(v.transpose(vk[:, :, 0, :], flat(cv[:, 2, :, :]).rearrange("p (g c) -> p g c", c=CH)))
            dve.sem_inc(tok_ready, 1)
            dve.wait_ge(mbeta_ready, s + 1)
            for j in range(J):
                n = 15 + j
                ring.wait_full(dve, first, st, n)
                bank = ring.bank(first, n)[:, :].rearrange("p (i a c) -> p i a c", i=I8, a=2)
                v.tensor_tensor(low.rearrange("p (i j) c -> p j i c", j=J)[:, j], bank[:, :, 0, :], mbeta[:, :, :].rearrange("p (i j) c -> p j i c", j=J)[:, j], ALU.mult)
                link(v.tensor_tensor(attnT[:, :, :].rearrange("p (i j) c -> p j i c", j=J)[:, j], bank[:, :, 1, :],
                                     upto[:, :].rearrange("p (o c) -> p o c", o=1).to_broadcast([P, I8, CH]), ALU.mult))
                dve.sem_inc(ring.free(first, n), 1)
            dve.sem_inc(gram_read, 1)
            link(v.transpose(lowp[:, :, :].rearrange("p c m -> p m c"), low.rearrange("p g m -> p m g")))
            invc = inv[:, :, :].rearrange("p j k -> p k j")
            for i in range(1, CH):
                t = prod[:, 0:i * i].rearrange("p (k j) -> p k j", k=i)
                link(v.tensor_tensor(t, invc[:, 0:i, 0:i], lowp[:, i:i + 1, 0:i].to_broadcast([P, i, i]), ALU.mult))
                link(v.tensor_reduce(inv[:, i, 0:i], t, AX_X, ALU.add))
            link(v.transpose(invT[:, :, :].rearrange("p g c -> p c g"), inv[:, :, :]))
            dve.sem_inc(inv_ready, 1)
            end_steps()

        def core(s):
            for j in range(J):
                dve.wait_ge(uw_ready, J * s + j + 1)
                v.transpose(wT[:, j, :, :], uw[:, j, :, 1, :]).then_inc(wT_ready, 1)
            for j in range(J):
                now, new = state[j % 2], state[(j + 1) % 2]
                dve.wait_ge(ws_done, J * s + j + 1)
                v.tensor_tensor(unew[:, :, :], uw[:, j, :, 0, :], ps_ws[:, 0:256].rearrange("p (i d) -> p i d", d=DK), ALU.subtract).then_inc(unew_ready, 1)
                dve.wait_ge(ds_done, J * s + j + 1)
                v.tensor_tensor(new[:, :, :], now[:, :, :], ps_ws[:, 256:512].rearrange("p (i d) -> p i d", d=DK), ALU.add).then_inc(state_ready, 1)
            dve.wait_ge(onorm_ready, s + 1)
            v.tensor_tensor(flat(o_ch[:, :, :]), flat(o_ch[:, :, :]), o_r[:, :], ALU.mult).then_inc(on_ready, 1)

        def rows(s):
            first, st = where("W", s, False)
            for b in range(B):
                ring.wait_full(dve, first, st, b)
            ys = [ring.bank(first, b)[:, :] for b in range(B)]
            moments(1, s, ys)
            dve.wait_ge(rs_ready[1], s + 1)
            dve.wait_ge(xres_loaded, 16 * (s + 1))
            if not (isinstance(s, int) and s == 0):
                dve.wait_ge(rows_out, 32 * s)
            for b in range(B):
                link(v.tensor_scalar(x2[:, b, :], ys[b], mv[:, 1, b, 0:1], rs[:, 1, b:b + 1], ALU.subtract, ALU.mult))
                dve.sem_inc(ring.free(first, b), 1)
            link(v.tensor_tensor(x2[:, :, :], x2[:, :, :], x_res[:, :, :], ALU.add))
            dve.sem_inc(xres_used, 1)
            moments(2, s, [x2[:, b, :] for b in range(B)])
            dve.wait_ge(rs_ready[2], s + 1)
            for b in range(B):
                last = v.tensor_scalar(h[:, b, :], x2[:, b, :], mv[:, 2, b, 0:1], rs[:, 2, b:b + 1], ALU.subtract, ALU.mult)
            last.then_inc(h_ready, 1)
            end_steps()

        def one_hot(dst, index, iota, n, count):
            for b in range(B):
                for k in range(count):
                    if k == 0:
                        link(v.tensor_scalar(dst[:, b, :], iota[:, :], index[:, b, n, k:k + 1], None, ALU.is_equal))
                    else:
                        link(v.scalar_tensor_tensor(out=dst[:, b, :], in0=iota[:, :], scalar=index[:, b, n, k:k + 1], in1=dst[:, b, :], op0=ALU.is_equal, op1=ALU.add))

        def route(s):
            dve.wait_ge(score_ready, s + 1)
            for b in range(B):
                last = v.tensor_tensor(sc[:, b, :], score[:, b, :], ebias[:, :], ALU.add)
            link(last)
            four = sc[:, :, :].rearrange("p b (g e) -> p b g e", e=EG)
            v.tensor_tensor(grp[:, 0, :, :, :], four[:, :, :, 0:2], four[:, :, :, 2:4], ALU.max)
            link(v.tensor_tensor(grp[:, 1, :, :, :], four[:, :, :, 0:2], four[:, :, :, 2:4], ALU.min))
            hi, lo = grp[:, 0], grp[:, 1]
            v.tensor_tensor(grp[:, 2, :, :, 0], hi[:, :, :, 0], hi[:, :, :, 1], ALU.max)
            v.tensor_tensor(grp[:, 2, :, :, 1], hi[:, :, :, 0], hi[:, :, :, 1], ALU.min)
            link(v.tensor_tensor(grp[:, 3, :, :, 0], lo[:, :, :, 0], lo[:, :, :, 1], ALU.max))
            link(v.tensor_tensor(grp[:, 3, :, :, 1], grp[:, 2, :, :, 1], grp[:, 3, :, :, 0], ALU.max))
            link(v.tensor_tensor(gs[:, :, :], grp[:, 2, :, :, 0], grp[:, 3, :, :, 1], ALU.add))
            for b in range(B):
                link(v.max(top[:, b, 0, :], gs[:, b, :]))
                link(v.max_index(topi[:, b, 0, :], top[:, b, 0, :], gs[:, b, :]))
                link(v.tensor_copy(topf[:, b, 0, :], topi[:, b, 0, :]))
            one_hot(gmask, topf, iota_g, 0, TOPG)
            link(v.tensor_tensor(masked[:, :, :].rearrange("p b (g e) -> p b g e", e=EG), four,
                                 gmask[:, :, :].rearrange("p b (g o) -> p b g o", o=1).to_broadcast([P, B, NG, EG]), ALU.mult))
            for b in range(B):
                link(v.max(top[:, b, 1, :], masked[:, b, :]))
                link(v.max_index(topi[:, b, 1, :], top[:, b, 1, :], masked[:, b, :]))
                link(v.tensor_copy(topf[:, b, 1, :], topi[:, b, 1, :]))
            one_hot(picked, topf, iota_e, 1, TOPK)
            link(v.tensor_tensor(weigh[:, :, :], picked[:, :, :], score[:, :, :], ALU.mult))
            dve.sem_inc(score_used, 1)
            link(v.tensor_reduce(wsum[:, :], weigh[:, :, :], AX_X, ALU.add))
            link(v.tensor_scalar(wsum[:, :], wsum[:, :], 1e-20, None, ALU.add))
            link(v.reciprocal(wsum[:, :], wsum[:, :]))
            for b in range(B):
                v.tensor_scalar(route_w[:, b, s, :], weigh[:, b, :], wsum[:, b:b + 1], SCALE, ALU.mult, ALU.mult)
                last = v.tensor_copy(route_m[:, b, s, :], picked[:, b, :])
            link(last)
            end_steps()

        dve.wait_ge(consts, 1)
        first_norm(0)
        dve.wait_ge(weights_in, 16 * 4)
        dve.wait_ge(small_in, 16 * SMALL)
        for ct in range(CT):
            last = v.tensor_scalar(wo[:, ct, :], wo[:, ct, :], onw[:, 0:1], None, ALU.mult)
        last.then_inc(wo_scaled, 1)
        front(0)
        with dve.Fori(1, STEPS) as s:
            first_norm(s)
            core(s - 1)
            rows(s - 1)
            front(s)
            route(s - 1)
        core(STEPS - 1)
        rows(STEPS - 1)
        route(STEPS - 1)





def expert_part(nc, ctx, dram, wring, route_m, route_w):
    def sb(name, shape, dt=F32):
        return ctx.enter_context(nc.sbuf_tensor(name, shape, dt))

    def sem(name):
        return ctx.enter_context(nc.semaphore(name))

    W_gate, W_up, W_down, x2_d, h_d, acc_d, out = dram
    PARTS = 6
    weights = wring[:, :].rearrange("p (q n) -> p q n", q=2)
    w_gate = [weights[:, q, 0:1024].rearrange("p (k i) -> p k i", k=KT) for q in range(2)]
    w_up = [weights[:, q, 1024:2048].rearrange("p (k i) -> p k i", k=KT) for q in range(2)]
    w_down = [weights[:, q, 2048:3072].rearrange("p (k d) -> p k d", k=2) for q in range(2)]

    ident = sb("ident2", [P, P])
    before = sb("before", [P, P], BF16)
    ones = sb("ones", [P, P], BF16)
    mask16 = sb("mask16", [P, NT * NE], BF16)
    place = sb("place", [P, NT, NE])
    carry = sb("carry", [P, NT, NE])
    slot16 = sb("slot16", [P, NE, NT], BF16)
    slots_i = sb("slots_i", [P, CAP], BF16)
    hot = [sb(f"hot{q}", [P, NT, CAP], BF16) for q in range(2)]
    facts = sb("facts", [P, NE, NT, PARTS], BF16)
    rest = sb("rest", [P, NT, NE])
    spare = sb("spare", [P, 1])
    table = sb("table", [P, NE, PARTS])
    row_f = sb("row_f", [P, NE])
    tmp_f = sb("tmp_f", [P, NE])
    row_i = sb("row_i", [P, NE], I32)
    slot_w = sb("slot_w", [P, NE])
    gidx = [sb(f"gidx{q}", [P, 1], I32) for q in range(2)]
    sidx = [sb(f"sidx{q}", [P, 1], I32) for q in range(2)]
    xg = [sb(f"xg{q}", [P, D]) for q in range(2)]
    xgT = [sb(f"xgT{q}", [P, KT, P]) for q in range(2)]
    sg = [sb(f"sg{q}", [P, 2, CAP]) for q in range(2)]
    hid = [sb(f"hid{q}", [P, 2, CAP]) for q in range(2)]
    ys = [sb(f"ys{q}", [P, D]) for q in range(2)]
    a_in = [sb(f"a_in{q}", [P, B, D]) for q in range(2)]
    r_in = [sb(f"r_in{q}", [P, B, D]) for q in range(2)]
    z_st = [sb(f"z_st{q}", [P, B, 6]) for q in range(2)]
    z_mv = [sb(f"z_mv{q}", [P, B, 2]) for q in range(2)]
    z_rs = [sb(f"z_rs{q}", [P, B]) for q in range(2)]
    eps = sb("eps_last", [P, 1])

    ps_x = [ctx.enter_context(nc.psum_tensor(f"ps_x{q}", [P, 512], F32)) for q in range(2)]
    ps_g = [ctx.enter_context(nc.psum_tensor(f"ps_g{q}", [P, 512], F32)) for q in range(2)]
    ps_y = [ctx.enter_context(nc.psum_tensor(f"ps_y{q}", [P, 512], F32)) for q in range(2)]
    ps_p = ctx.enter_context(nc.psum_tensor("ps_p", [P, 512], F32))
    ps_t = ctx.enter_context(nc.psum_tensor("ps_t", [P, 512], F32))

    filled2 = sem("e_filled")
    consts2 = sem("e_consts")
    mask_ready = sem("mask_ready")
    counted = sem("counted")
    facts_ready = sem("facts_ready")
    hot_ready = sem("hot_ready")
    table_done = sem("table_done")
    rows_ready = sem("rows_ready")
    w_in = [sem(f"w_in{q}") for q in range(2)]
    w_used = [sem(f"w_used{q}") for q in range(2)]
    gidx_ready = sem("gidx_ready")
    gathered = [sem(f"gathered{q}") for q in range(2)]
    turned = [sem(f"turned{q}") for q in range(2)]
    xgT_ready = [sem(f"xgT_ready{q}") for q in range(2)]
    gu_done = [sem(f"gu_done{q}") for q in range(2)]
    sg_ready = [sem(f"sg_ready{q}") for q in range(2)]
    gated = [sem(f"gated{q}") for q in range(2)]
    hid_ready = [sem(f"hid_ready{q}") for q in range(2)]
    y_done = [sem(f"y_done{q}") for q in range(2)]
    ys_ready = [sem(f"ys_ready{q}") for q in range(2)]
    sidx_ready = sem("sidx_ready")
    added = sem("added")
    z_in = [sem(f"z_in{q}") for q in range(2)]
    z_stats = [sem(f"z_stats{q}") for q in range(2)]
    z_rstd = [sem(f"z_rstd{q}") for q in range(2)]
    z_done = [sem(f"z_done{q}") for q in range(2)]
    z_out = [sem(f"z_out{q}") for q in range(2)]
    dve_chain = sem("dve_chain")
    act_chain = sem("act_chain")
    pool_passed = sem("pool_passed")

    block = ctx.enter_context(nc.Block())
    PAIRS = NE // 2
    ZP = STEPS // 2
    acc_t = acc_d[0:NTOK, :].rearrange("(t b p) d -> t p b d", p=P, b=B)
    x2_t = x2_d.rearrange("(t b p) d -> t p b d", p=P, b=B)
    out_t = out.rearrange("b (t p) d -> (b t) p d", p=P).rearrange("(t b) p d -> t p b d", b=B)

    @block.sync
    def _(sp):
        def load(e, q):
            sp.dma_start(w_gate[q], W_gate.rearrange("e (k p) i -> e p k i", p=P)[e]).then_inc(w_in[q], 16)
            sp.dma_start(w_up[q], W_up.rearrange("e (k p) i -> e p k i", p=P)[e]).then_inc(w_in[q], 16)
            sp.dma_start(w_down[q], W_down.rearrange("e (k p) d -> e p k d", p=P)[e]).then_inc(w_in[q], 16)

        def z_load(n, q):
            sp.dma_start(a_in[q][:, :, :], acc_t[n]).then_inc(z_in[q], 16)
            sp.dma_start(r_in[q][:, :, :], x2_t[n]).then_inc(z_in[q], 16)

        def z_store(n, r, q):
            sp.wait_ge(z_done[q], r + 1)
            sp.dma_start(out_t[n], a_in[q][:, :, :]).then_inc(z_out[q], 16)

        for q in range(2):
            load(q, q)
        with sp.Fori(1, PAIRS) as r:
            for q in range(2):
                sp.wait_ge(w_used[q], r)
                load(2 * r + q, q)
        sp.wait_ge(added, 16 * NE)
        for q in range(2):
            z_load(q, q)
        with sp.Fori(1, ZP) as r:
            for q in range(2):
                z_store(2 * (r - 1) + q, r - 1, q)
                sp.wait_ge(z_out[q], 16 * r)
                z_load(2 * r + q, q)
        for q in range(2):
            z_store(2 * (ZP - 1) + q, ZP - 1, q)
        for q in range(2):
            sp.wait_ge(z_out[q], 16 * ZP)

    @block.gpsimd
    def _(pool):
        g = nc.gpsimd
        g.memset(ident[:, :], 0.0)
        g.memset(before[:, :], 1.0)
        g.memset(ones[:, :], 1.0)
        for q in range(2):
            g.memset(xgT[q][:, :, :], 0.0)
        g.memset(eps[:, :], LN_EPS)
        g.memset(carry[:, :, :], 0.0)
        g.memset(facts[:, :, :, 5], 1.0)
        g.iota(slots_i[:, :], pattern=[[1, CAP]], base=0, channel_multiplier=0, allow_small_or_imprecise_dtypes=True)
        g.iota(spare[:, :], pattern=[[0, 1]], base=NTOK, channel_multiplier=1, allow_small_or_imprecise_dtypes=True)
        g.iota(facts[:, :, :, 3], pattern=[[0, NE], [1, NT]], base=0, channel_multiplier=0, allow_small_or_imprecise_dtypes=True)
        g.iota(facts[:, :, :, 4], pattern=[[0, NE], [0, NT]], base=0, channel_multiplier=1, allow_small_or_imprecise_dtypes=True).then_inc(filled2, 1)
        pool.wait_ge(filled2, 1)
        g.affine_select(out=ident[:, :], in_=ident[:, :], compare_op=ALU.not_equal, fill=1.0,
                        base=0, pattern=[[-1, P]], channel_multiplier=1)
        g.affine_select(out=before[:, :], in_=before[:, :], compare_op=ALU.is_gt, fill=0.0,
                        base=0, pattern=[[1, P]], channel_multiplier=-1).then_inc(consts2, 1)

        def gather(e, r, q):
            if not (isinstance(r, int) and r == 0):
                pool.wait_ge(turned[q], r)
            g.tensor_copy(gidx[q][0:CAP, :], row_i[0:CAP, bass.ds(e, 1)]).then_inc(gidx_ready, 1)
            pool.wait_ge(gidx_ready, 2 * r + q + 1)
            pool.sem_inc(pool_passed, 1)
            g.indirect_dma_start(out=xg[q][0:CAP, :], out_offset=None, in_=h_d[:, :],
                                 in_offset=bass.IndirectOffsetOnAxis(ap=gidx[q][0:CAP, 0:1], axis=0)).then_inc(gathered[q], 16)

        def scatter(e, r, q):
            if not (isinstance(r, int) and r == 0 and q == 0):
                pool.wait_ge(added, 16 * (2 * r + q))
            g.tensor_copy(sidx[q][0:CAP, :], row_i[0:CAP, bass.ds(e, 1)]).then_inc(sidx_ready, 1)
            pool.wait_ge(sidx_ready, 2 * r + q + 1)
            pool.wait_ge(ys_ready[q], r + 1)
            pool.sem_inc(pool_passed, 1)
            g.indirect_dma_start(out=acc_d[:, :], out_offset=bass.IndirectOffsetOnAxis(ap=sidx[q][0:CAP, 0:1], axis=0),
                                 in_=ys[q][0:CAP, :], in_offset=None, compute_op=ALU.add).then_inc(added, 16)

        pool.wait_ge(rows_ready, 1)
        for q in range(2):
            gather(q, 0, q)
        with pool.Fori(0, PAIRS - 1) as r:
            for q in range(2):
                gather(2 * r + q + 2, r + 1, q)
                scatter(2 * r + q, r, q)
        for q in range(2):
            scatter(NE - 2 + q, PAIRS - 1, q)

    @block.tensor
    def _(pe):
        te = nc.tensor
        pe.wait_ge(consts2, 1)
        pe.wait_ge(mask_ready, 1)
        te.matmul(ps_p[:, :], before[:, :], mask16[:, :], start=True, stop=True)
        te.matmul(ps_t[:, :], ones[:, :], mask16[:, :], start=True, stop=True).then_inc(counted, 1)
        pe.wait_ge(facts_ready, 1)
        with pe.Fori(0, PAIRS) as r:
            for q in range(2):
                pe.wait_ge(hot_ready, 2 * r + q + 1)
                for t in range(NT):
                    m = te.matmul(ps_p[0:CAP, bass.ds(r * 2 * PARTS + q * PARTS, PARTS)], hot[q][:, t, :], facts[:, 2 * r + q, t, :],
                                  start=(t == 0), stop=(t == NT - 1), skip_group_check=True)
                m.then_inc(table_done, 1)

        def up(r, q):
            pe.wait_ge(gathered[q], 16 * (r + 1))
            if not (isinstance(r, int) and r == 0):
                pe.wait_ge(xgT_ready[q], r)
            for k in range(KT):
                m = te.transpose(ps_x[q][:, k * P:k * P + CAP], xg[q][0:CAP, k * P:(k + 1) * P], ident[0:CAP, 0:CAP])
            m.then_inc(turned[q], 1)
            pe.wait_ge(w_in[q], 48 * (r + 1))
            pe.wait_ge(xgT_ready[q], r + 1)
            if not (isinstance(r, int) and r == 0):
                pe.wait_ge(hid_ready[q], r)
            for a, w in enumerate((w_gate[q], w_up[q])):
                for i in range(2):
                    for k in range(KT):
                        m = te.matmul(ps_g[q][:, (2 * a + i) * P:(2 * a + i + 1) * P], w[:, k, i * P:(i + 1) * P], xgT[q][:, k, :],
                                      start=(k == 0), stop=(k == KT - 1))
            m.then_inc(gu_done[q], 1)

        def down(r, q):
            pe.wait_ge(hid_ready[q], r + 1)
            if not (isinstance(r, int) and r == 0):
                pe.wait_ge(ys_ready[q], r)
            for i in range(2):
                m = te.matmul(ps_y[q][0:CAP, :], hid[q][:, i, :], w_down[q][:, i, :], start=(i == 0), stop=(i == 1))
            m.then_inc(y_done[q], 1)
            pe.wait_ge(y_done[q], r + 1)
            pe.sem_inc(w_used[q], 1)

        up(0, 0)
        up(0, 1)
        down(0, 0)
        with pe.Fori(1, PAIRS) as r:
            up(r, 0)
            down(r - 1, 1)
            up(r, 1)
            down(r, 0)
        down(PAIRS - 1, 1)

    @block.scalar
    def _(act):
        sc_e = nc.scalar

        def expert(r, q):
            act.wait_ge(turned[q], r + 1)
            if not (isinstance(r, int) and r == 0):
                act.wait_ge(gu_done[q], r)
            sc_e.activation(xgT[q][:, :, 0:CAP], ps_x[q][:, :].rearrange("p (k c) -> p k c", k=KT)[:, :, 0:CAP], ACT.Copy).then_inc(xgT_ready[q], 1)

        def gate(r, q):
            act.wait_ge(gu_done[q], r + 1)
            sc_e.activation(sg[q][:, :, :], ps_g[q][:, 0:2 * P].rearrange("p (i c) -> p i c", i=2)[:, :, 0:CAP], ACT.Exp, scale=-1.0).then_inc(act_chain, 1)
            act.wait_ge(act_chain, 1)
            sc_e.activation(sg[q][:, :, :], sg[q][:, :, :], ACT.Ln, bias=1.0).then_inc(act_chain, 1)
            act.wait_ge(act_chain, 2)
            act.sem_clear(act_chain)
            sc_e.activation(sg[q][:, :, :], sg[q][:, :, :], ACT.Exp, scale=-1.0).then_inc(sg_ready[q], 1)

        act.wait_ge(consts2, 1)
        expert(0, 0)
        expert(0, 1)
        gate(0, 0)
        with act.Fori(1, PAIRS) as r:
            gate(r - 1, 1)
            expert(r, 0)
            expert(r, 1)
            gate(r, 0)
        gate(PAIRS - 1, 1)
        with act.Fori(0, ZP) as r:
            for q in range(2):
                act.wait_ge(z_stats[q], r + 1)
                sc_e.activation(z_rs[q][:, :], z_mv[q][:, :, 1], ACT.Ln, bias=eps[:, 0:1]).then_inc(act_chain, 1)
                act.wait_ge(act_chain, 1)
                act.sem_clear(act_chain)
                sc_e.activation(z_rs[q][:, :], z_rs[q][:, :], ACT.Exp, scale=-0.5).then_inc(z_rstd[q], 1)

    @block.vector
    def _(dve):
        v = nc.vector

        class Steps:
            count = 0

        def link(ins):
            Steps.count += 1
            ins.then_inc(dve_chain, 1)
            dve.wait_ge(dve_chain, Steps.count)

        def end_steps():
            dve.sem_clear(dve_chain)
            Steps.count = 0

        dve.wait_ge(consts2, 1)
        mask = route_m[:, :, :, :].rearrange("p b t e -> p (b t) e")
        w32 = route_w[:, :, :, :].rearrange("p b t e -> p (b t) e")
        v.tensor_copy(mask16[:, :], mask.rearrange("p t e -> p (t e)")).then_inc(mask_ready, 1)
        by_e = facts[:, :, :, :].rearrange("p e t k -> p k t e")
        link(v.tensor_copy(by_e[:, 0], w32))
        link(v.tensor_tensor(rest[:, :, :], w32, by_e[:, 0], ALU.subtract))
        link(v.tensor_copy(by_e[:, 1], rest[:, :, :]))
        link(v.tensor_tensor(rest[:, :, :], rest[:, :, :], by_e[:, 1], ALU.subtract))
        link(v.tensor_copy(by_e[:, 2], rest[:, :, :]))
        dve.sem_inc(facts_ready, 1)
        dve.wait_ge(counted, 1)
        for t in range(1, NT):
            link(v.tensor_tensor(carry[:, t, :], carry[:, t - 1, :], ps_t[:, (t - 1) * NE:t * NE], ALU.add))
        link(v.tensor_tensor(place[:, :, :], ps_p[:, :].rearrange("p (t e) -> p t e", e=NE), carry[:, :, :], ALU.add))
        link(v.tensor_scalar(place[:, :, :], place[:, :, :], float(P - 1), float(P - 1), ALU.min, ALU.subtract))
        link(v.tensor_tensor(place[:, :, :], place[:, :, :], mask, ALU.mult))
        link(v.tensor_scalar(slot16[:, :, :].rearrange("p e t -> p t e"), place[:, :, :], float(P - 1), None, ALU.add))
        end_steps()
        with dve.Fori(0, PAIRS) as r:
            for q in range(2):
                if q == 0:
                    dve.wait_ge(table_done, 2 * r)
                v.tensor_tensor(hot[q][:, :, :], slot16[:, 2 * r + q, :].rearrange("p (t o) -> p t o", o=1).to_broadcast([P, NT, CAP]),
                                slots_i[:, :].rearrange("p (o c) -> p o c", o=1).to_broadcast([P, NT, CAP]), ALU.is_equal).then_inc(hot_ready, 1)
        dve.wait_ge(table_done, NE)
        link(v.tensor_copy(table[0:CAP, :, :], ps_p[0:CAP, 0:NE * PARTS].rearrange("p (e k) -> p e k", k=PARTS)))
        t_ = table[0:CAP, :, :]
        link(v.scalar_tensor_tensor(out=row_f[0:CAP, :], in0=t_[:, :, 3], scalar=float(P), in1=t_[:, :, 4], op0=ALU.mult, op1=ALU.add))
        link(v.tensor_scalar(tmp_f[0:CAP, :], t_[:, :, 5], -1.0, 1.0, ALU.mult, ALU.add))
        link(v.scalar_tensor_tensor(out=row_f[0:CAP, :], in0=tmp_f[0:CAP, :], scalar=spare[0:CAP, 0:1], in1=row_f[0:CAP, :], op0=ALU.mult, op1=ALU.add))
        v.tensor_copy(row_i[0:CAP, :], row_f[0:CAP, :]).then_inc(rows_ready, 1)
        link(v.tensor_tensor(slot_w[0:CAP, :], t_[:, :, 1], t_[:, :, 2], ALU.add))
        link(v.tensor_tensor(slot_w[0:CAP, :], slot_w[0:CAP, :], t_[:, :, 0], ALU.add))
        end_steps()

        def gate(r, q):
            dve.wait_ge(sg_ready[q], r + 1)
            if not (isinstance(r, int) and r == 0):
                dve.wait_ge(y_done[q], r)
            gates = ps_g[q][:, :].rearrange("p (a i c) -> p a i c", a=2, i=2)[:, :, :, 0:CAP]
            v.tensor_tensor(hid[q][:, :, :], gates[:, 0], sg[q][:, :, :], ALU.mult).then_inc(gated[q], 1)
            dve.wait_ge(gated[q], r + 1)
            v.tensor_tensor(hid[q][:, :, :], gates[:, 1], hid[q][:, :, :], ALU.mult).then_inc(hid_ready[q], 1)

        def weigh(e, r, q):
            dve.wait_ge(y_done[q], r + 1)
            if not (isinstance(r, int) and r == 0):
                dve.wait_ge(added, 16 * (2 * r + q - 1))
            v.tensor_scalar(ys[q][0:CAP, :], ps_y[q][0:CAP, :], slot_w[0:CAP, bass.ds(e, 1)], None, ALU.mult).then_inc(ys_ready[q], 1)

        gate(0, 0)

        def pair(r):
            gate(r - 1, 1)
            weigh(2 * (r - 1), r - 1, 0)
            gate(r, 0)
            weigh(2 * (r - 1) + 1, r - 1, 1)

        pair(1)
        with dve.Fori(2, PAIRS) as r:
            pair(r)
        gate(PAIRS - 1, 1)
        weigh(NE - 2, PAIRS - 1, 0)
        weigh(NE - 1, PAIRS - 1, 1)

        with dve.Fori(0, ZP) as r:
            for q in range(2):
                dve.wait_ge(z_in[q], 32 * (r + 1))
                for b in range(B):
                    last = v.bn_stats(z_st[q][:, b, :], a_in[q][:, b, :])
                link(last)
                for b in range(B):
                    last = v.bn_aggr(z_mv[q][:, b, :], z_st[q][:, b, :])
                last.then_inc(z_stats[q], 1)
                dve.wait_ge(z_rstd[q], r + 1)
                for b in range(B):
                    last = v.tensor_scalar(a_in[q][:, b, :], a_in[q][:, b, :], z_mv[q][:, b, 0:1], z_rs[q][:, b:b + 1], ALU.subtract, ALU.mult)
                link(last)
                v.tensor_tensor(a_in[q][:, :, :], a_in[q][:, :, :], r_in[q][:, :, :], ALU.add).then_inc(z_done[q], 1)
            end_steps()


def delta_moe_layer(nc, x, Wq, Wk, Wv, Wb, Wo, conv_q, conv_k, conv_v, onorm_w, router_w, e_bias,
                    W_gate, W_up, W_down, s_gate, s_up, s_down, out):
    x2_d = nc.dram_tensor("x2_rows", [NTOK, D], F32, kind="Internal").ap()
    h_d = nc.dram_tensor("h_rows", [NTOK + CAP, D], F32, kind="Internal").ap()
    acc_d = nc.dram_tensor("moe_rows", [NTOK + CAP, D], F32, kind="Internal").ap()
    with nc.sbuf_tensor("wring", [P, 2 * 3 * 1024], F32) as wring, \
            nc.sbuf_tensor("route_m", [P, B, STEPS, NE], F32) as route_m, \
            nc.sbuf_tensor("route_w", [P, B, STEPS, NE], F32) as route_w:
        with ExitStack() as ctx:
            step_part(nc, ctx, (x, Wq, Wk, Wv, Wb, Wo, conv_q, conv_k, conv_v, onorm_w, router_w, e_bias,
                                W_gate, W_up, W_down, s_gate, s_up, s_down, x2_d, h_d, acc_d), wring, route_m, route_w)
        with ExitStack() as ctx:
            expert_part(nc, ctx, (W_gate, W_up, W_down, x2_d, h_d, acc_d, out), wring, route_m, route_w)


_INS = ["attn_x", "attn_Wq", "attn_Wk", "attn_Wv", "attn_Wb", "attn_Wo", "attn_conv_q", "attn_conv_k", "attn_conv_v",
        "attn_onorm_w", "ffn_router_w", "ffn_e_bias", "ffn_W_gate", "ffn_W_up", "ffn_W_down",
        "ffn_shared_gate", "ffn_shared_up", "ffn_shared_down"]
_TURNED = {"ffn_router_w", "ffn_shared_gate", "ffn_shared_up", "ffn_shared_down"}


def kernel(**inputs):
    import numpy as _np
    import concourse.bacc as _bacc
    from concourse import mybir as _mybir
    from concourse.bass_utils import run_bass_kernel_spmd as _run

    nc = _bacc.Bacc("TRN2", target_bir_lowering=False, num_devices=1)
    arrays, args = {}, []
    for name in _INS:
        a = _np.asarray(inputs["L0_" + name])
        a = _np.ascontiguousarray(a.T if name in _TURNED else a)
        arrays[f"in_{name}"] = a
        args.append(nc.dram_tensor(f"in_{name}", a.shape, _mybir.dt.from_np(a.dtype), kind="ExternalInput").ap())
    out = nc.dram_tensor("out_0", (B, SEQ, D), _mybir.dt.from_np(_np.dtype("float32")), kind="ExternalOutput").ap()
    delta_moe_layer(nc, *args, out)
    r = _run(nc, [arrays], core_ids=[0])
    return r.results[0]["out_0"]
```

```python
from contextlib import ExitStack

import concourse.bass as bass
from concourse import mybir

F32 = mybir.dt.float32
BF16 = mybir.dt.bfloat16
I32 = mybir.dt.int32
U32 = mybir.dt.uint32
ALU = mybir.AluOpType
ACT = mybir.ActivationFunctionType
AX_X = mybir.AxisListType.X

P = 128
B, SEQ, D = 2, 1024, 512
H, DK = 16, 32
TT = 128
STEPS = SEQ // TT
KT = D // P
CT = H * DK // P
HT = P // DK
CH = 32
J = TT // CH
COLS = B * TT
I8 = CT * B
G = I8 * J
TAPS = 4
HALO = TAPS - 1
NE, EI = 32, 256
NG, EG = 8, 4
TOPG, TOPK = 3, 4
SCALE = 2.5
NT = B * STEPS
NTOK = B * SEQ
CAP = -(-5 * NTOK // (4 * NE))
FF = 512
FT = FF // P
LN_EPS, L2_EPS, RMS_EPS = 1e-5, 1e-6, 1e-5

SMALL = 1 + 1 + HT + 3 + 4
RING = 6

SIZE = dict(X=2, P=9, U=4, S=4, O=2, G=4, W=2, V=2, T=7)
LAG = dict(P=0, S=0, G=0, X=-1, U=1, O=1, W=1, T=1, V=2)
ORDER = dict(begin="XPSGX", one="PUSOGWXT", loop="PUSOGWVXT", seven="PUSOGWVT", end="UOWVTV")
LOOP_FROM, LOOP_TO = 2, STEPS - 1
JOBS = sum(SIZE[c] for c in ORDER["loop"])
assert JOBS % RING == 0
TURNS = JOBS // RING


def first_job(phase, section, again=False):
    base = 0
    for name, order in ORDER.items():
        if name == phase:
            break
        base += sum(SIZE[c] for c in order) * (LOOP_TO - LOOP_FROM if name == "loop" else 1)
    order = ORDER[phase]
    at = order.rindex(section) if again else order.index(section)
    base += sum(SIZE[c] for c in order[:at])
    return base + (LAG[section] - LOOP_FROM) * JOBS if phase == "loop" else base


class Ring:

    def __init__(self, banks, filled, freed):
        self.banks, self.filled, self.freed = banks, filled, freed

    def bank(self, first, n):
        return self.banks[(first + n) % RING]

    def wait_free(self, pe, first, step, n):
        turn = (first + n) // RING
        if isinstance(step, int) and turn + TURNS * step == 0:
            return
        pe.wait_ge(self.freed[(first + n) % RING], step * TURNS + turn)

    def wait_full(self, eng, first, step, n):
        eng.wait_ge(self.filled[(first + n) % RING], step * TURNS + (first + n) // RING + 1)

    def full(self, first, n):
        return self.filled[(first + n) % RING]

    def free(self, first, n):
        return self.freed[(first + n) % RING]


def where(phase, section, step, again=False):
    return first_job(phase, section, again), step if phase == "loop" else 0


def step_part(nc, ctx, dram, wring, route_m, route_w):
    def sb(name, shape, dt=F32):
        return ctx.enter_context(nc.sbuf_tensor(name, shape, dt))

    def sem(name):
        return ctx.enter_context(nc.semaphore(name))

    (x, Wq, Wk, Wv, Wb, Wo, conv_q, conv_k, conv_v, onorm_w, router_w, e_bias, W_gate, W_up, W_down,
     s_gate, s_up, s_down, x2_d, h_d, acc_d) = dram

    wqkv = wring[:, :].rearrange("p (s k n) -> p s k n", s=3, k=KT)
    wb = sb("wb", [P, KT, H])
    wo = sb("wo", [P, CT, D])
    wr = sb("wr", [P, KT, 4 * NE])
    sg_w = sb("sg_w", [P, KT, FF])
    su_w = sb("su_w", [P, KT, FF])
    sd_w = sb("sd_w", [P, FT, D])
    taps = sb("taps", [P, 3, TAPS])
    onw = sb("onw", [P, 1])
    ebias = sb("ebias", [P, NE])

    ident = sb("ident", [P, P])
    heads1 = sb("heads1", [P, P])
    headsm = sb("headsm", [P, P])
    spread = sb("spread", [H, CT, P])
    below = sb("below", [P, CH])
    upto = sb("upto", [P, CH])
    eps_ln = sb("eps_ln", [P, 1])
    eps_l2 = sb("eps_l2", [P, 1])
    eps_q = sb("eps_q", [P, 1])
    eps_rms = sb("eps_rms", [P, 1])
    iota_g = sb("iota_g", [P, NG])
    iota_e = sb("iota_e", [P, NE])

    x_in = sb("x_in", [P, B, D])
    x_res = sb("x_res", [P, B, D])
    stats = sb("stats", [P, B, 6])
    mv = sb("mv", [P, 3, B, 2])
    rs = sb("rs", [P, 3, B])
    xnT = sb("xnT", [P, KT, COLS])
    pre = sb("pre", [P, 3, I8, HALO + TT])
    cv = sb("cv", [P, 3, I8, TT])
    sig = sb("sig", [P, 3, I8 * TT])
    b16 = sb("b16", [H, COLS])
    kq = sb("kq", [P, G, 2, CH])
    beta = sb("beta", [P, G, CH])
    mbeta = sb("mbeta", [P, G, CH])
    k_tok = sb("k_tok", [P, G, DK])
    vk = sb("vk", [P, G, 2, DK])
    low = sig[:, 1, :].rearrange("p (g c) -> p g c", g=G)
    prod = sig[:, 0, :]
    lowp = sb("lowp", [P, CH, CH])
    inv = sb("inv", [P, CH, CH])
    invT = sb("invT", [P, G, CH])
    attnT = sb("attnT", [P, G, CH])
    uw = sb("uw", [P, J, I8, 2, DK])
    wT = sb("wT", [P, J, I8, CH])
    unew = sb("unew", [P, I8, DK])
    state = [sb(f"state{n}", [P, I8, DK]) for n in range(2)]
    o_ch = sb("o_ch", [P, I8, TT])
    o_r = sb("o_r", [P, I8 * TT])
    x2 = sb("x2", [P, B, D])
    h = sb("h", [P, B, D])
    hT = sb("hT", [P, KT, COLS])
    sh_g = cv[:, 0, :, :].rearrange("p i t -> p (i t)").rearrange("p (f c) -> p f c", f=FT)
    sh_u = cv[:, 1, :, :].rearrange("p i t -> p (i t)").rearrange("p (f c) -> p f c", f=FT)
    sh_s = cv[:, 2, :, :].rearrange("p i t -> p (i t)").rearrange("p (f c) -> p f c", f=FT)
    sh_h = sb("sh_h", [P, FT, COLS])
    acc_sb = sb("acc_sb", [P, B, D])
    score = sb("score", [P, B, NE])
    sc = sb("sc", [P, B, NE])
    grp = sb("grp", [P, 4, B, NG, 2])
    gs = sb("gs", [P, B, NG])
    top = sb("top", [P, B, 2, 8])
    topi = sb("topi", [P, B, 2, 8], U32)
    topf = sb("topf", [P, B, 2, 8])
    gmask = sb("gmask", [P, B, NG])
    masked = sb("masked", [P, B, NE])
    picked = sb("picked", [P, B, NE])
    weigh = sb("weigh", [P, B, NE])
    wsum = sb("wsum", [P, B])

    banks = [ctx.enter_context(nc.psum_tensor(f"bank{n}", [P, 512], F32)) for n in range(8)]
    ring = Ring(banks[:RING], [sem(f"filled{n}") for n in range(RING)], [sem(f"freed{n}") for n in range(RING)])
    ps_ws, ps_o = banks[6], banks[7]

    consts = sem("consts")
    consts_go = sem("consts_go")
    proj_in = sem("proj_in")
    weights_in = sem("weights_in")
    small_in = sem("small_in")
    wo_scaled = sem("wo_scaled")
    x_loaded = sem("x_loaded")
    xres_loaded = sem("xres_loaded")
    stats_ready = [sem(f"stats_ready{n}") for n in range(3)]
    rs_ready = [sem(f"rs_ready{n}") for n in range(3)]
    xn_ready = sem("xn_ready")
    xnT_ready = sem("xnT_ready")
    beta_ready = sem("beta_ready")
    pre_ready = [sem(f"pre_ready{n}") for n in range(3)]
    conv_done = [sem(f"conv_done{n}") for n in range(3)]
    sig_ready = [sem(f"sig_ready{n}") for n in range(3)]
    act_ready = [sem(f"act_ready{n}") for n in range(3)]
    sq_ready = [sem(f"sq_ready{n}") for n in range(2)]
    norm_ready = [sem(f"norm_ready{n}") for n in range(2)]
    halo_done = sem("halo_done")
    kq_ready = sem("kq_ready")
    betaT_ready = sem("betaT_ready")
    mbeta_ready = sem("mbeta_ready")
    tok_ready = sem("tok_ready")
    vk_ready = sem("vk_ready")
    gram_read = sem("gram_read")
    inv_ready = sem("inv_ready")
    uw_ready = sem("uw_ready")
    wT_ready = sem("wT_ready")
    ws_done = sem("ws_done")
    unew_ready = sem("unew_ready")
    ds_done = sem("ds_done")
    state_ready = sem("state_ready")
    o_done = sem("o_done")
    o_out = sem("o_out")
    osq_ready = sem("osq_ready")
    onorm_ready = sem("onorm_ready")
    on_ready = sem("on_ready")
    h_ready = sem("h_ready")
    rows_out = sem("rows_out")
    hT_ready = sem("hT_ready")
    gate_sig = sem("gate_sig")
    up_out = sem("up_out")
    hid_ready = sem("hid_ready")
    shared_done = sem("shared_done")
    acc_ready = sem("acc_ready")
    acc_out = sem("acc_out")
    score_ready = sem("score_ready")
    score_used = sem("score_used")
    dve_step = sem("dve_step")
    act_step = sem("act_step")
    pool_step = sem("pool_step")
    pe_passed = sem("pe_passed")
    moe_in = sem("moe_in")

    def quad(n):
        return slice(DK * n, DK * n + DK)

    block = ctx.enter_context(nc.Block())

    @block.sync
    def _(sp):
        sp.dma_start(x_in[:, :, :], x[:, 0:TT, :].rearrange("b p d -> p b d")).then_inc(x_loaded, 16)
        small = [(wb[:, :, :], Wb.rearrange("(k p) n -> p k n", p=P)),
                 (ebias[:, :], e_bias.rearrange("(o n) -> o n", o=1).to_broadcast([P, NE]))]
        for n in range(HT):
            small.append((onw[quad(n), :], onorm_w.rearrange("(n o) -> n o", o=1)))
        for n, w in enumerate((conv_q, conv_k, conv_v)):
            small.append((taps[:, n, :], w.rearrange("(o n) -> o n", o=1).to_broadcast([P, TAPS])))
        for n in range(4):
            small.append((wr[:, :, NE * n:NE * n + NE], router_w.rearrange("(k p) e -> p k e", p=P)))
        for n, w in enumerate((Wk, Wq, Wv)):
            s = (1, 0, 2)[n]
            sp.dma_start(wqkv[:, s, :, :], w.rearrange("(k p) n -> p k n", p=P)).then_inc(proj_in, 16)
        for dst, src in small:
            sp.dma_start(dst, src).then_inc(small_in, 16)
        for dst, src in ((wo, Wo), (sg_w, s_gate), (su_w, s_up), (sd_w, s_down)):
            sp.dma_start(dst[:, :, :], src.rearrange("(k p) n -> p k n", p=P)).then_inc(weights_in, 16)
        assert len(small) == SMALL

        def load_x(s):
            sp.wait_ge(xnT_ready, 2 * s)
            sp.dma_start(x_in[:, :, :], x.rearrange("b (t p) d -> t p b d", p=TT)[s]).then_inc(x_loaded, 16)

        def rows(s):
            sp.dma_start(x_res[:, :, :], x.rearrange("b (t p) d -> t p b d", p=TT)[s]).then_inc(xres_loaded, 16)
            sp.wait_ge(h_ready, s + 1)
            sp.dma_start(x2_d.rearrange("(b t p) d -> t p b d", p=TT, b=B)[s], x2[:, :, :]).then_inc(rows_out, 16)
            sp.dma_start(h_d[0:NTOK, :].rearrange("(b t p) d -> t p b d", p=TT, b=B)[s], h[:, :, :]).then_inc(rows_out, 16)

        def shared_out(s):
            sp.wait_ge(acc_ready, s + 1)
            sp.dma_start(acc_d[0:NTOK, :].rearrange("(b t p) d -> t p b d", p=TT, b=B)[s], acc_sb[:, :, :]).then_inc(acc_out, 16)

        sp.wait_ge(consts, 1)
        sp.dma_start(h_d[NTOK:NTOK + CAP, :], acc_sb[0:CAP, 0, :]).then_inc(acc_out, 16)
        sp.dma_start(acc_d[NTOK:NTOK + CAP, :], acc_sb[0:CAP, 0, :]).then_inc(acc_out, 16)

        load_x(1)
        load_x(2)
        rows(0)
        for n in range(1, 2):
            load_x(n + 2)
            rows(n)
            shared_out(n - 1)
        with sp.Fori(2, STEPS - 2) as s:
            load_x(s + 2)
            rows(s)
            shared_out(s - 1)
        for n in range(STEPS - 2, STEPS):
            rows(n)
            shared_out(n - 1)
        shared_out(STEPS - 1)
        sp.wait_ge(rows_out, 32 * STEPS)
        sp.wait_ge(acc_out, 32 + 16 * STEPS)

    @block.gpsimd
    def _(pool):
        g = nc.gpsimd
        g.memset(ident[:, :], 0.0)
        g.memset(heads1[:, :], 0.0)
        g.memset(headsm[:, :], 0.0)
        g.memset(spread[:, :, :], 1.0)
        g.memset(below[:, :], -1.0)
        g.memset(upto[:, :], 1.0)
        g.memset(inv[:, :, :], 0.0)
        g.memset(pre[:, :, :, 0:HALO], 0.0)
        g.memset(state[0][:, :, :], 0.0)
        g.memset(eps_ln[:, :], LN_EPS)
        g.memset(eps_l2[:, :], L2_EPS)
        g.memset(eps_q[:, :], L2_EPS * DK)
        g.memset(eps_rms[:, :], RMS_EPS)
        g.iota(iota_g[:, :], pattern=[[1, NG]], base=0, channel_multiplier=0, allow_small_or_imprecise_dtypes=True)
        g.iota(iota_e[:, :], pattern=[[1, NE]], base=0, channel_multiplier=0, allow_small_or_imprecise_dtypes=True)
        g.memset(acc_sb[:, :, :], 0.0).then_inc(consts_go, 1)
        pool.wait_ge(consts_go, 1)
        made = [1]

        def alone(ins):
            made[0] += 1
            ins.then_inc(consts_go, 1)
            pool.wait_ge(consts_go, made[0])

        for n in range(HT):
            alone(g.memset(heads1[quad(n), quad(n)], 1.0))
            alone(g.memset(headsm[quad(n), quad(n)], 1.0 / DK))
            alone(g.affine_select(out=below[quad(n), :], in_=below[quad(n), :], compare_op=ALU.is_gt, fill=0.0,
                                  base=0, pattern=[[-1, CH]], channel_multiplier=1))
            alone(g.affine_select(out=upto[quad(n), :], in_=upto[quad(n), :], compare_op=ALU.is_ge, fill=0.0,
                                  base=0, pattern=[[1, CH]], channel_multiplier=-1))
        g.affine_select(out=ident[:, :], in_=ident[:, :], compare_op=ALU.not_equal, fill=1.0,
                        base=0, pattern=[[-1, P]], channel_multiplier=1)
        g.affine_select(out=inv[:, :, :], in_=inv[:, :, :], compare_op=ALU.not_equal, fill=1.0,
                        base=0, pattern=[[1, CH], [-1, CH]], channel_multiplier=0)
        g.affine_select(out=spread[:, :, :].rearrange("h c (a d) -> h c a d", a=HT),
                        in_=spread[:, :, :].rearrange("h c (a d) -> h c a d", a=HT), compare_op=ALU.is_equal, fill=0.0,
                        base=0, pattern=[[-HT, CT], [-1, HT], [0, DK]], channel_multiplier=1).then_inc(consts, 1)

        def mask_beta(s):
            pool.wait_ge(betaT_ready, s + 1)
            if not (isinstance(s, int) and s == 0):
                pool.wait_ge(gram_read, s)
            g.tensor_tensor(mbeta[:, :, :], beta[:, :, :], below[:, :].rearrange("p (o c) -> p o c", o=1).to_broadcast([P, G, CH]), ALU.mult).then_inc(mbeta_ready, 1)

        def by_beta(s):
            pool.wait_ge(tok_ready, s + 1)
            g.tensor_tensor(vk[:, :, 0, :], vk[:, :, 0, :], beta[:, :, :], ALU.mult)
            g.tensor_tensor(vk[:, :, 1, :], k_tok[:, :, :], beta[:, :, :], ALU.mult).then_inc(vk_ready, 1)

        def shared(s):
            pool.wait_ge(gate_sig, s + 1)
            g.tensor_tensor(sh_g, sh_g, sh_s, ALU.mult).then_inc(pool_step, 1)
            pool.wait_ge(pool_step, 1)
            pool.wait_ge(up_out, s + 1)
            if not (isinstance(s, int) and s == 0):
                pool.wait_ge(shared_done, s)
            g.tensor_tensor(sh_h[:, :, :], sh_g, sh_u, ALU.mult).then_inc(hid_ready, 1)
            pool.sem_clear(pool_step)

        mask_beta(0)
        by_beta(0)

        def body(s):
            mask_beta(s)
            by_beta(s)
            shared(s - 1)

        body(1)
        with pool.Fori(LOOP_FROM, LOOP_TO) as s:
            body(s)
        body(STEPS - 1)
        shared(STEPS - 1)

    @block.tensor
    def _(pe):
        te = nc.tensor

        def turn_x(s, phase, again=False):
            first, st = where(phase, "X", s, again)
            pe.wait_ge(xn_ready, s + 1)
            for n in range(2):
                ring.wait_free(pe, first, st, n)
                bank = ring.bank(first, n)
                for k in range(2):
                    for b in range(B):
                        kt = 2 * n + k
                        m = te.transpose(bank[:, k * COLS + b * TT:k * COLS + (b + 1) * TT], x_in[:, b, kt * P:(kt + 1) * P], ident[:, :])
                m.then_inc(ring.full(first, n), 1)

        def project(s, phase):
            first, st = where(phase, "P", s)

            def start(n):
                ring.wait_free(pe, first, st, n)
                return ring.bank(first, n)

            pe.wait_ge(proj_in, 48)
            pe.wait_ge(small_in, 16 * SMALL)
            pe.wait_ge(xnT_ready, 2 * (s + 1))
            bank = start(0)
            for kt in range(KT):
                m = te.matmul(bank[0:H, 0:COLS], wb[:, kt, :], xnT[:, kt, :], start=(kt == 0), stop=(kt == KT - 1))
            m.then_inc(ring.full(first, 0), 1)
            for a, w in enumerate((1, 0, 2)):
                for half in range(2):
                    n = 1 + 2 * a + half + (2 if a == 2 else 0)
                    bank = start(n)
                    for c in range(2):
                        ct = 2 * half + c
                        for kt in range(KT):
                            m = te.matmul(bank[:, c * COLS:(c + 1) * COLS], wqkv[:, w, kt, ct * P:(ct + 1) * P], xnT[:, kt, :],
                                          start=(kt == 0), stop=(kt == KT - 1))
                    m.then_inc(ring.full(first, n), 1)
                if a == 1:
                    pe.wait_ge(beta_ready, s + 1)
                    for half in range(2):
                        n = 5 + half
                        bank = start(n)
                        for c in range(2):
                            m = te.matmul(bank[:, c * COLS:(c + 1) * COLS], spread[:, 2 * half + c, :], b16[:, :], start=True, stop=True)
                        m.then_inc(ring.full(first, n), 1)

        def squares(s, phase, a):
            first, st = where(phase, "S", s)
            pe.wait_ge(sq_ready[a], s + 1)
            for half in range(2):
                n = 2 * a + half
                ring.wait_free(pe, first, st, n)
                bank = ring.bank(first, n)
                for c in range(2):
                    m = te.matmul(bank[:, c * COLS:(c + 1) * COLS], heads1[:, :], sig[:, a, (2 * half + c) * COLS:(2 * half + c + 1) * COLS],
                                  start=True, stop=True)
                m.then_inc(ring.full(first, n), 1)

        def gram(s, phase):
            first, st = where(phase, "G", s)
            pe.wait_ge(kq_ready, 2 * (s + 1))
            for j in range(J):
                ring.wait_free(pe, first, st, j)
                bank = ring.bank(first, j)
                pe.sem_inc(pe_passed, 1)
                for i in range(I8):
                    for hh in range(HT):
                        m = te.matmul(bank[quad(hh), i * 64:(i + 1) * 64], kq[quad(hh), i * J + j, 0, :], kq[quad(hh), i * J + j, :, :].rearrange("p a c -> p (a c)"),
                                      start=True, stop=True)
                m.then_inc(ring.full(first, j), 1)

        def core(s, phase, squares_of):
            first, st = where(phase, "U", s)
            pe.wait_ge(inv_ready, s + 1)
            pe.wait_ge(vk_ready, s + 1)
            for j in range(J):
                ring.wait_free(pe, first, st, j)
                bank = ring.bank(first, j)
                pe.sem_inc(pe_passed, 1)
                for i in range(I8):
                    for hh in range(HT):
                        m = te.matmul(bank[quad(hh), i * 64:(i + 1) * 64], invT[quad(hh), i * J + j, :], vk[quad(hh), i * J + j, :, :].rearrange("p a c -> p (a c)"),
                                      start=True, stop=True)
                m.then_inc(ring.full(first, j), 1)
            for j in range(J):
                now = state[j % 2]
                pe.wait_ge(wT_ready, J * s + j + 1)
                if not (isinstance(s, int) and s == 0 and j == 0):
                    pe.wait_ge(state_ready, J * s + j)
                pe.sem_inc(pe_passed, 1)
                for i in range(I8):
                    for hh in range(HT):
                        m = te.matmul(ps_ws[quad(hh), i * DK:(i + 1) * DK], wT[quad(hh), j, i, :], now[quad(hh), i, :], start=True, stop=True)
                m.then_inc(ws_done, 1)
                if not (isinstance(s, int) and s == 0 and j == 0):
                    pe.wait_ge(o_out, J * s + j)
                pe.sem_inc(pe_passed, 1)
                for i in range(I8):
                    for hh in range(HT):
                        te.matmul(ps_o[quad(hh), i * CH:(i + 1) * CH], now[quad(hh), i, :], kq[quad(hh), i * J + j, 1, :],
                                  start=(i == 0), stop=False, skip_group_check=True)
                pe.wait_ge(unew_ready, J * s + j + 1)
                pe.sem_inc(pe_passed, 1)
                for i in range(I8):
                    for hh in range(HT):
                        m = te.matmul(ps_ws[quad(hh), 256 + i * DK:256 + (i + 1) * DK], k_tok[quad(hh), i * J + j, :], unew[quad(hh), i, :], start=True, stop=True,
                                      skip_group_check=True)
                m.then_inc(ds_done, 1)
                for i in range(I8):
                    for hh in range(HT):
                        m = te.matmul(ps_o[quad(hh), i * CH:(i + 1) * CH], unew[quad(hh), i, :], attnT[quad(hh), i * J + j, :],
                                      start=False, stop=(i == I8 - 1), skip_group_check=True)
                m.then_inc(o_done, 1)
                if squares_of is not None and j in (1, 2):
                    squares(squares_of, phase, j - 1)

        def output_squares(s, phase):
            first, st = where(phase, "O", s)
            pe.wait_ge(osq_ready, s + 1)
            for half in range(2):
                ring.wait_free(pe, first, st, half)
                bank = ring.bank(first, half)
                for c in range(2):
                    m = te.matmul(bank[:, c * COLS:(c + 1) * COLS], headsm[:, :], o_r[:, (2 * half + c) * COLS:(2 * half + c + 1) * COLS], start=True, stop=True)
                m.then_inc(ring.full(first, half), 1)

        def out_proj(s, phase):
            first, st = where(phase, "W", s)
            pe.wait_ge(on_ready, s + 1)
            pe.wait_ge(wo_scaled, 1)
            for b in range(B):
                ring.wait_free(pe, first, st, b)
                bank = ring.bank(first, b)
                for ct in range(CT):
                    m = te.matmul(bank[:, :], o_ch[:, ct * B + b, :], wo[:, ct, :], start=(ct == 0), stop=(ct == CT - 1))
                m.then_inc(ring.full(first, b), 1)

        def shared_up(s, phase):
            first, st = where(phase, "T", s)
            pe.wait_ge(h_ready, s + 1)
            for n in range(2):
                ring.wait_free(pe, first, st, n)
                bank = ring.bank(first, n)
                for k in range(2):
                    for b in range(B):
                        kt = 2 * n + k
                        m = te.transpose(bank[:, k * COLS + b * TT:k * COLS + (b + 1) * TT], h[:, b, kt * P:(kt + 1) * P], ident[:, :])
                m.then_inc(ring.full(first, n), 1)
            pe.wait_ge(hT_ready, 2 * (s + 1))
            ring.wait_free(pe, first, st, 2)
            bank = ring.bank(first, 2)
            for b in range(B):
                for kt in range(KT):
                    m = te.matmul(bank[:, b * P:(b + 1) * P], hT[:, kt, b * TT:(b + 1) * TT], wr[:, kt, :], start=(kt == 0), stop=(kt == KT - 1))
            m.then_inc(ring.full(first, 2), 1)
            pe.wait_ge(weights_in, 16 * 4)
            for a, w in enumerate((sg_w, su_w)):
                for half in range(2):
                    n = 3 + 2 * a + half
                    ring.wait_free(pe, first, st, n)
                    bank = ring.bank(first, n)
                    for c in range(2):
                        ft = 2 * half + c
                        for kt in range(KT):
                            m = te.matmul(bank[:, c * COLS:(c + 1) * COLS], w[:, kt, ft * P:(ft + 1) * P], hT[:, kt, :], start=(kt == 0), stop=(kt == KT - 1))
                    m.then_inc(ring.full(first, n), 1)

        def shared_down(s, phase, again=False):
            first, st = where(phase, "V", s, again)
            pe.wait_ge(hid_ready, s + 1)
            for b in range(B):
                ring.wait_free(pe, first, st, b)
                bank = ring.bank(first, b)
                for ft in range(FT):
                    m = te.matmul(bank[:, :], sh_h[:, ft, b * TT:(b + 1) * TT], sd_w[:, ft, :], start=(ft == 0), stop=(ft == FT - 1))
                m.then_inc(ring.full(first, b), 1)
            pe.wait_ge(ring.full(first, 1), st * TURNS + (first + 1) // RING + 1)
            pe.sem_inc(shared_done, 1)

        pe.wait_ge(consts, 1)
        turn_x(0, "begin")
        project(0, "begin")
        squares(0, "begin", 0)
        squares(0, "begin", 1)
        gram(0, "begin")
        turn_x(1, "begin", again=True)

        def body(s, phase):
            project(s, phase)
            core(s - 1, phase, s)
            output_squares(s - 1, phase)
            gram(s, phase)
            out_proj(s - 1, phase)
            if phase != "one":
                shared_down(s - 2, phase)
            if phase != "seven":
                turn_x(s + 1, phase)
            shared_up(s - 1, phase)

        body(1, "one")
        with pe.Fori(LOOP_FROM, LOOP_TO) as s:
            body(s, "loop")
        body(STEPS - 1, "seven")
        core(STEPS - 1, "end", None)
        output_squares(STEPS - 1, "end")
        out_proj(STEPS - 1, "end")
        shared_down(STEPS - 2, "end")
        shared_up(STEPS - 1, "end")
        shared_down(STEPS - 1, "end", again=True)

    @block.scalar
    def _(act):
        sc_e = nc.scalar

        class Steps:
            count = 0

        def link(ins):
            Steps.count += 1
            ins.then_inc(act_step, 1)
            act.wait_ge(act_step, Steps.count)

        def end_steps():
            act.sem_clear(act_step)
            Steps.count = 0

        def rstd(n, s):
            act.wait_ge(stats_ready[n], s + 1)
            link(sc_e.activation(rs[:, n, :], mv[:, n, :, 1], ACT.Ln, bias=eps_ln[:, 0:1]))
            sc_e.activation(rs[:, n, :], rs[:, n, :], ACT.Exp, scale=-0.5).then_inc(rs_ready[n], 1)

        def sigmoid(dst, src, done=None):
            link(sc_e.activation(dst, src, ACT.Exp, scale=-1.0))
            link(sc_e.activation(dst, dst, ACT.Ln, bias=1.0))
            return sc_e.activation(dst, dst, ACT.Exp, scale=-1.0)

        def release(first, n):
            act.sem_inc(ring.free(first, n), 1)

        def take_x(s, phase, again=False):
            first, st = where(phase, "X", s, again)
            for n in range(2):
                ring.wait_full(act, first, st, n)
                link(sc_e.activation(xnT[:, 2 * n:2 * n + 2, :], ring.bank(first, n)[:, :].rearrange("p (k c) -> p k c", k=2), ACT.Copy))
                release(first, n)
                act.sem_inc(xnT_ready, 1)

        def take_beta(s, phase):
            first, st = where(phase, "P", s)
            ring.wait_full(act, first, st, 0)
            link(sc_e.activation(b16[:, :], ring.bank(first, 0)[0:H, 0:COLS], ACT.Exp, scale=-1.0))
            release(first, 0)
            link(sc_e.activation(b16[:, :], b16[:, :], ACT.Ln, bias=1.0))
            sc_e.activation(b16[:, :], b16[:, :], ACT.Exp, scale=-1.0).then_inc(beta_ready, 1)

        def take_projection(s, phase, a, w):
            first, st = where(phase, "P", s)
            if not (isinstance(s, int) and s == 0):
                act.wait_ge(halo_done, 3 * (s - 1) + a + 1)
            for half in range(2):
                n = 1 + 2 * a + half + (2 if a == 2 else 0)
                ring.wait_full(act, first, st, n)
                link(sc_e.activation(pre[:, w, 4 * half:4 * half + 4, HALO:], ring.bank(first, n)[:, :].rearrange("p (i t) -> p i t", t=TT), ACT.Copy))
                release(first, n)
            act.sem_inc(pre_ready[w], 1)

        def silu_factor(s, w):
            act.wait_ge(conv_done[w], s + 1)
            slot = (1, 0, 2)[w]
            sigmoid(sig[:, slot, :], cv[:, w, :, :].rearrange("p i t -> p (i t)")).then_inc(sig_ready[w], 1)

        def square(s, a, w):
            act.wait_ge(act_ready[w], s + 1)
            sc_e.activation(sig[:, a, :], cv[:, w, :, :].rearrange("p i t -> p (i t)"), ACT.Square).then_inc(sq_ready[a], 1)

        def norms(s, phase, a):
            first, st = where(phase, "S", s)
            for half in range(2):
                n = 2 * a + half
                part = sig[:, a, half * 512:(half + 1) * 512]
                ring.wait_full(act, first, st, n)
                link(sc_e.activation(part, ring.bank(first, n)[:, :], ACT.Ln, bias=(eps_l2, eps_q)[a][:, 0:1], scale=(1.0, float(DK))[a]))
                release(first, n)
                link(sc_e.activation(part, part, ACT.Exp, scale=-0.5))
            act.sem_inc(norm_ready[a], 1)

        def take_uw(s, phase):
            first, st = where(phase, "U", s)
            for j in range(J):
                ring.wait_full(act, first, st, j)
                link(sc_e.activation(uw[:, j, :, :, :].rearrange("p i a d -> p (i a d)"), ring.bank(first, j)[:, :], ACT.Copy))
                release(first, j)
                act.sem_inc(uw_ready, 1)

        def take_output(s, j):
            act.wait_ge(o_done, J * s + j + 1)
            link(sc_e.activation(o_ch[:, :, j * CH:(j + 1) * CH], ps_o[:, 0:I8 * CH].rearrange("p (i c) -> p i c", c=CH), ACT.Copy))
            act.sem_inc(o_out, 1)

        def output_norm(s, phase):
            first, st = where(phase, "O", s)
            sc_e.activation(o_r[:, :], o_ch[:, :, :].rearrange("p i t -> p (i t)"), ACT.Square).then_inc(osq_ready, 1)
            ring.wait_full(act, first, st, 1)
            for half in range(2):
                part = o_r[:, half * 512:(half + 1) * 512]
                ring.wait_full(act, first, st, half)
                link(sc_e.activation(part, ring.bank(first, half)[:, :], ACT.Ln, bias=eps_rms[:, 0:1]))
                release(first, half)
                link(sc_e.activation(part, part, ACT.Exp, scale=-0.5))
            act.sem_inc(onorm_ready, 1)

        def take_rows(s, phase):
            first, st = where(phase, "T", s)
            for n in range(2):
                ring.wait_full(act, first, st, n)
                link(sc_e.activation(hT[:, 2 * n:2 * n + 2, :], ring.bank(first, n)[:, :].rearrange("p (k c) -> p k c", k=2), ACT.Copy))
                release(first, n)
                act.sem_inc(hT_ready, 1)
            ring.wait_full(act, first, st, 2)
            if not (isinstance(s, int) and s == 0):
                act.wait_ge(score_used, s)
            link(sc_e.activation(score[:, :, :], ring.bank(first, 2)[:, 0:B * P].rearrange("p (b e) -> p b e", b=B)[:, :, 0:NE], ACT.Exp, scale=-1.0))
            release(first, 2)
            link(sc_e.activation(score[:, :, :], score[:, :, :], ACT.Ln, bias=1.0))
            sc_e.activation(score[:, :, :], score[:, :, :], ACT.Exp, scale=-1.0).then_inc(score_ready, 1)
            act.wait_ge(tok_ready, s + (1 if phase == "end" else 2))
            for half in range(2):
                n = 3 + half
                ring.wait_full(act, first, st, n)
                src = ring.bank(first, n)[:, :].rearrange("p (f c) -> p f c", f=2)
                sc_e.activation(sh_g[:, 2 * half:2 * half + 2, :], src, ACT.Copy)
                link(sc_e.activation(sh_s[:, 2 * half:2 * half + 2, :], src, ACT.Exp, scale=-1.0))
                release(first, n)
            link(sc_e.activation(sh_s, sh_s, ACT.Ln, bias=1.0))
            sc_e.activation(sh_s, sh_s, ACT.Exp, scale=-1.0).then_inc(gate_sig, 1)
            for half in range(2):
                n = 5 + half
                ring.wait_full(act, first, st, n)
                link(sc_e.activation(sh_u[:, 2 * half:2 * half + 2, :], ring.bank(first, n)[:, :].rearrange("p (f c) -> p f c", f=2), ACT.Copy))
                release(first, n)
            act.sem_inc(up_out, 1)

        def take_shared(s, phase, again=False):
            first, st = where(phase, "V", s, again)
            act.wait_ge(acc_out, 32 + 16 * s)
            for b in range(B):
                ring.wait_full(act, first, st, b)
                link(sc_e.activation(acc_sb[:, b, :], ring.bank(first, b)[:, :], ACT.Copy))
                release(first, b)
            act.sem_inc(acc_ready, 1)

        sc_e.preload_act_table_set("natural_log_exp_and_others")
        act.wait_ge(consts, 1)
        rstd(0, 0)
        take_x(0, "begin")
        take_beta(0, "begin")
        for a, w in enumerate((1, 0, 2)):
            take_projection(0, "begin", a, w)
        for a, w in enumerate((1, 0)):
            silu_factor(0, w)
            square(0, a, w)
        silu_factor(0, 2)
        for a in range(2):
            norms(0, "begin", a)
        rstd(0, 1)
        take_x(1, "begin", again=True)
        end_steps()

        def body(s, phase):
            take_beta(s, phase)
            for a, w in enumerate((1, 0, 2)):
                take_projection(s, phase, a, w)
            take_uw(s - 1, phase)
            silu_factor(s, 1)
            silu_factor(s, 0)
            square(s, 0, 1)
            take_output(s - 1, 0)
            silu_factor(s, 2)
            square(s, 1, 0)
            take_output(s - 1, 1)
            norms(s, phase, 0)
            if phase != "seven":
                rstd(0, s + 1)
            take_output(s - 1, 2)
            norms(s, phase, 1)
            take_output(s - 1, 3)
            output_norm(s - 1, phase)
            rstd(1, s - 1)
            rstd(2, s - 1)
            if phase != "one":
                take_shared(s - 2, phase)
            if phase != "seven":
                take_x(s + 1, phase)
            take_rows(s - 1, phase)
            end_steps()

        body(1, "one")
        with act.Fori(LOOP_FROM, LOOP_TO) as s:
            body(s, "loop")
        body(STEPS - 1, "seven")
        take_uw(STEPS - 1, "end")
        for j in range(J):
            take_output(STEPS - 1, j)
        output_norm(STEPS - 1, "end")
        rstd(1, STEPS - 1)
        rstd(2, STEPS - 1)
        take_shared(STEPS - 2, "end")
        take_rows(STEPS - 1, "end")
        take_shared(STEPS - 1, "end", again=True)

    @block.vector
    def _(dve):
        v = nc.vector

        class Steps:
            count = 0

        def link(ins):
            Steps.count += 1
            ins.then_inc(dve_step, 1)
            dve.wait_ge(dve_step, Steps.count)

        def end_steps():
            dve.sem_clear(dve_step)
            Steps.count = 0

        def flat(ap):
            return ap.rearrange("p i t -> p (i t)")

        def moments(n, s, srcs):
            for b in range(B):
                last = v.bn_stats(stats[:, b, :], srcs[b])
            link(last)
            for b in range(B):
                last = v.bn_aggr(mv[:, n, b, :], stats[:, b, :])
            last.then_inc(stats_ready[n], 1)

        def first_norm(s):
            dve.wait_ge(x_loaded, 16 * (s + 1))
            moments(0, s, [x_in[:, b, :] for b in range(B)])
            dve.wait_ge(rs_ready[0], s + 1)
            for b in range(B):
                last = v.tensor_scalar(x_in[:, b, :], x_in[:, b, :], mv[:, 0, b, 0:1], rs[:, 0, b:b + 1], ALU.subtract, ALU.mult)
            last.then_inc(xn_ready, 1)

        def conv(a, w, s):
            dve.wait_ge(pre_ready[w], s + 1)
            if a == 0 and not (isinstance(s, int) and s < 2):
                dve.wait_ge(hid_ready, s - 1)
            out = cv[:, w, :, :]
            link(v.tensor_scalar(out, pre[:, w, :, 0:TT], taps[:, w, 0:1], None, ALU.mult))
            for n in range(1, TAPS):
                link(v.scalar_tensor_tensor(out=out, in0=pre[:, w, :, n:n + TT], scalar=taps[:, w, n:n + 1], in1=out, op0=ALU.mult, op1=ALU.add))
            dve.sem_inc(conv_done[w], 1)
            link(v.tensor_copy(pre[:, w, :, 0:HALO], pre[:, w, :, TT:TT + HALO]))
            dve.sem_inc(halo_done, 1)

        def silu(w, s):
            slot = (1, 0, 2)[w]
            dve.wait_ge(sig_ready[w], s + 1)
            link(v.tensor_tensor(flat(cv[:, w, :, :]), flat(cv[:, w, :, :]), sig[:, slot, :], ALU.mult))
            dve.sem_inc(act_ready[w], 1)

        def normalise(a, w, s):
            dve.wait_ge(norm_ready[a], s + 1)
            link(v.tensor_tensor(kq[:, :, a, :], flat(cv[:, w, :, :]).rearrange("p (g c) -> p g c", c=CH), sig[:, a, :].rearrange("p (g c) -> p g c", c=CH), ALU.mult))
            dve.sem_inc(kq_ready, 1)

        def turn_beta(s, phase):
            first, st = where(phase, "P", s)
            if not (isinstance(s, int) and s == 0):
                dve.wait_ge(vk_ready, s)
            for half in range(2):
                n = 5 + half
                ring.wait_full(dve, first, st, n)
                link(v.transpose(beta[:, half * 16:(half + 1) * 16, :].rearrange("p g c -> p (g c)"), ring.bank(first, n)[:, :]))
                dve.sem_inc(ring.free(first, n), 1)
            dve.sem_inc(betaT_ready, 1)

        def turn_v():
            link(v.transpose(vk[:, :, 0, :], flat(cv[:, 2, :, :]).rearrange("p (g c) -> p g c", c=CH)))

        def turn_k():
            link(v.transpose(k_tok[:, :, :], kq[:, :, 0, :]))
            dve.sem_inc(tok_ready, 1)

        def masks(s, phase):
            first, st = where(phase, "G", s)
            dve.wait_ge(mbeta_ready, s + 1)
            for j in range(J):
                ring.wait_full(dve, first, st, j)
                bank = ring.bank(first, j)[:, :].rearrange("p (i a c) -> p i a c", i=I8, a=2)
                v.tensor_tensor(low.rearrange("p (i j) c -> p j i c", j=J)[:, j], bank[:, :, 0, :], mbeta[:, :, :].rearrange("p (i j) c -> p j i c", j=J)[:, j], ALU.mult)
                link(v.tensor_tensor(attnT[:, :, :].rearrange("p (i j) c -> p j i c", j=J)[:, j], bank[:, :, 1, :],
                                     upto[:, :].rearrange("p (o c) -> p o c", o=1).to_broadcast([P, I8, CH]), ALU.mult))
                dve.sem_inc(ring.free(first, j), 1)
            dve.sem_inc(gram_read, 1)

        def inverse():
            link(v.transpose(lowp[:, :, :].rearrange("p c m -> p m c"), low.rearrange("p g m -> p m g")))
            invc = inv[:, :, :].rearrange("p j k -> p k j")
            for i in range(1, CH):
                t = prod[:, 0:i * i].rearrange("p (k j) -> p k j", k=i)
                link(v.tensor_tensor(t, invc[:, 0:i, 0:i], lowp[:, i:i + 1, 0:i].to_broadcast([P, i, i]), ALU.mult))
                link(v.tensor_reduce(inv[:, i, 0:i], t, AX_X, ALU.add))
            link(v.transpose(invT[:, :, :].rearrange("p g c -> p c g"), inv[:, :, :]))
            dve.sem_inc(inv_ready, 1)

        def turn_w(s):
            for j in range(J):
                dve.wait_ge(uw_ready, J * s + j + 1)
                v.transpose(wT[:, j, :, :], uw[:, j, :, 1, :]).then_inc(wT_ready, 1)

        def new_values(s, j):
            dve.wait_ge(ws_done, J * s + j + 1)
            v.tensor_tensor(unew[:, :, :], uw[:, j, :, 0, :], ps_ws[:, 0:256].rearrange("p (i d) -> p i d", d=DK), ALU.subtract).then_inc(unew_ready, 1)

        def next_state(s, j):
            now, new = state[j % 2], state[(j + 1) % 2]
            dve.wait_ge(ds_done, J * s + j + 1)
            v.tensor_tensor(new[:, :, :], now[:, :, :], ps_ws[:, 256:512].rearrange("p (i d) -> p i d", d=DK), ALU.add).then_inc(state_ready, 1)

        def scale_output(s):
            dve.wait_ge(onorm_ready, s + 1)
            v.tensor_tensor(flat(o_ch[:, :, :]), flat(o_ch[:, :, :]), o_r[:, :], ALU.mult).then_inc(on_ready, 1)

        def rows(s, phase):
            first, st = where(phase, "W", s)
            for b in range(B):
                ring.wait_full(dve, first, st, b)
            ys = [ring.bank(first, b)[:, :] for b in range(B)]
            moments(1, s, ys)
            dve.wait_ge(rs_ready[1], s + 1)
            dve.wait_ge(xres_loaded, 16 * (s + 1))
            if not (isinstance(s, int) and s == 0):
                dve.wait_ge(rows_out, 32 * s)
            for b in range(B):
                link(v.tensor_scalar(x2[:, b, :], ys[b], mv[:, 1, b, 0:1], rs[:, 1, b:b + 1], ALU.subtract, ALU.mult))
                dve.sem_inc(ring.free(first, b), 1)
            link(v.tensor_tensor(x2[:, :, :], x2[:, :, :], x_res[:, :, :], ALU.add))
            moments(2, s, [x2[:, b, :] for b in range(B)])
            dve.wait_ge(rs_ready[2], s + 1)
            for b in range(B):
                last = v.tensor_scalar(h[:, b, :], x2[:, b, :], mv[:, 2, b, 0:1], rs[:, 2, b:b + 1], ALU.subtract, ALU.mult)
            last.then_inc(h_ready, 1)

        def one_hot(dst, index, iota, n, count):
            for b in range(B):
                for k in range(count):
                    if k == 0:
                        link(v.tensor_scalar(dst[:, b, :], iota[:, :], index[:, b, n, k:k + 1], None, ALU.is_equal))
                    else:
                        link(v.scalar_tensor_tensor(out=dst[:, b, :], in0=iota[:, :], scalar=index[:, b, n, k:k + 1], in1=dst[:, b, :], op0=ALU.is_equal, op1=ALU.add))

        def route(s):
            dve.wait_ge(score_ready, s + 1)
            for b in range(B):
                last = v.tensor_tensor(sc[:, b, :], score[:, b, :], ebias[:, :], ALU.add)
            link(last)
            four = sc[:, :, :].rearrange("p b (g e) -> p b g e", e=EG)
            v.tensor_tensor(grp[:, 0, :, :, :], four[:, :, :, 0:2], four[:, :, :, 2:4], ALU.max)
            link(v.tensor_tensor(grp[:, 1, :, :, :], four[:, :, :, 0:2], four[:, :, :, 2:4], ALU.min))
            hi, lo = grp[:, 0], grp[:, 1]
            v.tensor_tensor(grp[:, 2, :, :, 0], hi[:, :, :, 0], hi[:, :, :, 1], ALU.max)
            v.tensor_tensor(grp[:, 2, :, :, 1], hi[:, :, :, 0], hi[:, :, :, 1], ALU.min)
            link(v.tensor_tensor(grp[:, 3, :, :, 0], lo[:, :, :, 0], lo[:, :, :, 1], ALU.max))
            link(v.tensor_tensor(grp[:, 3, :, :, 1], grp[:, 2, :, :, 1], grp[:, 3, :, :, 0], ALU.max))
            link(v.tensor_tensor(gs[:, :, :], grp[:, 2, :, :, 0], grp[:, 3, :, :, 1], ALU.add))
            for b in range(B):
                link(v.max(top[:, b, 0, :], gs[:, b, :]))
                link(v.max_index(topi[:, b, 0, :], top[:, b, 0, :], gs[:, b, :]))
                link(v.tensor_copy(topf[:, b, 0, :], topi[:, b, 0, :]))
            one_hot(gmask, topf, iota_g, 0, TOPG)
            link(v.tensor_tensor(masked[:, :, :].rearrange("p b (g e) -> p b g e", e=EG), four,
                                 gmask[:, :, :].rearrange("p b (g o) -> p b g o", o=1).to_broadcast([P, B, NG, EG]), ALU.mult))
            for b in range(B):
                link(v.max(top[:, b, 1, :], masked[:, b, :]))
                link(v.max_index(topi[:, b, 1, :], top[:, b, 1, :], masked[:, b, :]))
                link(v.tensor_copy(topf[:, b, 1, :], topi[:, b, 1, :]))
            one_hot(picked, topf, iota_e, 1, TOPK)
            link(v.tensor_tensor(weigh[:, :, :], picked[:, :, :], score[:, :, :], ALU.mult))
            dve.sem_inc(score_used, 1)
            link(v.tensor_reduce(wsum[:, :], weigh[:, :, :], AX_X, ALU.add))
            link(v.tensor_scalar(wsum[:, :], wsum[:, :], 1e-20, None, ALU.add))
            link(v.reciprocal(wsum[:, :], wsum[:, :]))
            for b in range(B):
                v.tensor_scalar(route_w[:, b, s, :], weigh[:, b, :], wsum[:, b:b + 1], SCALE, ALU.mult, ALU.mult)
                last = v.tensor_copy(route_m[:, b, s, :], picked[:, b, :])
            link(last)

        dve.wait_ge(consts, 1)
        first_norm(0)
        dve.wait_ge(weights_in, 16 * 4)
        dve.wait_ge(small_in, 16 * SMALL)
        for ct in range(CT):
            last = v.tensor_scalar(wo[:, ct, :], wo[:, ct, :], onw[:, 0:1], None, ALU.mult)
        last.then_inc(wo_scaled, 1)
        for a, w in enumerate((1, 0, 2)):
            conv(a, w, 0)
        for w in (1, 0, 2):
            silu(w, 0)
        turn_beta(0, "begin")
        for a, w in enumerate((1, 0)):
            normalise(a, w, 0)
        turn_v()
        turn_k()
        masks(0, "begin")
        first_norm(1)
        inverse()
        end_steps()

        def body(s, phase):
            turn_beta(s, phase)
            conv(0, 1, s)
            turn_w(s - 1)
            new_values(s - 1, 0)
            conv(1, 0, s)
            next_state(s - 1, 0)
            silu(1, s)
            new_values(s - 1, 1)
            conv(2, 2, s)
            next_state(s - 1, 1)
            silu(0, s)
            new_values(s - 1, 2)
            silu(2, s)
            if phase != "seven":
                first_norm(s + 1)
            next_state(s - 1, 2)
            normalise(0, 1, s)
            new_values(s - 1, 3)
            turn_v()
            next_state(s - 1, 3)
            normalise(1, 0, s)
            turn_k()
            scale_output(s - 1)
            masks(s, phase)
            if phase != "one":
                route(s - 2)
            rows(s - 1, phase)
            inverse()
            end_steps()

        body(1, "one")
        with dve.Fori(LOOP_FROM, LOOP_TO) as s:
            body(s, "loop")
        body(STEPS - 1, "seven")
        turn_w(STEPS - 1)
        for j in range(J):
            new_values(STEPS - 1, j)
            next_state(STEPS - 1, j)
        scale_output(STEPS - 1)
        route(STEPS - 2)
        rows(STEPS - 1, "end")
        route(STEPS - 1)






def expert_part(nc, ctx, dram, wring, route_m, route_w):
    def sb(name, shape, dt=F32):
        return ctx.enter_context(nc.sbuf_tensor(name, shape, dt))

    def sem(name):
        return ctx.enter_context(nc.semaphore(name))

    W_gate, W_up, W_down, x2_d, h_d, acc_d, out = dram
    PARTS = 6
    SLOTS = 8
    TURNS_E = NE // SLOTS
    ZQ = 4
    ZR = STEPS // ZQ
    per_expert = 3 * EI * KT
    more = [sb(f"wring{q}", [P, per_expert]) for q in range(2, SLOTS)]
    slots = [wring[:, q * per_expert:(q + 1) * per_expert] for q in range(2)] + [m[:, :] for m in more]
    w_gate = [w[:, 0:1024].rearrange("p (k i) -> p k i", k=KT) for w in slots]
    w_up = [w[:, 1024:2048].rearrange("p (k i) -> p k i", k=KT) for w in slots]
    w_down = [w[:, 2048:3072].rearrange("p (k d) -> p k d", k=2) for w in slots]

    ident = sb("ident2", [P, P])
    before = sb("before", [P, P], BF16)
    ones = sb("ones", [P, P], BF16)
    mask16 = sb("mask16", [P, NT * NE], BF16)
    place = sb("place", [P, NT, NE])
    carry = sb("carry", [P, NT, NE])
    slot16 = sb("slot16", [P, NE, NT], BF16)
    slots_i = sb("slots_i", [P, CAP], BF16)
    hot = [sb(f"hot{q}", [P, NT, CAP], BF16) for q in range(2)]
    facts = sb("facts", [P, NE, NT, PARTS], BF16)
    rest = sb("rest", [P, NT, NE])
    spare = sb("spare", [P, 1])
    table = sb("table", [P, NE, PARTS])
    row_f = sb("row_f", [P, NE])
    tmp_f = sb("tmp_f", [P, NE])
    row_i = sb("row_i", [P, NE], I32)
    slot_w = sb("slot_w", [P, NE])
    gidx = [sb(f"gidx{q}", [P, 1], I32) for q in range(4)]
    sidx = [sb(f"sidx{q}", [P, 1], I32) for q in range(2)]
    xg = [sb(f"xg{q}", [P, D]) for q in range(4)]
    xgT = [sb(f"xgT{q}", [P, KT, P]) for q in range(2)]
    sg = [sb(f"sg{q}", [P, 2, CAP]) for q in range(2)]
    hid = [sb(f"hid{q}", [P, 2, CAP]) for q in range(2)]
    ys = [sb(f"ys{q}", [P, D]) for q in range(4)]
    r_all = sb("r_all", [P, NT, D])
    a_in = [more[q][:, 0:ZR * B * D].rearrange("p (r b d) -> p r b d", r=ZR, b=B) for q in range(ZQ)]
    z_st = [sb(f"z_st{q}", [P, B, 6]) for q in range(ZQ)]
    z_mv = [sb(f"z_mv{q}", [P, B, 2]) for q in range(ZQ)]
    z_rs = [sb(f"z_rs{q}", [P, B]) for q in range(ZQ)]
    z_shift = [sb(f"z_shift{q}", [P, B]) for q in range(ZQ)]
    eps = sb("eps_last", [P, 1])

    ps_x = [ctx.enter_context(nc.psum_tensor(f"ps_x{q}", [P, 512], F32)) for q in range(2)]
    ps_g = [ctx.enter_context(nc.psum_tensor(f"ps_g{q}", [P, 512], F32)) for q in range(2)]
    ps_y = [ctx.enter_context(nc.psum_tensor(f"ps_y{q}", [P, 512], F32)) for q in range(2)]
    ps_p = ctx.enter_context(nc.psum_tensor("ps_p", [P, 512], F32))
    ps_t = ctx.enter_context(nc.psum_tensor("ps_t", [P, 512], F32))

    filled2 = sem("e_filled")
    consts2 = sem("e_consts")
    mask_ready = sem("mask_ready")
    counted = sem("counted")
    facts_ready = sem("facts_ready")
    hot_ready = sem("hot_ready")
    table_done = sem("table_done")
    rows_ready = sem("rows_ready")
    w_in = [sem(f"w_in{q}") for q in range(SLOTS)]
    gidx_ready = sem("gidx_ready")
    gathered = [sem(f"gathered{q}") for q in range(4)]
    turned = sem("turned")
    xgT_ready = sem("xgT_ready")
    gu_done = sem("gu_done")
    sg_ready = sem("sg_ready")
    gated = sem("gated")
    hid_ready = sem("hid_ready")
    y_done = sem("y_done")
    ys_ready = sem("ys_ready")
    sidx_ready = sem("sidx_ready")
    added = sem("added")
    r_in = sem("r_in")
    z_in = [sem(f"z_in{q}") for q in range(ZQ)]
    z_stats = sem("z_stats")
    z_rstd = sem("z_rstd")
    z_shifts = sem("z_shifts")
    z_norm = sem("z_norm")
    z_first = sem("z_first")
    z_second = sem("z_second")
    z_out = sem("z_out")
    dve_chain = sem("dve_chain")
    act_chain = sem("act_chain")
    pool_passed = sem("pool_passed")

    block = ctx.enter_context(nc.Block())
    PAIRS = NE // 2
    acc_t = acc_d[0:NTOK, :].rearrange("(t b p) d -> t p b d", p=P, b=B)
    out_t = out.rearrange("b (t p) d -> (b t) p d", p=P).rearrange("(t b) p d -> t p b d", b=B)

    def over_experts(eng, step):
        for q in range(SLOTS):
            step(q, q)
        with eng.Fori(1, TURNS_E) as r:
            for q in range(SLOTS):
                step(SLOTS * r + q, q)

    def since(eng, semaphore, e, count, each=1):
        if not (isinstance(e, int) and count <= 0):
            eng.wait_ge(semaphore, each * count)

    @block.sync
    def _(sp):
        def load(e, q):
            since(sp, y_done, e, e - SLOTS + 1)
            sp.dma_start(w_gate[q], W_gate.rearrange("e (p k) i -> e p k i", k=KT)[e]).then_inc(w_in[q], 16)
            sp.dma_start(w_up[q], W_up.rearrange("e (p k) i -> e p k i", k=KT)[e]).then_inc(w_in[q], 16)
            sp.dma_start(w_down[q], W_down.rearrange("e (k p) d -> e p k d", p=P)[e]).then_inc(w_in[q], 16)

        over_experts(sp, load)
        sp.dma_start(r_all[:, :, :], x2_d.rearrange("(t p) d -> p t d", p=P)).then_inc(r_in, 16)

        sp.wait_ge(added, 16 * NE)
        for r in range(ZR):
            for q in range(ZQ):
                if r > 0:
                    sp.wait_ge(z_in[q], 16 * r)
                sp.dma_start(a_in[q][:, r, :, :], acc_t[ZQ * r + q]).then_inc(z_in[q], 16)
        for r in range(ZR):
            for q in range(ZQ):
                n = ZQ * r + q
                sp.wait_ge(z_first, n + 1)
                sp.wait_ge(z_second, n + 1)
                sp.dma_start(out_t[n], a_in[q][:, r, :, :]).then_inc(z_out, 16)
        sp.wait_ge(z_out, 16 * STEPS)

    @block.gpsimd
    def _(pool):
        g = nc.gpsimd
        g.memset(ident[:, :], 0.0)
        g.memset(before[:, :], 1.0)
        g.memset(ones[:, :], 1.0)
        for q in range(2):
            g.memset(xgT[q][:, :, :], 0.0)
        g.memset(eps[:, :], LN_EPS)
        g.memset(carry[:, :, :], 0.0)
        g.memset(facts[:, :, :, 5], 1.0)
        g.iota(slots_i[:, :], pattern=[[1, CAP]], base=0, channel_multiplier=0, allow_small_or_imprecise_dtypes=True)
        g.iota(spare[:, :], pattern=[[0, 1]], base=NTOK, channel_multiplier=1, allow_small_or_imprecise_dtypes=True)
        g.iota(facts[:, :, :, 3], pattern=[[0, NE], [1, NT]], base=0, channel_multiplier=0, allow_small_or_imprecise_dtypes=True)
        g.iota(facts[:, :, :, 4], pattern=[[0, NE], [0, NT]], base=0, channel_multiplier=1, allow_small_or_imprecise_dtypes=True).then_inc(filled2, 1)
        pool.wait_ge(filled2, 1)
        g.affine_select(out=ident[:, :], in_=ident[:, :], compare_op=ALU.not_equal, fill=1.0,
                        base=0, pattern=[[-1, P]], channel_multiplier=1)
        g.affine_select(out=before[:, :], in_=before[:, :], compare_op=ALU.is_gt, fill=0.0,
                        base=0, pattern=[[1, P]], channel_multiplier=-1).then_inc(consts2, 1)

        def gather(e, q):
            since(pool, turned, e, e - 3)
            g.tensor_copy(gidx[q % 4][0:CAP, :], row_i[0:CAP, bass.ds(e, 1)]).then_inc(gidx_ready, 1)
            pool.wait_ge(gidx_ready, e + 1)
            pool.sem_inc(pool_passed, 1)
            g.indirect_dma_start(out=xg[q % 4][0:CAP, :], out_offset=None, in_=h_d[:, :],
                                 in_offset=bass.IndirectOffsetOnAxis(ap=gidx[q % 4][0:CAP, 0:1], axis=0)).then_inc(gathered[q % 4], 16)

        def scatter(e, q):
            g.tensor_copy(sidx[q % 2][0:CAP, :], row_i[0:CAP, bass.ds(e, 1)]).then_inc(sidx_ready, 1)
            pool.wait_ge(sidx_ready, e + 1)
            pool.wait_ge(ys_ready, e + 1)
            since(pool, added, e, e, 16)
            pool.sem_inc(pool_passed, 1)
            g.indirect_dma_start(out=acc_d[:, :], out_offset=bass.IndirectOffsetOnAxis(ap=sidx[q % 2][0:CAP, 0:1], axis=0),
                                 in_=ys[q % 4][0:CAP, :], in_offset=None, compute_op=ALU.add).then_inc(added, 16)

        AHEAD = 3

        def step(e, q):
            gather(e, q)
            if not (isinstance(e, int) and e < AHEAD):
                scatter(e - AHEAD, (q - AHEAD) % SLOTS)

        pool.wait_ge(rows_ready, 1)
        over_experts(pool, step)
        for e in range(NE - AHEAD, NE):
            scatter(e, e % SLOTS)

        for r in range(ZR):
            for q in range(ZQ):
                n = ZQ * r + q
                pool.wait_ge(z_norm, n + 1)
                pool.wait_ge(r_in, 16)
                g.tensor_tensor(a_in[q][:, r, 1, :], a_in[q][:, r, 1, :], r_all[:, 2 * n + 1, :], ALU.add).then_inc(z_second, 1)

    @block.tensor
    def _(pe):
        te = nc.tensor
        pe.wait_ge(consts2, 1)
        pe.wait_ge(mask_ready, 1)
        te.matmul(ps_p[:, :], before[:, :], mask16[:, :], start=True, stop=True)
        te.matmul(ps_t[:, :], ones[:, :], mask16[:, :], start=True, stop=True).then_inc(counted, 1)
        pe.wait_ge(facts_ready, 1)
        with pe.Fori(0, PAIRS) as r:
            for q in range(2):
                pe.wait_ge(hot_ready, 2 * r + q + 1)
                for t in range(NT):
                    m = te.matmul(ps_p[0:CAP, bass.ds(r * 2 * PARTS + q * PARTS, PARTS)], hot[q][:, t, :], facts[:, 2 * r + q, t, :],
                                  start=(t == 0), stop=(t == NT - 1), skip_group_check=True)
                m.then_inc(table_done, 1)

        def turn(e, q):
            x = xg[q % 4][0:CAP, :].rearrange("c (p k) -> c k p", k=KT)
            pe.wait_ge(gathered[q % 4], 16 * (e // 4 + 1) if isinstance(e, int) else 4 * (e - q % 4) + 16)
            since(pe, xgT_ready, e, e - 1)
            for k in range(KT):
                m = te.transpose(ps_x[q % 2][:, k * P:k * P + CAP], x[:, k, :], ident[0:CAP, 0:CAP])
            m.then_inc(turned, 1)

        def gate_up(e, q):
            pe.wait_ge(w_in[q], 48 * (e // SLOTS + 1) if isinstance(e, int) else 6 * (e - q) + 48)
            pe.wait_ge(xgT_ready, e + 1)
            since(pe, hid_ready, e, e - 1)
            for a, w in enumerate((w_gate[q], w_up[q])):
                for i in range(2):
                    for k in range(KT):
                        m = te.matmul(ps_g[q % 2][:, (2 * a + i) * P:(2 * a + i + 1) * P], w[:, k, i * P:(i + 1) * P], xgT[q % 2][:, k, :],
                                      start=(k == 0), stop=(k == KT - 1))
            m.then_inc(gu_done, 1)

        def down(e, q):
            pe.wait_ge(hid_ready, e + 1)
            since(pe, ys_ready, e, e - 1)
            for i in range(2):
                m = te.matmul(ps_y[q % 2][0:CAP, :], hid[q % 2][:, i, :], w_down[q][:, i, :], start=(i == 0), stop=(i == 1))
            m.then_inc(y_done, 1)

        def step(e, q):
            turn(e, q)
            if not (isinstance(e, int) and e < 2):
                down(e - 2, (q - 2) % SLOTS)
            gate_up(e, q)

        over_experts(pe, step)
        down(NE - 2, SLOTS - 2)
        down(NE - 1, SLOTS - 1)

    @block.scalar
    def _(act):
        sc_e = nc.scalar

        def rows(e, q):
            act.wait_ge(turned, e + 1)
            since(act, gu_done, e, e - 1)
            sc_e.activation(xgT[q % 2][:, :, 0:CAP], ps_x[q % 2][:, :].rearrange("p (k c) -> p k c", k=KT)[:, :, 0:CAP], ACT.Copy).then_inc(xgT_ready, 1)

        def gate(e, q):
            act.wait_ge(gu_done, e + 1)
            s = sg[q % 2][:, :, :]
            sc_e.activation(s, ps_g[q % 2][:, 0:2 * P].rearrange("p (i c) -> p i c", i=2)[:, :, 0:CAP], ACT.Exp, scale=-1.0).then_inc(act_chain, 1)
            act.wait_ge(act_chain, 1)
            sc_e.activation(s, s, ACT.Ln, bias=1.0).then_inc(act_chain, 1)
            act.wait_ge(act_chain, 2)
            act.sem_clear(act_chain)
            sc_e.activation(s, s, ACT.Exp, scale=-1.0).then_inc(sg_ready, 1)

        def step(e, q):
            rows(e, q)
            if not (isinstance(e, int) and e < 1):
                gate(e - 1, (q - 1) % SLOTS)

        sc_e.preload_act_table_set("natural_log_exp_and_others")
        act.wait_ge(consts2, 1)
        over_experts(act, step)
        gate(NE - 1, SLOTS - 1)

        def z_inverse(r, q):
            act.wait_ge(z_stats, ZQ * r + q + 1)
            sc_e.activation(z_rs[q][:, :], z_mv[q][:, :, 1], ACT.Ln, bias=eps[:, 0:1]).then_inc(act_chain, 1)
            act.wait_ge(act_chain, 1)
            act.sem_clear(act_chain)
            sc_e.activation(z_rs[q][:, :], z_rs[q][:, :], ACT.Exp, scale=-0.5).then_inc(z_rstd, 1)

        def z_scale(r, q):
            act.wait_ge(z_shifts, ZQ * r + q + 1)
            for b in range(B):
                last = sc_e.activation(a_in[q][:, r, b, :], a_in[q][:, r, b, :], ACT.Identity, bias=z_shift[q][:, b:b + 1], scale=z_rs[q][:, b:b + 1])
            last.then_inc(z_norm, 1)

        for n in range(STEPS):
            z_inverse(n // ZQ, n % ZQ)
            if n > 0:
                z_scale((n - 1) // ZQ, (n - 1) % ZQ)
        z_scale(ZR - 1, ZQ - 1)

    @block.vector
    def _(dve):
        v = nc.vector

        class Steps:
            count = 0

        def link(ins):
            Steps.count += 1
            ins.then_inc(dve_chain, 1)
            dve.wait_ge(dve_chain, Steps.count)

        def end_steps():
            dve.sem_clear(dve_chain)
            Steps.count = 0

        dve.wait_ge(consts2, 1)
        mask = route_m[:, :, :, :].rearrange("p b t e -> p (b t) e")
        w32 = route_w[:, :, :, :].rearrange("p b t e -> p (b t) e")
        v.tensor_copy(mask16[:, :], mask.rearrange("p t e -> p (t e)")).then_inc(mask_ready, 1)
        by_e = facts[:, :, :, :].rearrange("p e t k -> p k t e")
        link(v.tensor_copy(by_e[:, 0], w32))
        link(v.tensor_tensor(rest[:, :, :], w32, by_e[:, 0], ALU.subtract))
        link(v.tensor_copy(by_e[:, 1], rest[:, :, :]))
        link(v.tensor_tensor(rest[:, :, :], rest[:, :, :], by_e[:, 1], ALU.subtract))
        link(v.tensor_copy(by_e[:, 2], rest[:, :, :]))
        dve.sem_inc(facts_ready, 1)
        dve.wait_ge(counted, 1)
        for t in range(1, NT):
            link(v.tensor_tensor(carry[:, t, :], carry[:, t - 1, :], ps_t[:, (t - 1) * NE:t * NE], ALU.add))
        link(v.tensor_tensor(place[:, :, :], ps_p[:, :].rearrange("p (t e) -> p t e", e=NE), carry[:, :, :], ALU.add))
        link(v.tensor_scalar(place[:, :, :], place[:, :, :], float(P - 1), float(P - 1), ALU.min, ALU.subtract))
        link(v.tensor_tensor(place[:, :, :], place[:, :, :], mask, ALU.mult))
        link(v.tensor_scalar(slot16[:, :, :].rearrange("p e t -> p t e"), place[:, :, :], float(P - 1), None, ALU.add))
        end_steps()
        with dve.Fori(0, PAIRS) as r:
            for q in range(2):
                if q == 0:
                    dve.wait_ge(table_done, 2 * r)
                v.tensor_tensor(hot[q][:, :, :], slot16[:, 2 * r + q, :].rearrange("p (t o) -> p t o", o=1).to_broadcast([P, NT, CAP]),
                                slots_i[:, :].rearrange("p (o c) -> p o c", o=1).to_broadcast([P, NT, CAP]), ALU.is_equal).then_inc(hot_ready, 1)
        dve.wait_ge(table_done, NE)
        link(v.tensor_copy(table[0:CAP, :, :], ps_p[0:CAP, 0:NE * PARTS].rearrange("p (e k) -> p e k", k=PARTS)))
        t_ = table[0:CAP, :, :]
        link(v.scalar_tensor_tensor(out=row_f[0:CAP, :], in0=t_[:, :, 3], scalar=float(P), in1=t_[:, :, 4], op0=ALU.mult, op1=ALU.add))
        link(v.tensor_scalar(tmp_f[0:CAP, :], t_[:, :, 5], -1.0, 1.0, ALU.mult, ALU.add))
        link(v.scalar_tensor_tensor(out=row_f[0:CAP, :], in0=tmp_f[0:CAP, :], scalar=spare[0:CAP, 0:1], in1=row_f[0:CAP, :], op0=ALU.mult, op1=ALU.add))
        v.tensor_copy(row_i[0:CAP, :], row_f[0:CAP, :]).then_inc(rows_ready, 1)
        link(v.tensor_tensor(slot_w[0:CAP, :], t_[:, :, 1], t_[:, :, 2], ALU.add))
        link(v.tensor_tensor(slot_w[0:CAP, :], slot_w[0:CAP, :], t_[:, :, 0], ALU.add))
        end_steps()

        def gate(e, q):
            dve.wait_ge(sg_ready, e + 1)
            since(dve, y_done, e, e - 1)
            gates = ps_g[q % 2][:, :].rearrange("p (a i c) -> p a i c", a=2, i=2)[:, :, :, 0:CAP]
            v.tensor_tensor(hid[q % 2][:, :, :], gates[:, 0], sg[q % 2][:, :, :], ALU.mult).then_inc(gated, 1)
            dve.wait_ge(gated, e + 1)
            v.tensor_tensor(hid[q % 2][:, :, :], gates[:, 1], hid[q % 2][:, :, :], ALU.mult).then_inc(hid_ready, 1)

        def weigh(e, q):
            dve.wait_ge(y_done, e + 1)
            since(dve, added, e, e - 3, 16)
            v.tensor_scalar(ys[q % 4][0:CAP, :], ps_y[q % 2][0:CAP, :], slot_w[0:CAP, bass.ds(e, 1)], None, ALU.mult).then_inc(ys_ready, 1)

        def step(e, q):
            if not (isinstance(e, int) and e < 1):
                gate(e - 1, (q - 1) % SLOTS)
            if not (isinstance(e, int) and e < 2):
                weigh(e - 2, (q - 2) % SLOTS)

        over_experts(dve, step)
        gate(NE - 1, SLOTS - 1)
        weigh(NE - 2, SLOTS - 2)
        weigh(NE - 1, SLOTS - 1)

        def z_moments(r, q):
            dve.wait_ge(z_in[q], 16 * (r + 1))
            for b in range(B):
                last = v.bn_stats(z_st[q][:, b, :], a_in[q][:, r, b, :])
            link(last)
            for b in range(B):
                last = v.bn_aggr(z_mv[q][:, b, :], z_st[q][:, b, :])
            last.then_inc(z_stats, 1)

        def z_bias(r, q):
            dve.wait_ge(z_rstd, ZQ * r + q + 1)
            v.scalar_tensor_tensor(out=z_shift[q][:, :], in0=z_mv[q][:, :, 0], scalar=-1.0, in1=z_rs[q][:, :], op0=ALU.mult, op1=ALU.mult).then_inc(z_shifts, 1)

        def z_add(r, q):
            n = ZQ * r + q
            dve.wait_ge(z_norm, n + 1)
            dve.wait_ge(r_in, 16)
            v.tensor_tensor(a_in[q][:, r, 0, :], a_in[q][:, r, 0, :], r_all[:, 2 * n, :], ALU.add).then_inc(z_first, 1)

        for n in range(STEPS):
            z_moments(n // ZQ, n % ZQ)
            z_bias(n // ZQ, n % ZQ)
            if n > 1:
                z_add((n - 2) // ZQ, (n - 2) % ZQ)
        for n in range(STEPS - 2, STEPS):
            z_add(n // ZQ, n % ZQ)


def delta_moe_layer(nc, x, Wq, Wk, Wv, Wb, Wo, conv_q, conv_k, conv_v, onorm_w, router_w, e_bias,
                    W_gate, W_up, W_down, s_gate, s_up, s_down, out):
    x2_d = nc.dram_tensor("x2_rows", [NTOK, D], F32, kind="Internal").ap()
    h_d = nc.dram_tensor("h_rows", [NTOK + CAP, D], F32, kind="Internal").ap()
    acc_d = nc.dram_tensor("moe_rows", [NTOK + CAP, D], F32, kind="Internal").ap()
    with nc.sbuf_tensor("wring", [P, 2 * 3 * 1024], F32) as wring, \
            nc.sbuf_tensor("route_m", [P, B, STEPS, NE], F32) as route_m, \
            nc.sbuf_tensor("route_w", [P, B, STEPS, NE], F32) as route_w:
        with ExitStack() as ctx:
            step_part(nc, ctx, (x, Wq, Wk, Wv, Wb, Wo, conv_q, conv_k, conv_v, onorm_w, router_w, e_bias,
                                W_gate, W_up, W_down, s_gate, s_up, s_down, x2_d, h_d, acc_d), wring, route_m, route_w)
        with ExitStack() as ctx:
            expert_part(nc, ctx, (W_gate, W_up, W_down, x2_d, h_d, acc_d, out), wring, route_m, route_w)


_INS = ["attn_x", "attn_Wq", "attn_Wk", "attn_Wv", "attn_Wb", "attn_Wo", "attn_conv_q", "attn_conv_k", "attn_conv_v",
        "attn_onorm_w", "ffn_router_w", "ffn_e_bias", "ffn_W_gate", "ffn_W_up", "ffn_W_down",
        "ffn_shared_gate", "ffn_shared_up", "ffn_shared_down"]
_TURNED = {"ffn_router_w", "ffn_shared_gate", "ffn_shared_up", "ffn_shared_down"}


def kernel(**inputs):
    import numpy as _np
    import concourse.bacc as _bacc
    from concourse import mybir as _mybir
    from concourse.bass_utils import run_bass_kernel_spmd as _run

    nc = _bacc.Bacc("TRN2", target_bir_lowering=False, num_devices=1)
    arrays, args = {}, []
    for name in _INS:
        a = _np.asarray(inputs["L0_" + name])
        a = _np.ascontiguousarray(a.T if name in _TURNED else a)
        arrays[f"in_{name}"] = a
        args.append(nc.dram_tensor(f"in_{name}", a.shape, _mybir.dt.from_np(a.dtype), kind="ExternalInput").ap())
    out = nc.dram_tensor("out_0", (B, SEQ, D), _mybir.dt.from_np(_np.dtype("float32")), kind="ExternalOutput").ap()
    delta_moe_layer(nc, *args, out)
    r = _run(nc, [arrays], core_ids=[0])
    return r.results[0]["out_0"]
```

```python
from contextlib import ExitStack

import concourse.bass as bass
from concourse import mybir

F32 = mybir.dt.float32
BF16 = mybir.dt.bfloat16
I32 = mybir.dt.int32
U32 = mybir.dt.uint32
ALU = mybir.AluOpType
ACT = mybir.ActivationFunctionType
AX_X = mybir.AxisListType.X

P = 128
B, SEQ, D = 2, 1024, 512
H, DK = 16, 32
TT = 128
STEPS = SEQ // TT
KT = D // P
CT = H * DK // P
HT = P // DK
CH = 32
HB = CH // 2
J = TT // CH
COLS = B * TT
I8 = CT * B
G = I8 * J
TAPS = 4
HALO = TAPS - 1
NE, EI = 32, 256
NG, EG = 8, 4
TOPG, TOPK = 3, 4
SCALE = 2.5
NT = B * STEPS
NTOK = B * SEQ
CAP = -(-5 * NTOK // (4 * NE))
FF = 512
FT = FF // P
LN_EPS, L2_EPS, RMS_EPS = 1e-5, 1e-6, 1e-5

SMALL = 1 + 1 + HT + 3 + 4
RING = 6

SIZE = dict(X=2, P=9, H=2, R=1, U=2, A=2, V=2, E=2, K=2, F=2, Q=2, O=2, G=4, W=2)
LAG = dict(P=0, K=0, Q=0, G=0, X=-1, U=1, A=1, O=1, W=1, H=2, R=2, E=2, F=2, V=3)
ORDER = dict(begin="XPKQGX", one="PUAKQXOGW", two="PHURAEKFQXOGW", loop="PHURAVEKFQXOGW", seven="PHURAVEKFQOGW",
             end="HURAVEFOWVHREFV")
LOOP_FROM, LOOP_TO = 3, STEPS - 1
JOBS = sum(SIZE[c] for c in ORDER["loop"])
assert JOBS % RING == 0
TURNS = JOBS // RING


def first_job(phase, section, nth=0):
    base = 0
    for name, order in ORDER.items():
        if name == phase:
            break
        base += sum(SIZE[c] for c in order) * (LOOP_TO - LOOP_FROM if name == "loop" else 1)
    order = ORDER[phase]
    at = [n for n, c in enumerate(order) if c == section][nth]
    base += sum(SIZE[c] for c in order[:at])
    return base + (LAG[section] - LOOP_FROM) * JOBS if phase == "loop" else base


class Ring:

    def __init__(self, banks, filled, freed):
        self.banks, self.filled, self.freed = banks, filled, freed

    def bank(self, first, n):
        return self.banks[(first + n) % RING]

    def wait_free(self, pe, first, step, n):
        turn = (first + n) // RING
        if isinstance(step, int) and turn + TURNS * step == 0:
            return
        pe.wait_ge(self.freed[(first + n) % RING], step * TURNS + turn)

    def wait_full(self, eng, first, step, n):
        eng.wait_ge(self.filled[(first + n) % RING], step * TURNS + (first + n) // RING + 1)

    def full(self, first, n):
        return self.filled[(first + n) % RING]

    def free(self, first, n):
        return self.freed[(first + n) % RING]


def where(phase, section, step, nth=0):
    return first_job(phase, section, nth), step if phase == "loop" else 0


def step_part(nc, ctx, dram, shared):
    def sb(name, shape, dt=F32):
        return ctx.enter_context(nc.sbuf_tensor(name, shape, dt))

    def sem(name):
        return ctx.enter_context(nc.semaphore(name))

    (x, Wq, Wk, Wv, Wb, Wo, conv_q, conv_k, conv_v, onorm_w, router_w, e_bias,
     s_gate, s_up, s_down, x2_d, h_d, acc_d) = dram
    wring, ident, eps_ln, iota_e = shared["wring"], shared["ident"], shared["eps_ln"], shared["iota_e"]
    before, ones, slots_i, spare, tile_1, token = (shared[n] for n in ("before", "ones", "slots_i", "spare", "tile_1", "token"))
    route_m, route_w, route_k = shared["route_m"], shared["route_w"], shared["route_k"]

    wqkv = wring[:, :].rearrange("p (s k n) -> p s k n", s=3, k=KT)
    wb = sb("wb", [P, KT, H])
    wo = sb("wo", [P, CT, D])
    wr = sb("wr", [P, KT, 4 * NE])
    sg_w = sb("sg_w", [P, KT, FF])
    su_w = sb("su_w", [P, KT, FF])
    sd_w = sb("sd_w", [P, FT, D])
    taps = sb("taps", [P, 3, TAPS])
    onw = sb("onw", [P, 1])
    ebias = sb("ebias", [P, NE])

    heads1 = sb("heads1", [P, P])
    headsm = sb("headsm", [P, P])
    spread = sb("spread", [H, CT, P])
    below = sb("below", [P, CH])
    upto = sb("upto", [P, CH])
    eps_l2 = sb("eps_l2", [P, 1])
    eps_q = sb("eps_q", [P, 1])
    eps_rms = sb("eps_rms", [P, 1])
    iota_g = sb("iota_g", [P, NG])

    x_in = sb("x_in", [P, B, D])
    x_res = sb("x_res", [P, B, D])
    stats = sb("stats", [P, B, 6])
    mv = sb("mv", [P, 3, B, 2])
    rs = sb("rs", [P, 3, B])
    shift = sb("shift", [P, 3, B])
    xnT = sb("xnT", [P, KT, COLS])
    pre = sb("pre", [P, 3, I8, HALO + TT])
    cv = sb("cv", [P, 3, I8, TT])
    sig = sb("sig", [P, 3, I8 * TT])
    b16 = sb("b16", [H, COLS])
    kq = sb("kq", [P, G, 2, CH])
    beta = sb("beta", [P, G, CH])
    mbeta = sb("mbeta", [P, G, CH])
    k_tok = sb("k_tok", [P, G, DK])
    vk = sb("vk", [P, G, 2, DK])
    low = sig[:, 1, :].rearrange("p (g c) -> p g c", g=G)
    prod = sig[:, 0, :]
    low_pad = sb("low_pad", [P, 2, HB * (CH + 1)])
    inv_pad = sb("inv_pad", [P, 2, HB * (CH + 1)])
    lowp, inv = (pad[:, :, :].rearrange("p a r -> p (a r)")[:, 0:CH * CH].rearrange("p (j k) -> p j k", k=CH)
                 for pad in (low_pad, inv_pad))
    low_diag, inv_diag = (pad[:, :, 0:HB * CH].rearrange("p a (j k) -> p a j k", k=CH)[:, :, :, 0:HB]
                          for pad in (low_pad, inv_pad))
    invT = sb("invT", [P, G, CH])
    attnT = sb("attnT", [P, G, CH])
    uw = sb("uw", [P, J, I8, 2, DK])
    wT = sb("wT", [P, J, I8, CH])
    unew = sb("unew", [P, I8, DK])
    state = [sb(f"state{n}", [P, I8, DK]) for n in range(2)]
    o_ch = sb("o_ch", [P, I8, TT])
    o_r = sb("o_r", [P, I8 * TT])
    x2 = sb("x2", [P, B, D])
    h = sb("h", [P, B, D])
    hT = sb("hT", [P, KT, COLS])
    sh_h = sb("sh_h", [P, FT, COLS])
    acc_sb = sb("acc_sb", [P, B, D])
    score = sb("score", [P, B, NE])
    sc = sb("sc", [P, B, NE])
    grp = sb("grp", [P, 4, B, NG, 2])
    gs = sb("gs", [P, B, NG])
    top = sb("top", [P, B, 2, 8])
    topi = sb("topi", [P, B, 2, 8], U32)
    topf = sb("topf", [P, B, 2, 8])
    gmask = sb("gmask", [P, B, NG])
    masked = sb("masked", [P, B, NE])
    picked = sb("picked", [P, B, NE])
    weigh = sb("weigh", [P, B, NE])
    wsum = sb("wsum", [P, B])

    banks = [ctx.enter_context(nc.psum_tensor(f"bank{n}", [P, 512], F32)) for n in range(8)]
    ring = Ring(banks[:RING], [sem(f"filled{n}") for n in range(RING)], [sem(f"freed{n}") for n in range(RING)])
    ps_ws, ps_o = banks[6], banks[7]

    consts = sem("consts")
    consts_go = sem("consts_go")
    first_go = sem("first_go")
    first_consts = sem("first_consts")
    proj_in = [sem(f"proj_in{n}") for n in range(3)]
    weights_in = sem("weights_in")
    small_in = sem("small_in")
    wo_scaled = sem("wo_scaled")
    x_loaded = sem("x_loaded")
    xres_loaded = sem("xres_loaded")
    stats_ready = [sem(f"stats_ready{n}") for n in range(3)]
    shift_ready = [sem(f"shift_ready{n}") for n in range(3)]
    y_scaled = sem("y_scaled")
    rs_ready = [sem(f"rs_ready{n}") for n in range(3)]
    xn_ready = sem("xn_ready")
    xnT_ready = sem("xnT_ready")
    beta_ready = sem("beta_ready")
    pre_ready = [sem(f"pre_ready{n}") for n in range(3)]
    conv_done = [sem(f"conv_done{n}") for n in range(3)]
    sig_ready = [sem(f"sig_ready{n}") for n in range(3)]
    act_ready = [sem(f"act_ready{n}") for n in range(3)]
    sq_ready = [sem(f"sq_ready{n}") for n in range(2)]
    norm_ready = [sem(f"norm_ready{n}") for n in range(2)]
    halo_done = sem("halo_done")
    kq_ready = sem("kq_ready")
    betaT_ready = sem("betaT_ready")
    mbeta_ready = sem("mbeta_ready")
    tok_ready = sem("tok_ready")
    vk_ready = sem("vk_ready")
    gram_read = sem("gram_read")
    inv_ready = sem("inv_ready")
    uw_ready = sem("uw_ready")
    wT_ready = sem("wT_ready")
    ws_done = sem("ws_done")
    unew_ready = sem("unew_ready")
    ds_done = sem("ds_done")
    state_ready = sem("state_ready")
    o_done = sem("o_done")
    o_out = sem("o_out")
    osq_ready = sem("osq_ready")
    onorm_ready = sem("onorm_ready")
    on_ready = sem("on_ready")
    h_ready = sem("h_ready")
    rows_out = sem("rows_out")
    hT_ready = sem("hT_ready")
    gate_sig = sem("gate_sig")
    hid_ready = sem("hid_ready")
    acc_ready = sem("acc_ready")
    acc_out = sem("acc_out")
    score_ready = sem("score_ready")
    score_used = sem("score_used")
    dve_step = sem("dve_step")
    act_step = sem("act_step")
    pe_passed = sem("pe_passed")

    def quad(n):
        return slice(DK * n, DK * n + DK)

    block = ctx.enter_context(nc.Block())

    @block.sync
    def _(sp):
        sp.dma_start(x_in[:, :, :], x[:, 0:TT, :].rearrange("b p d -> p b d")).then_inc(x_loaded, 16)
        small = [(wb[:, :, :], Wb.rearrange("(k p) n -> p k n", p=P)),
                 (ebias[:, :], e_bias.rearrange("(o n) -> o n", o=1).to_broadcast([P, NE]))]
        for n in range(HT):
            small.append((onw[quad(n), :], onorm_w.rearrange("(n o) -> n o", o=1)))
        for n, w in enumerate((conv_q, conv_k, conv_v)):
            small.append((taps[:, n, :], w.rearrange("(o n) -> o n", o=1).to_broadcast([P, TAPS])))
        for n in range(4):
            small.append((wr[:, :, NE * n:NE * n + NE], router_w.rearrange("(k p) e -> p k e", p=P)))
        for dst, src in small:
            sp.dma_start(dst, src).then_inc(small_in, 16)
        for n, w in ((1, Wk), (0, Wq), (2, Wv)):
            sp.dma_start(wqkv[:, n, :, :], w.rearrange("(k p) n -> p k n", p=P)).then_inc(proj_in[n], 16)
        for dst, src in ((wo, Wo), (sg_w, s_gate), (su_w, s_up), (sd_w, s_down)):
            sp.dma_start(dst[:, :, :], src.rearrange("(k p) n -> p k n", p=P)).then_inc(weights_in, 16)
        assert len(small) == SMALL

        def load_x(s):
            sp.wait_ge(xnT_ready, 2 * s)
            sp.dma_start(x_in[:, :, :], x.rearrange("b (t p) d -> t p b d", p=TT)[s]).then_inc(x_loaded, 16)

        def load_residual(s):
            sp.dma_start(x_res[:, :, :], x.rearrange("b (t p) d -> t p b d", p=TT)[s]).then_inc(xres_loaded, 16)

        def rows(s):
            sp.wait_ge(h_ready, s + 1)
            sp.dma_start(x2_d.rearrange("(b t p) d -> t p b d", p=TT, b=B)[s], x2[:, :, :]).then_inc(rows_out, 16)
            sp.dma_start(h_d[0:NTOK, :].rearrange("(b t p) d -> t p b d", p=TT, b=B)[s], h[:, :, :]).then_inc(rows_out, 16)

        def shared_out(s):
            sp.wait_ge(acc_ready, s + 1)
            sp.dma_start(acc_d[0:NTOK, :].rearrange("(b t p) d -> t p b d", p=TT, b=B)[s], acc_sb[:, :, :]).then_inc(acc_out, 16)

        sp.wait_ge(consts, 1)
        sp.dma_start(h_d[NTOK:NTOK + CAP, :], acc_sb[0:CAP, 0, :]).then_inc(acc_out, 16)
        sp.dma_start(acc_d[NTOK:NTOK + CAP, :], acc_sb[0:CAP, 0, :]).then_inc(acc_out, 16)

        load_x(1)
        for n in range(2):
            load_x(n + 2)
            load_residual(n)
            rows(n)
        with sp.Fori(2, STEPS - 2) as s:
            load_x(s + 2)
            load_residual(s)
            shared_out(s - 2)
            rows(s)
        for n in range(STEPS - 2, STEPS):
            load_residual(n)
            shared_out(n - 2)
            rows(n)
        for n in range(STEPS - 2, STEPS):
            shared_out(n)
        sp.wait_ge(rows_out, 32 * STEPS)
        sp.wait_ge(acc_out, 32 + 16 * STEPS)

    @block.gpsimd
    def _(pool):
        g = nc.gpsimd
        g.memset(eps_ln[:, :], LN_EPS)
        g.memset(ident[:, :], 0.0).then_inc(first_go, 1)
        pool.wait_ge(first_go, 1)
        g.affine_select(out=ident[:, :], in_=ident[:, :], compare_op=ALU.not_equal, fill=1.0,
                        base=0, pattern=[[-1, P]], channel_multiplier=1).then_inc(first_consts, 1)
        g.memset(heads1[:, :], 0.0)
        g.memset(headsm[:, :], 0.0)
        g.memset(spread[:, :, :], 1.0)
        g.memset(below[:, :], -1.0)
        g.memset(upto[:, :], 1.0)
        g.memset(inv, 0.0)
        g.memset(pre[:, :, :, 0:HALO], 0.0)
        g.memset(state[0][:, :, :], 0.0)
        g.memset(eps_l2[:, :], L2_EPS)
        g.memset(eps_q[:, :], L2_EPS * DK)
        g.memset(eps_rms[:, :], RMS_EPS)
        g.iota(iota_g[:, :], pattern=[[1, NG]], base=0, channel_multiplier=0, allow_small_or_imprecise_dtypes=True)
        g.iota(iota_e[:, :], pattern=[[1, NE]], base=0, channel_multiplier=0, allow_small_or_imprecise_dtypes=True)
        g.memset(before[:, :], 1.0)
        g.memset(ones[:, :], 1.0)
        g.iota(slots_i[:, :], pattern=[[1, CAP]], base=0, channel_multiplier=0, allow_small_or_imprecise_dtypes=True)
        g.iota(spare[:, :], pattern=[[0, 1]], base=NTOK + P, channel_multiplier=1, allow_small_or_imprecise_dtypes=True)
        g.iota(tile_1[:, :], pattern=[[1, NT]], base=1, channel_multiplier=0, allow_small_or_imprecise_dtypes=True)
        g.iota(token[:, :], pattern=[[0, 1]], base=0, channel_multiplier=1, allow_small_or_imprecise_dtypes=True)
        g.memset(acc_sb[:, :, :], 0.0).then_inc(consts_go, 1)
        pool.wait_ge(consts_go, 1)
        made = [1]

        def alone(ins):
            made[0] += 1
            ins.then_inc(consts_go, 1)
            pool.wait_ge(consts_go, made[0])

        for n in range(HT):
            alone(g.memset(heads1[quad(n), quad(n)], 1.0))
            alone(g.memset(headsm[quad(n), quad(n)], 1.0 / DK))
            alone(g.affine_select(out=below[quad(n), :], in_=below[quad(n), :], compare_op=ALU.is_gt, fill=0.0,
                                  base=0, pattern=[[-1, CH]], channel_multiplier=1))
            alone(g.affine_select(out=upto[quad(n), :], in_=upto[quad(n), :], compare_op=ALU.is_ge, fill=0.0,
                                  base=0, pattern=[[1, CH]], channel_multiplier=-1))
        g.affine_select(out=before[:, :], in_=before[:, :], compare_op=ALU.is_gt, fill=0.0,
                        base=0, pattern=[[1, P]], channel_multiplier=-1)
        g.affine_select(out=inv, in_=inv, compare_op=ALU.not_equal, fill=1.0,
                        base=0, pattern=[[1, CH], [-1, CH]], channel_multiplier=0)
        g.affine_select(out=spread[:, :, :].rearrange("h c (a d) -> h c a d", a=HT),
                        in_=spread[:, :, :].rearrange("h c (a d) -> h c a d", a=HT), compare_op=ALU.is_equal, fill=0.0,
                        base=0, pattern=[[-HT, CT], [-1, HT], [0, DK]], channel_multiplier=1).then_inc(consts, 1)

        def mask_beta(s):
            pool.wait_ge(betaT_ready, s + 1)
            if not (isinstance(s, int) and s == 0):
                pool.wait_ge(gram_read, s)
            g.tensor_tensor(mbeta[:, :, :], beta[:, :, :], below[:, :].rearrange("p (o c) -> p o c", o=1).to_broadcast([P, G, CH]), ALU.mult).then_inc(mbeta_ready, 1)

        def by_beta(s):
            pool.wait_ge(tok_ready, s + 1)
            g.tensor_tensor(vk[:, :, 0, :], vk[:, :, 0, :], beta[:, :, :], ALU.mult)
            g.tensor_tensor(vk[:, :, 1, :], k_tok[:, :, :], beta[:, :, :], ALU.mult).then_inc(vk_ready, 1)

        mask_beta(0)
        by_beta(0)

        def body(s):
            mask_beta(s)
            by_beta(s)

        with pool.Fori(1, STEPS) as s:
            body(s)

    @block.tensor
    def _(pe):
        te = nc.tensor

        def turn_x(s, phase, nth=0):
            first, st = where(phase, "X", s, nth)
            pe.wait_ge(xn_ready, s + 1)
            for n in range(2):
                ring.wait_free(pe, first, st, n)
                bank = ring.bank(first, n)
                for k in range(2):
                    for b in range(B):
                        kt = 2 * n + k
                        m = te.transpose(bank[:, k * COLS + b * TT:k * COLS + (b + 1) * TT], x_in[:, b, kt * P:(kt + 1) * P], ident[:, :])
                m.then_inc(ring.full(first, n), 1)

        def project(s, phase):
            first, st = where(phase, "P", s)

            def start(n):
                ring.wait_free(pe, first, st, n)
                return ring.bank(first, n)

            pe.wait_ge(small_in, 16 * SMALL)
            pe.wait_ge(xnT_ready, 2 * (s + 1))
            bank = start(0)
            for kt in range(KT):
                m = te.matmul(bank[0:H, 0:COLS], wb[:, kt, :], xnT[:, kt, :], start=(kt == 0), stop=(kt == KT - 1))
            m.then_inc(ring.full(first, 0), 1)
            for a, w in enumerate((1, 0, 2)):
                pe.wait_ge(proj_in[w], 16)
                for half in range(2):
                    n = 1 + 2 * a + half
                    bank = start(n)
                    for c in range(2):
                        ct = 2 * half + c
                        for kt in range(KT):
                            m = te.matmul(bank[:, c * COLS:(c + 1) * COLS], wqkv[:, w, kt, ct * P:(ct + 1) * P], xnT[:, kt, :],
                                          start=(kt == 0), stop=(kt == KT - 1))
                    m.then_inc(ring.full(first, n), 1)
            pe.wait_ge(beta_ready, s + 1)
            for half in range(2):
                n = 7 + half
                bank = start(n)
                for c in range(2):
                    m = te.matmul(bank[:, c * COLS:(c + 1) * COLS], spread[:, 2 * half + c, :], b16[:, :], start=True, stop=True)
                m.then_inc(ring.full(first, n), 1)

        def squares(s, phase, a):
            first, st = where(phase, "KQ"[a], s)
            pe.wait_ge(sq_ready[a], s + 1)
            for half in range(2):
                ring.wait_free(pe, first, st, half)
                bank = ring.bank(first, half)
                for c in range(2):
                    m = te.matmul(bank[:, c * COLS:(c + 1) * COLS], heads1[:, :], sig[:, a, (2 * half + c) * COLS:(2 * half + c + 1) * COLS],
                                  start=True, stop=True)
                m.then_inc(ring.full(first, half), 1)

        def gram(s, phase):
            first, st = where(phase, "G", s)
            pe.wait_ge(kq_ready, 2 * (s + 1))
            for j in range(J):
                ring.wait_free(pe, first, st, j)
                bank = ring.bank(first, j)
                pe.sem_inc(pe_passed, 1)
                for i in range(I8):
                    for hh in range(HT):
                        m = te.matmul(bank[quad(hh), i * 64:(i + 1) * 64], kq[quad(hh), i * J + j, 0, :], kq[quad(hh), i * J + j, :, :].rearrange("p a c -> p (a c)"),
                                      start=True, stop=True)
                m.then_inc(ring.full(first, j), 1)

        def u_and_w(s, phase, part):
            first, st = where(phase, "UA"[part], s)
            pe.wait_ge(inv_ready, s + 1)
            pe.wait_ge(vk_ready, s + 1)
            for n in range(J // 2):
                j = part * J // 2 + n
                ring.wait_free(pe, first, st, n)
                bank = ring.bank(first, n)
                pe.sem_inc(pe_passed, 1)
                for i in range(I8):
                    for hh in range(HT):
                        m = te.matmul(bank[quad(hh), i * 64:(i + 1) * 64], invT[quad(hh), i * J + j, :], vk[quad(hh), i * J + j, :, :].rearrange("p a c -> p (a c)"),
                                      start=True, stop=True)
                m.then_inc(ring.full(first, n), 1)

        def between(n, phase, core_of):
            here = core_of + 1
            if phase in ("loop", "seven", "end") and n < 4:
                shared_down(here - 3, phase, n // 2, n % 2)
            if phase != "one" and n in (4, 5, 6, 7):
                shared_up(here - 2, phase, "E", (n - 4) // 2, (n - 4) % 2)
            if phase != "one" and n in (9, 10, 11, 12):
                shared_up(here - 2, phase, "F", (n - 9) // 2, (n - 9) % 2)
            if phase != "end" and n in (8, 13):
                squares(here, phase, 0 if n == 8 else 1)

        def core(s, phase):
            for j in range(J):
                now = state[j % 2]
                pe.wait_ge(wT_ready, J * s + j + 1)
                if not (isinstance(s, int) and s == 0 and j == 0):
                    pe.wait_ge(state_ready, J * s + j)
                pe.sem_inc(pe_passed, 1)
                for i in range(I8):
                    for hh in range(HT):
                        m = te.matmul(ps_ws[quad(hh), i * DK:(i + 1) * DK], wT[quad(hh), j, i, :], now[quad(hh), i, :], start=True, stop=True)
                m.then_inc(ws_done, 1)
                between(4 * j, phase, s)
                if not (isinstance(s, int) and s == 0 and j == 0):
                    pe.wait_ge(o_out, J * s + j)
                pe.sem_inc(pe_passed, 1)
                for i in range(I8):
                    for hh in range(HT):
                        te.matmul(ps_o[quad(hh), i * CH:(i + 1) * CH], now[quad(hh), i, :], kq[quad(hh), i * J + j, 1, :],
                                  start=(i == 0), stop=False, skip_group_check=True)
                between(4 * j + 1, phase, s)
                pe.wait_ge(unew_ready, J * s + j + 1)
                pe.sem_inc(pe_passed, 1)
                for i in range(I8):
                    for hh in range(HT):
                        m = te.matmul(ps_ws[quad(hh), 256 + i * DK:256 + (i + 1) * DK], k_tok[quad(hh), i * J + j, :], unew[quad(hh), i, :], start=True, stop=True,
                                      skip_group_check=True)
                m.then_inc(ds_done, 1)
                between(4 * j + 2, phase, s)
                pe.sem_inc(pe_passed, 1)
                for i in range(I8):
                    for hh in range(HT):
                        m = te.matmul(ps_o[quad(hh), i * CH:(i + 1) * CH], unew[quad(hh), i, :], attnT[quad(hh), i * J + j, :],
                                      start=False, stop=(i == I8 - 1), skip_group_check=True)
                m.then_inc(o_done, 1)
                between(4 * j + 3, phase, s)

        def output_squares(s, phase):
            first, st = where(phase, "O", s)
            pe.wait_ge(osq_ready, s + 1)
            for half in range(2):
                ring.wait_free(pe, first, st, half)
                bank = ring.bank(first, half)
                for c in range(2):
                    m = te.matmul(bank[:, c * COLS:(c + 1) * COLS], headsm[:, :], o_r[:, (2 * half + c) * COLS:(2 * half + c + 1) * COLS], start=True, stop=True)
                m.then_inc(ring.full(first, half), 1)

        def out_proj(s, phase):
            first, st = where(phase, "W", s)
            pe.wait_ge(on_ready, s + 1)
            pe.wait_ge(wo_scaled, 1)
            for b in range(B):
                ring.wait_free(pe, first, st, b)
                bank = ring.bank(first, b)
                for ct in range(CT):
                    m = te.matmul(bank[:, :], o_ch[:, ct * B + b, :], wo[:, ct, :], start=(ct == 0), stop=(ct == CT - 1))
                m.then_inc(ring.full(first, b), 1)

        def turn_h(s, phase, nth=0):
            first, st = where(phase, "H", s, nth)
            pe.wait_ge(h_ready, s + 1)
            for n in range(2):
                ring.wait_free(pe, first, st, n)
                bank = ring.bank(first, n)
                for k in range(2):
                    for b in range(B):
                        kt = 2 * n + k
                        m = te.transpose(bank[:, k * COLS + b * TT:k * COLS + (b + 1) * TT], h[:, b, kt * P:(kt + 1) * P], ident[:, :])
                m.then_inc(ring.full(first, n), 1)

        def router(s, phase, nth=0):
            first, st = where(phase, "R", s, nth)
            pe.wait_ge(hT_ready, 2 * (s + 1))
            ring.wait_free(pe, first, st, 0)
            bank = ring.bank(first, 0)
            for b in range(B):
                for kt in range(KT):
                    m = te.matmul(bank[:, b * P:(b + 1) * P], hT[:, kt, b * TT:(b + 1) * TT], wr[:, kt, :], start=(kt == 0), stop=(kt == KT - 1))
            m.then_inc(ring.full(first, 0), 1)

        def shared_up(s, phase, section, a, c, nth=0):
            first, st = where(phase, section, s, nth)
            half, w = "EF".index(section), (sg_w, su_w)[a]
            if c == 0:
                pe.wait_ge(weights_in, 16 * 4)
                ring.wait_free(pe, first, st, a)
            bank = ring.bank(first, a)
            ft = 2 * half + c
            for kt in range(KT):
                m = te.matmul(bank[:, c * COLS:(c + 1) * COLS], w[:, kt, ft * P:(ft + 1) * P], hT[:, kt, :], start=(kt == 0), stop=(kt == KT - 1))
            if c == 1:
                m.then_inc(ring.full(first, a), 1)

        def shared_down(s, phase, b, half, nth=0):
            first, st = where(phase, "V", s, nth)
            if half == 0:
                pe.wait_ge(hid_ready, s + 1)
                ring.wait_free(pe, first, st, b)
            bank = ring.bank(first, b)
            for ft in range(2 * half, 2 * half + 2):
                m = te.matmul(bank[:, :], sh_h[:, ft, b * TT:(b + 1) * TT], sd_w[:, ft, :], start=(ft == 0), stop=(ft == FT - 1))
            if half == 1:
                m.then_inc(ring.full(first, b), 1)

        pe.wait_ge(first_consts, 1)
        turn_x(0, "begin")
        pe.wait_ge(consts, 1)
        project(0, "begin")
        squares(0, "begin", 0)
        squares(0, "begin", 1)
        gram(0, "begin")
        turn_x(1, "begin", nth=1)

        def body(s, phase):
            project(s, phase)
            if phase != "one":
                turn_h(s - 2, phase)
            u_and_w(s - 1, phase, 0)
            if phase != "one":
                router(s - 2, phase)
            u_and_w(s - 1, phase, 1)
            core(s - 1, phase)
            if phase != "seven":
                turn_x(s + 1, phase)
            output_squares(s - 1, phase)
            gram(s, phase)
            out_proj(s - 1, phase)

        body(1, "one")
        body(2, "two")
        with pe.Fori(LOOP_FROM, LOOP_TO) as s:
            body(s, "loop")
        body(STEPS - 1, "seven")
        turn_h(STEPS - 2, "end")
        u_and_w(STEPS - 1, "end", 0)
        router(STEPS - 2, "end")
        u_and_w(STEPS - 1, "end", 1)
        core(STEPS - 1, "end")
        output_squares(STEPS - 1, "end")
        out_proj(STEPS - 1, "end")
        for n in range(4):
            shared_down(STEPS - 2, "end", n // 2, n % 2, nth=1)
        turn_h(STEPS - 1, "end", nth=1)
        router(STEPS - 1, "end", nth=1)
        for section in "EF":
            for n in range(4):
                shared_up(STEPS - 1, "end", section, n // 2, n % 2, nth=1)
        for n in range(4):
            shared_down(STEPS - 1, "end", n // 2, n % 2, nth=2)

    @block.scalar
    def _(act):
        sc_e = nc.scalar

        class Steps:
            count = 0

        def link(ins):
            Steps.count += 1
            ins.then_inc(act_step, 1)
            act.wait_ge(act_step, Steps.count)

        def end_steps():
            act.sem_clear(act_step)
            Steps.count = 0

        def rstd(n, s):
            act.wait_ge(stats_ready[n], s + 1)
            link(sc_e.activation(rs[:, n, :], mv[:, n, :, 1], ACT.Ln, bias=eps_ln[:, 0:1]))
            sc_e.activation(rs[:, n, :], rs[:, n, :], ACT.Exp, scale=-0.5).then_inc(rs_ready[n], 1)

        def sigmoid(dst, src, done=None):
            link(sc_e.activation(dst, src, ACT.Exp, scale=-1.0))
            link(sc_e.activation(dst, dst, ACT.Ln, bias=1.0))
            return sc_e.activation(dst, dst, ACT.Exp, scale=-1.0)

        def release(first, n):
            act.sem_inc(ring.free(first, n), 1)

        def take_x(s, phase, nth=0):
            first, st = where(phase, "X", s, nth)
            for n in range(2):
                ring.wait_full(act, first, st, n)
                link(sc_e.activation(xnT[:, 2 * n:2 * n + 2, :], ring.bank(first, n)[:, :].rearrange("p (k c) -> p k c", k=2), ACT.Copy))
                release(first, n)
                act.sem_inc(xnT_ready, 1)

        def take_beta(s, phase):
            first, st = where(phase, "P", s)
            ring.wait_full(act, first, st, 0)
            link(sc_e.activation(b16[:, :], ring.bank(first, 0)[0:H, 0:COLS], ACT.Exp, scale=-1.0))
            release(first, 0)
            link(sc_e.activation(b16[:, :], b16[:, :], ACT.Ln, bias=1.0))
            sc_e.activation(b16[:, :], b16[:, :], ACT.Exp, scale=-1.0).then_inc(beta_ready, 1)

        def take_projection(s, phase, a, w):
            first, st = where(phase, "P", s)
            if not (isinstance(s, int) and s == 0):
                act.wait_ge(halo_done, 3 * (s - 1) + a + 1)
            for half in range(2):
                n = 1 + 2 * a + half
                ring.wait_full(act, first, st, n)
                link(sc_e.activation(pre[:, w, 4 * half:4 * half + 4, HALO:], ring.bank(first, n)[:, :].rearrange("p (i t) -> p i t", t=TT), ACT.Copy))
                release(first, n)
            act.sem_inc(pre_ready[w], 1)

        def silu_factor(s, w):
            act.wait_ge(conv_done[w], s + 1)
            slot = (1, 0, 2)[w]
            sigmoid(sig[:, slot, :], cv[:, w, :, :].rearrange("p i t -> p (i t)")).then_inc(sig_ready[w], 1)

        def square(s, a, w):
            act.wait_ge(act_ready[w], s + 1)
            sc_e.activation(sig[:, a, :], cv[:, w, :, :].rearrange("p i t -> p (i t)"), ACT.Square).then_inc(sq_ready[a], 1)

        def norms(s, phase, a):
            first, st = where(phase, "KQ"[a], s)
            for half in range(2):
                n = half
                part = sig[:, a, half * 512:(half + 1) * 512]
                ring.wait_full(act, first, st, n)
                link(sc_e.activation(part, ring.bank(first, n)[:, :], ACT.Ln, bias=(eps_l2, eps_q)[a][:, 0:1], scale=(1.0, float(DK))[a]))
                release(first, n)
                link(sc_e.activation(part, part, ACT.Exp, scale=-0.5))
            act.sem_inc(norm_ready[a], 1)

        def take_uw(s, phase, part):
            first, st = where(phase, "UA"[part], s)
            for n in range(J // 2):
                j = part * J // 2 + n
                ring.wait_full(act, first, st, n)
                link(sc_e.activation(uw[:, j, :, :, :].rearrange("p i a d -> p (i a d)"), ring.bank(first, n)[:, :], ACT.Copy))
                release(first, n)
                act.sem_inc(uw_ready, 1)

        def take_output(s, j):
            act.wait_ge(o_done, J * s + j + 1)
            link(sc_e.activation(o_ch[:, :, j * CH:(j + 1) * CH], ps_o[:, 0:I8 * CH].rearrange("p (i c) -> p i c", c=CH), ACT.Copy))
            act.sem_inc(o_out, 1)

        def square_output():
            sc_e.activation(o_r[:, :], o_ch[:, :, :].rearrange("p i t -> p (i t)"), ACT.Square).then_inc(osq_ready, 1)

        def output_norm(s, phase):
            first, st = where(phase, "O", s)
            ring.wait_full(act, first, st, 1)
            for half in range(2):
                part = o_r[:, half * 512:(half + 1) * 512]
                ring.wait_full(act, first, st, half)
                link(sc_e.activation(part, ring.bank(first, half)[:, :], ACT.Ln, bias=eps_rms[:, 0:1]))
                release(first, half)
                link(sc_e.activation(part, part, ACT.Exp, scale=-0.5))
            act.sem_inc(onorm_ready, 1)

        def take_h(s, phase, nth=0):
            first, st = where(phase, "H", s, nth)
            for n in range(2):
                ring.wait_full(act, first, st, n)
                link(sc_e.activation(hT[:, 2 * n:2 * n + 2, :], ring.bank(first, n)[:, :].rearrange("p (k c) -> p k c", k=2), ACT.Copy))
                release(first, n)
                act.sem_inc(hT_ready, 1)

        def take_scores(s, phase, nth=0):
            first, st = where(phase, "R", s, nth)
            ring.wait_full(act, first, st, 0)
            if not (isinstance(s, int) and s == 0):
                act.wait_ge(score_used, s)
            link(sc_e.activation(score[:, :, :], ring.bank(first, 0)[:, 0:B * P].rearrange("p (b e) -> p b e", b=B)[:, :, 0:NE], ACT.Exp, scale=-1.0))
            release(first, 0)
            link(sc_e.activation(score[:, :, :], score[:, :, :], ACT.Ln, bias=1.0))
            sc_e.activation(score[:, :, :], score[:, :, :], ACT.Exp, scale=-1.0).then_inc(score_ready, 1)

        def scale_y(s, phase):
            first, st = where(phase, "W", s)
            act.wait_ge(shift_ready[1], s + 1)
            if not (isinstance(s, int) and s == 0):
                act.wait_ge(rows_out, 32 * s)
            for b in range(B):
                link(sc_e.activation(x2[:, b, :], ring.bank(first, b)[:, :], ACT.Identity, bias=shift[:, 1, b:b + 1], scale=rs[:, 1, b:b + 1]))
                release(first, b)
            act.sem_inc(y_scaled, 1)

        def scale_h(s):
            act.wait_ge(shift_ready[2], s + 1)
            for b in range(B):
                last = sc_e.activation(h[:, b, :], x2[:, b, :], ACT.Identity, bias=shift[:, 2, b:b + 1], scale=rs[:, 2, b:b + 1])
            last.then_inc(h_ready, 1)

        def gate_factor(s, phase, half, nth=0):
            first, st = where(phase, "EF"[half], s, nth)
            ring.wait_full(act, first, st, 0)
            sigmoid(sh_h[:, 2 * half:2 * half + 2, :], ring.bank(first, 0)[:, :].rearrange("p (f c) -> p f c", f=2)).then_inc(gate_sig, 1)

        def take_shared(s, phase, b, nth=0):
            first, st = where(phase, "V", s, nth)
            if b == 0:
                act.wait_ge(acc_out, 32 + 16 * s)
            ring.wait_full(act, first, st, b)
            link(sc_e.activation(acc_sb[:, b, :], ring.bank(first, b)[:, :], ACT.Copy))
            release(first, b)
            if b == B - 1:
                act.sem_inc(acc_ready, 1)

        sc_e.preload_act_table_set("natural_log_exp_and_others")
        act.wait_ge(first_consts, 1)
        rstd(0, 0)
        take_x(0, "begin")
        act.wait_ge(consts, 1)
        take_beta(0, "begin")
        for a, w in enumerate((1, 0, 2)):
            take_projection(0, "begin", a, w)
        for a, w in enumerate((1, 0)):
            silu_factor(0, w)
            square(0, a, w)
        silu_factor(0, 2)
        for a in range(2):
            norms(0, "begin", a)
        rstd(0, 1)
        take_x(1, "begin", nth=1)
        end_steps()

        def body(s, phase):
            take_beta(s, phase)
            for a, w in enumerate((1, 0, 2)):
                take_projection(s, phase, a, w)
            if phase != "one":
                take_h(s - 2, phase)
            take_uw(s - 1, phase, 0)
            if phase != "one":
                take_scores(s - 2, phase)
            take_uw(s - 1, phase, 1)
            silu_factor(s, 1)
            if phase in ("loop", "seven"):
                take_shared(s - 3, phase, 0)
            silu_factor(s, 0)
            if phase in ("loop", "seven"):
                take_shared(s - 3, phase, 1)
            square(s, 0, 1)
            take_output(s - 1, 0)
            if phase != "one":
                gate_factor(s - 2, phase, 0)
            silu_factor(s, 2)
            square(s, 1, 0)
            take_output(s - 1, 1)
            norms(s, phase, 0)
            if phase != "one":
                gate_factor(s - 2, phase, 1)
            if phase != "seven":
                rstd(0, s + 1)
            take_output(s - 1, 2)
            norms(s, phase, 1)
            take_output(s - 1, 3)
            square_output()
            if phase != "seven":
                take_x(s + 1, phase)
            output_norm(s - 1, phase)
            rstd(1, s - 1)
            scale_y(s - 1, phase)
            rstd(2, s - 1)
            scale_h(s - 1)
            end_steps()

        body(1, "one")
        body(2, "two")
        with act.Fori(LOOP_FROM, LOOP_TO) as s:
            body(s, "loop")
        body(STEPS - 1, "seven")
        take_h(STEPS - 2, "end")
        take_uw(STEPS - 1, "end", 0)
        take_scores(STEPS - 2, "end")
        take_uw(STEPS - 1, "end", 1)
        for b in range(B):
            take_shared(STEPS - 3, "end", b)
        take_output(STEPS - 1, 0)
        gate_factor(STEPS - 2, "end", 0)
        take_output(STEPS - 1, 1)
        gate_factor(STEPS - 2, "end", 1)
        take_output(STEPS - 1, 2)
        take_output(STEPS - 1, 3)
        square_output()
        output_norm(STEPS - 1, "end")
        rstd(1, STEPS - 1)
        scale_y(STEPS - 1, "end")
        rstd(2, STEPS - 1)
        scale_h(STEPS - 1)
        for b in range(B):
            take_shared(STEPS - 2, "end", b, nth=1)
        take_h(STEPS - 1, "end", nth=1)
        take_scores(STEPS - 1, "end", nth=1)
        for half in range(2):
            gate_factor(STEPS - 1, "end", half, nth=1)
        for b in range(B):
            take_shared(STEPS - 1, "end", b, nth=2)

    @block.vector
    def _(dve):
        v = nc.vector

        class Steps:
            count = 0

        def link(ins):
            Steps.count += 1
            ins.then_inc(dve_step, 1)
            dve.wait_ge(dve_step, Steps.count)

        def end_steps():
            dve.sem_clear(dve_step)
            Steps.count = 0

        def flat(ap):
            return ap.rearrange("p i t -> p (i t)")

        def moments(n, s, srcs):
            for b in range(B):
                last = v.bn_stats(stats[:, b, :], srcs[b])
            link(last)
            for b in range(B):
                last = v.bn_aggr(mv[:, n, b, :], stats[:, b, :])
            last.then_inc(stats_ready[n], 1)

        def first_norm(s):
            dve.wait_ge(x_loaded, 16 * (s + 1))
            moments(0, s, [x_in[:, b, :] for b in range(B)])
            dve.wait_ge(rs_ready[0], s + 1)
            for b in range(B):
                last = v.tensor_scalar(x_in[:, b, :], x_in[:, b, :], mv[:, 0, b, 0:1], rs[:, 0, b:b + 1], ALU.subtract, ALU.mult)
            last.then_inc(xn_ready, 1)

        def conv(a, w, s):
            dve.wait_ge(pre_ready[w], s + 1)
            out = cv[:, w, :, :]
            link(v.tensor_scalar(out, pre[:, w, :, 0:TT], taps[:, w, 0:1], None, ALU.mult))
            for n in range(1, TAPS):
                link(v.scalar_tensor_tensor(out=out, in0=pre[:, w, :, n:n + TT], scalar=taps[:, w, n:n + 1], in1=out, op0=ALU.mult, op1=ALU.add))
            dve.sem_inc(conv_done[w], 1)
            link(v.tensor_copy(pre[:, w, :, 0:HALO], pre[:, w, :, TT:TT + HALO]))
            dve.sem_inc(halo_done, 1)

        def silu(w, s):
            slot = (1, 0, 2)[w]
            dve.wait_ge(sig_ready[w], s + 1)
            link(v.tensor_tensor(flat(cv[:, w, :, :]), flat(cv[:, w, :, :]), sig[:, slot, :], ALU.mult))
            dve.sem_inc(act_ready[w], 1)

        def normalise(a, w, s):
            dve.wait_ge(norm_ready[a], s + 1)
            link(v.tensor_tensor(kq[:, :, a, :], flat(cv[:, w, :, :]).rearrange("p (g c) -> p g c", c=CH), sig[:, a, :].rearrange("p (g c) -> p g c", c=CH), ALU.mult))
            dve.sem_inc(kq_ready, 1)

        def turn_beta(s, phase):
            first, st = where(phase, "P", s)
            if not (isinstance(s, int) and s == 0):
                dve.wait_ge(vk_ready, s)
            for half in range(2):
                n = 7 + half
                ring.wait_full(dve, first, st, n)
                link(v.transpose(beta[:, half * 16:(half + 1) * 16, :].rearrange("p g c -> p (g c)"), ring.bank(first, n)[:, :]))
                dve.sem_inc(ring.free(first, n), 1)
            dve.sem_inc(betaT_ready, 1)

        def turn_v():
            link(v.transpose(vk[:, :, 0, :], flat(cv[:, 2, :, :]).rearrange("p (g c) -> p g c", c=CH)))

        def turn_k():
            link(v.transpose(k_tok[:, :, :], kq[:, :, 0, :]))
            dve.sem_inc(tok_ready, 1)

        def masks(s, phase):
            first, st = where(phase, "G", s)
            dve.wait_ge(mbeta_ready, s + 1)
            for j in range(J):
                ring.wait_full(dve, first, st, j)
                bank = ring.bank(first, j)[:, :].rearrange("p (i a c) -> p i a c", i=I8, a=2)
                v.tensor_tensor(low.rearrange("p (i j) c -> p j i c", j=J)[:, j], bank[:, :, 0, :], mbeta[:, :, :].rearrange("p (i j) c -> p j i c", j=J)[:, j], ALU.mult)
                link(v.tensor_tensor(attnT[:, :, :].rearrange("p (i j) c -> p j i c", j=J)[:, j], bank[:, :, 1, :],
                                     upto[:, :].rearrange("p (o c) -> p o c", o=1).to_broadcast([P, I8, CH]), ALU.mult))
                dve.sem_inc(ring.free(first, j), 1)
            dve.sem_inc(gram_read, 1)

        def problems():
            link(v.transpose(lowp.rearrange("p c m -> p m c"), low.rearrange("p g m -> p m g")))

        def inverse_diagonal():
            by_column = inv_diag.rearrange("p a j k -> p a k j")
            for i in range(1, HB):
                t = prod[:, 0:2 * i * i].rearrange("p (a k j) -> p a k j", a=2, k=i)
                link(v.tensor_tensor(t, by_column[:, :, 0:i, 0:i], low_diag[:, :, i:i + 1, 0:i].to_broadcast([P, 2, i, i]), ALU.mult))
                link(v.tensor_reduce(inv_diag[:, :, i, 0:i], t, AX_X, ALU.add))

        def product(out, left, right, rows, cols, inner):
            t = prod[:, 0:rows * cols * inner].rearrange("p (i k j) -> p i k j", i=rows, k=cols)
            link(v.tensor_tensor(t, left.rearrange("p i (o j) -> p i o j", o=1).to_broadcast([P, rows, cols, inner]),
                                 right.rearrange("p j (o k) -> p o k j", o=1).to_broadcast([P, rows, cols, inner]), ALU.mult))
            link(v.tensor_reduce(out, t, AX_X, ALU.add))

        def below_times_first(n):
            r0, nr, c0, nc_ = ((0, 8, 0, 8), (8, 8, 0, 8), (0, 16, 8, 8))[n]
            product(lowp[:, r0:r0 + nr, HB + c0:HB + c0 + nc_], lowp[:, HB + r0:HB + r0 + nr, c0:HB], inv[:, c0:HB, c0:c0 + nc_], nr, nc_, HB - c0)

        def second_times(n):
            r0, nr, nj = ((0, 8, 8), (8, 4, 16), (12, 4, 16))[n]
            product(inv[:, HB + r0:HB + r0 + nr, 0:HB], inv[:, HB + r0:HB + r0 + nr, HB:HB + nj], lowp[:, 0:nj, HB:CH], nr, HB, nj)

        def inverse_by_token():
            link(v.transpose(invT[:, :, :].rearrange("p g c -> p c g"), inv))
            dve.sem_inc(inv_ready, 1)

        def hidden(s, phase, half, nth=0):
            first, st = where(phase, "EF"[half], s, nth)
            out = sh_h[:, 2 * half:2 * half + 2, :].rearrange("p f c -> p (f c)")
            dve.wait_ge(gate_sig, 2 * s + half + 1)
            link(v.tensor_tensor(out, ring.bank(first, 0)[:, :], out, ALU.mult))
            dve.sem_inc(ring.free(first, 0), 1)
            ring.wait_full(dve, first, st, 1)
            link(v.tensor_tensor(out, ring.bank(first, 1)[:, :], out, ALU.mult))
            dve.sem_inc(ring.free(first, 1), 1)
            if half == 1:
                dve.sem_inc(hid_ready, 1)

        def turn_w(s):
            for j in range(J):
                dve.wait_ge(uw_ready, J * s + j + 1)
                v.transpose(wT[:, j, :, :], uw[:, j, :, 1, :]).then_inc(wT_ready, 1)

        def new_values(s, j):
            dve.wait_ge(ws_done, J * s + j + 1)
            v.tensor_tensor(unew[:, :, :], uw[:, j, :, 0, :], ps_ws[:, 0:256].rearrange("p (i d) -> p i d", d=DK), ALU.subtract).then_inc(unew_ready, 1)

        def next_state(s, j):
            now, new = state[j % 2], state[(j + 1) % 2]
            dve.wait_ge(ds_done, J * s + j + 1)
            v.tensor_tensor(new[:, :, :], now[:, :, :], ps_ws[:, 256:512].rearrange("p (i d) -> p i d", d=DK), ALU.add).then_inc(state_ready, 1)

        def scale_output(s):
            dve.wait_ge(onorm_ready, s + 1)
            v.tensor_tensor(flat(o_ch[:, :, :]), flat(o_ch[:, :, :]), o_r[:, :], ALU.mult).then_inc(on_ready, 1)

        def rows_moments(s, phase):
            first, st = where(phase, "W", s)
            for b in range(B):
                ring.wait_full(dve, first, st, b)
            moments(1, s, [ring.bank(first, b)[:, :] for b in range(B)])

        def mean_shift(n, s):
            dve.wait_ge(rs_ready[n], s + 1)
            v.scalar_tensor_tensor(out=shift[:, n, :], in0=mv[:, n, :, 0], scalar=-1.0, in1=rs[:, n, :], op0=ALU.mult, op1=ALU.mult).then_inc(shift_ready[n], 1)

        def rows_residual(s):
            dve.wait_ge(y_scaled, s + 1)
            dve.wait_ge(xres_loaded, 16 * (s + 1))
            link(v.tensor_tensor(x2[:, :, :], x2[:, :, :], x_res[:, :, :], ALU.add))
            moments(2, s, [x2[:, b, :] for b in range(B)])

        def one_hot(dst, index, iota, n, count):
            for b in range(B):
                for k in range(count):
                    if k == 0:
                        link(v.tensor_scalar(dst[:, b, :], iota[:, :], index[:, b, n, k:k + 1], None, ALU.is_equal))
                    else:
                        link(v.scalar_tensor_tensor(out=dst[:, b, :], in0=iota[:, :], scalar=index[:, b, n, k:k + 1], in1=dst[:, b, :], op0=ALU.is_equal, op1=ALU.add))

        def route_groups(s):
            dve.wait_ge(score_ready, s + 1)
            for b in range(B):
                last = v.tensor_tensor(sc[:, b, :], score[:, b, :], ebias[:, :], ALU.add)
            link(last)
            four = sc[:, :, :].rearrange("p b (g e) -> p b g e", e=EG)
            v.tensor_tensor(grp[:, 0, :, :, :], four[:, :, :, 0:2], four[:, :, :, 2:4], ALU.max)
            link(v.tensor_tensor(grp[:, 1, :, :, :], four[:, :, :, 0:2], four[:, :, :, 2:4], ALU.min))
            hi, lo = grp[:, 0], grp[:, 1]
            v.tensor_tensor(grp[:, 2, :, :, 0], hi[:, :, :, 0], hi[:, :, :, 1], ALU.max)
            v.tensor_tensor(grp[:, 2, :, :, 1], hi[:, :, :, 0], hi[:, :, :, 1], ALU.min)
            link(v.tensor_tensor(grp[:, 3, :, :, 0], lo[:, :, :, 0], lo[:, :, :, 1], ALU.max))
            link(v.tensor_tensor(grp[:, 3, :, :, 1], grp[:, 2, :, :, 1], grp[:, 3, :, :, 0], ALU.max))
            link(v.tensor_tensor(gs[:, :, :], grp[:, 2, :, :, 0], grp[:, 3, :, :, 1], ALU.add))
            for b in range(B):
                link(v.max(top[:, b, 0, :], gs[:, b, :]))
                link(v.max_index(topi[:, b, 0, :], top[:, b, 0, :], gs[:, b, :]))
                link(v.tensor_copy(topf[:, b, 0, :], topi[:, b, 0, :]))
            one_hot(gmask, topf, iota_g, 0, TOPG)
            link(v.tensor_tensor(masked[:, :, :].rearrange("p b (g e) -> p b g e", e=EG), four,
                                 gmask[:, :, :].rearrange("p b (g o) -> p b g o", o=1).to_broadcast([P, B, NG, EG]), ALU.mult))

        def route_experts(s):
            for b in range(B):
                link(v.max(top[:, b, 1, :], masked[:, b, :]))
                link(v.max_index(topi[:, b, 1, :], top[:, b, 1, :], masked[:, b, :]))
                link(v.tensor_copy(topf[:, b, 1, :], topi[:, b, 1, :]))
            one_hot(picked, topf, iota_e, 1, TOPK)
            link(v.tensor_tensor(weigh[:, :, :], picked[:, :, :], score[:, :, :], ALU.mult))
            dve.sem_inc(score_used, 1)
            link(v.tensor_reduce(wsum[:, :], weigh[:, :, :], AX_X, ALU.add))
            link(v.tensor_scalar(wsum[:, :], wsum[:, :], 1e-20, None, ALU.add))
            link(v.reciprocal(wsum[:, :], wsum[:, :]))
            for b in range(B):
                v.tensor_scalar(route_w[:, b, s, :], weigh[:, b, :], wsum[:, b:b + 1], SCALE, ALU.mult, ALU.mult)
                v.tensor_copy(route_m[:, b, s, :], picked[:, b, :])
                last = v.tensor_copy(route_k[:, b, s, :], topf[:, b, 1, 0:TOPK])
            link(last)

        first_norm(0)
        dve.wait_ge(consts, 1)
        dve.wait_ge(small_in, 16 * SMALL)
        for a, w in enumerate((1, 0, 2)):
            conv(a, w, 0)
        for w in (1, 0, 2):
            silu(w, 0)
        turn_beta(0, "begin")
        for a, w in enumerate((1, 0)):
            normalise(a, w, 0)
        turn_v()
        turn_k()
        masks(0, "begin")
        first_norm(1)
        dve.wait_ge(weights_in, 16 * 4)
        for ct in range(CT):
            last = v.tensor_scalar(wo[:, ct, :], wo[:, ct, :], onw[:, 0:1], None, ALU.mult)
        last.then_inc(wo_scaled, 1)
        problems()
        inverse_diagonal()
        for n in range(3):
            below_times_first(n)
        for n in range(3):
            second_times(n)
        inverse_by_token()
        end_steps()

        def body(s, phase):
            turn_beta(s, phase)
            conv(0, 1, s)
            turn_w(s - 1)
            new_values(s - 1, 0)
            conv(1, 0, s)
            next_state(s - 1, 0)
            silu(1, s)
            if phase != "one":
                route_groups(s - 2)
            new_values(s - 1, 1)
            conv(2, 2, s)
            next_state(s - 1, 1)
            silu(0, s)
            if phase != "one":
                route_experts(s - 2)
            new_values(s - 1, 2)
            silu(2, s)
            if phase != "one":
                hidden(s - 2, phase, 0)
            next_state(s - 1, 2)
            normalise(0, 1, s)
            if phase != "seven":
                first_norm(s + 1)
            new_values(s - 1, 3)
            turn_v()
            next_state(s - 1, 3)
            if phase != "one":
                hidden(s - 2, phase, 1)
            normalise(1, 0, s)
            turn_k()
            scale_output(s - 1)
            masks(s, phase)
            problems()
            inverse_diagonal()
            rows_moments(s - 1, phase)
            below_times_first(0)
            mean_shift(1, s - 1)
            below_times_first(1)
            rows_residual(s - 1)
            below_times_first(2)
            mean_shift(2, s - 1)
            second_times(0)
            second_times(1)
            second_times(2)
            inverse_by_token()
            end_steps()

        body(1, "one")
        body(2, "two")
        with dve.Fori(LOOP_FROM, LOOP_TO) as s:
            body(s, "loop")
        body(STEPS - 1, "seven")
        turn_w(STEPS - 1)
        for j in range(J):
            new_values(STEPS - 1, j)
            if j == 1:
                route_groups(STEPS - 2)
            if j == 2:
                hidden(STEPS - 2, "end", 0)
            next_state(STEPS - 1, j)
            if j == 1:
                route_experts(STEPS - 2)
        hidden(STEPS - 2, "end", 1)
        scale_output(STEPS - 1)
        rows_moments(STEPS - 1, "end")
        mean_shift(1, STEPS - 1)
        rows_residual(STEPS - 1)
        mean_shift(2, STEPS - 1)
        route_groups(STEPS - 1)
        route_experts(STEPS - 1)
        for half in range(2):
            hidden(STEPS - 1, "end", half, nth=1)


def expert_part(nc, ctx, dram, shared):
    def sb(name, shape, dt=F32):
        return ctx.enter_context(nc.sbuf_tensor(name, shape, dt))

    def sem(name):
        return ctx.enter_context(nc.semaphore(name))

    W_gate, W_up, W_down, x2_d, h_d, acc_d, out = dram
    wring, ident, eps, iota_e = shared["wring"], shared["ident"], shared["eps_ln"], shared["iota_e"]
    before, ones, slots_i, spare, tile_1, token = (shared[n] for n in ("before", "ones", "slots_i", "spare", "tile_1", "token"))
    route_m, route_w, route_k = shared["route_m"], shared["route_w"], shared["route_k"]
    FACTS = 5
    QT = NT // 4
    SLOTS = 8
    TURNS_E = NE // SLOTS
    FIRST = 4
    ZQ = 4
    ZR = STEPS // ZQ
    per_expert = 3 * EI * KT
    more = [sb(f"wring{q}", [P, per_expert]) for q in range(2, SLOTS)]
    slots = [wring[:, q * per_expert:(q + 1) * per_expert] for q in range(2)] + [m[:, :] for m in more]
    w_gate = [w[:, 0:1024].rearrange("p (k i) -> p k i", k=KT) for w in slots]
    w_up = [w[:, 1024:2048].rearrange("p (k i) -> p k i", k=KT) for w in slots]
    w_down = [w[:, 2048:3072].rearrange("p (k d) -> p k d", k=2) for w in slots]

    pick_of = sb("pick_of", [P, NT, TOPK, NE], BF16)
    w_part = sb("w_part", [P, 3, NT, NE], BF16)
    rest = sb("rest", [P, NT, NE])
    fact = sb("fact", [P, NT, TOPK, FACTS, NE], BF16)
    place = sb("place", [P, NT, NE])
    chosen = sb("chosen", [P, NT, TOPK, NE])
    slot = sb("slot", [P, NT, TOPK])
    at_slot = sb("at_slot", [P, NT, TOPK, CAP], BF16)
    table = sb("table", [P, FACTS, NE])
    row_f = sb("row_f", [P, NE])
    tmp_f = sb("tmp_f", [P, NE])
    row_i = sb("row_i", [P, NE], I32)
    slot_w = sb("slot_w", [P, NE])
    gidx = [sb(f"gidx{q}", [P, 1], I32) for q in range(4)]
    sidx = [sb(f"sidx{q}", [P, 1], I32) for q in range(2)]
    xg = [sb(f"xg{q}", [P, D]) for q in range(4)]
    xgT = [sb(f"xgT{q}", [P, KT, P]) for q in range(2)]
    sg = [sb(f"sg{q}", [P, 2, CAP]) for q in range(2)]
    hid = [sb(f"hid{q}", [P, 2, CAP]) for q in range(2)]
    ys = [sb(f"ys{q}", [P, D]) for q in range(4)]
    r_all = sb("r_all", [P, NT, D])
    a_in = [more[q][:, 0:ZR * B * D].rearrange("p (r b d) -> p r b d", r=ZR, b=B) for q in range(ZQ)]
    z_st = [sb(f"z_st{q}", [P, B, 6]) for q in range(ZQ)]
    z_mv = [sb(f"z_mv{q}", [P, B, 2]) for q in range(ZQ)]
    z_rs = [sb(f"z_rs{q}", [P, B]) for q in range(ZQ)]
    z_shift = [sb(f"z_shift{q}", [P, B]) for q in range(ZQ)]

    ps_x = [ctx.enter_context(nc.psum_tensor(f"ps_x{q}", [P, 512], F32)) for q in range(2)]
    ps_g = [ctx.enter_context(nc.psum_tensor(f"ps_g{q}", [P, 512], F32)) for q in range(2)]
    ps_y = [ctx.enter_context(nc.psum_tensor(f"ps_y{q}", [P, 512], F32)) for q in range(2)]
    ps_p = ctx.enter_context(nc.psum_tensor("ps_p", [P, 512], F32))
    ps_t = ctx.enter_context(nc.psum_tensor("ps_t", [P, 512], F32))

    padded = sem("padded")
    counted = sem("counted")
    picks_ready = sem("picks_ready")
    tile_facts = sem("tile_facts")
    token_facts = sem("token_facts")
    facts_ready = sem("facts_ready")
    slots_ready = sem("slots_ready")
    table_done = sem("table_done")
    rows_ready = sem("rows_ready")
    w_in = [sem(f"w_in{q}") for q in range(SLOTS)]
    gidx_ready = sem("gidx_ready")
    gathered = [sem(f"gathered{q}") for q in range(4)]
    turned = sem("turned")
    xgT_ready = sem("xgT_ready")
    gu_done = sem("gu_done")
    sg_ready = sem("sg_ready")
    gated = sem("gated")
    hid_ready = sem("hid_ready")
    y_done = sem("y_done")
    ys_ready = sem("ys_ready")
    sidx_ready = sem("sidx_ready")
    added = sem("added")
    r_in = sem("r_in")
    z_in = [sem(f"z_in{q}") for q in range(ZQ)]
    z_stats = sem("z_stats")
    z_rstd = sem("z_rstd")
    z_shifts = sem("z_shifts")
    z_norm = sem("z_norm")
    z_first = sem("z_first")
    z_second = sem("z_second")
    z_out = sem("z_out")
    dve_chain = sem("dve_chain")
    act_chain = sem("act_chain")
    pool_passed = sem("pool_passed")

    block = ctx.enter_context(nc.Block())
    acc_t = acc_d[0:NTOK, :].rearrange("(t b p) d -> t p b d", p=P, b=B)
    out_t = out.rearrange("b (t p) d -> (b t) p d", p=P).rearrange("(t b) p d -> t p b d", b=B)

    def over_experts(eng, step):
        for q in range(SLOTS):
            step(q, q)
        with eng.Fori(1, TURNS_E) as r:
            for q in range(SLOTS):
                step(SLOTS * r + q, q)

    def since(eng, semaphore, e, count, each=1):
        if not (isinstance(e, int) and count <= 0):
            eng.wait_ge(semaphore, each * count)

    @block.sync
    def _(sp):
        def load(e, q):
            since(sp, y_done, e, e - SLOTS + 1)
            if isinstance(e, int) and e == FIRST:
                for n in range(FIRST):
                    sp.wait_ge(gathered[n], 16)
            sp.dma_start(w_gate[q], W_gate.rearrange("e (p k) i -> e p k i", k=KT)[e]).then_inc(w_in[q], 16)
            sp.dma_start(w_up[q], W_up.rearrange("e (p k) i -> e p k i", k=KT)[e]).then_inc(w_in[q], 16)
            sp.dma_start(w_down[q], W_down.rearrange("e (k p) d -> e p k d", p=P)[e]).then_inc(w_in[q], 16)

        over_experts(sp, load)
        sp.dma_start(r_all[:, :, :], x2_d.rearrange("(t p) d -> p t d", p=P)).then_inc(r_in, 16)

        sp.wait_ge(added, 16 * NE)
        for r in range(ZR):
            for q in range(ZQ):
                if r > 0:
                    sp.wait_ge(z_in[q], 16 * r)
                sp.dma_start(a_in[q][:, r, :, :], acc_t[ZQ * r + q]).then_inc(z_in[q], 16)
        for r in range(ZR):
            for q in range(ZQ):
                n = ZQ * r + q
                sp.wait_ge(z_first, n + 1)
                sp.wait_ge(z_second, n + 1)
                sp.dma_start(out_t[n], a_in[q][:, r, :, :]).then_inc(z_out, 16)
        sp.wait_ge(z_out, 16 * STEPS)

    @block.gpsimd
    def _(pool):
        g = nc.gpsimd
        for q in range(2):
            ins = g.memset(xgT[q][:, :, :], 0.0)
        ins.then_inc(padded, 1)
        pool.wait_ge(picks_ready, 1)
        g.tensor_tensor(fact[:, :, :, 3, :], pick_of[:, :, :, :],
                        tile_1[:, :].rearrange("p (t a b) -> p t a b", a=1, b=1).to_broadcast([P, NT, TOPK, NE]), ALU.mult).then_inc(tile_facts, 1)

        def gather(e, q):
            since(pool, turned, e, e - 3)
            g.tensor_copy(gidx[q % 4][0:CAP, :], row_i[0:CAP, bass.ds(e, 1)]).then_inc(gidx_ready, 1)
            pool.wait_ge(gidx_ready, e + 1)
            pool.sem_inc(pool_passed, 1)
            g.indirect_dma_start(out=xg[q % 4][0:CAP, :], out_offset=None, in_=h_d[:, :],
                                 in_offset=bass.IndirectOffsetOnAxis(ap=gidx[q % 4][0:CAP, 0:1], axis=0)).then_inc(gathered[q % 4], 16)

        def scatter(e, q):
            g.tensor_copy(sidx[q % 2][0:CAP, :], row_i[0:CAP, bass.ds(e, 1)]).then_inc(sidx_ready, 1)
            pool.wait_ge(sidx_ready, e + 1)
            pool.wait_ge(ys_ready, e + 1)
            since(pool, added, e, e, 16)
            pool.sem_inc(pool_passed, 1)
            g.indirect_dma_start(out=acc_d[:, :], out_offset=bass.IndirectOffsetOnAxis(ap=sidx[q % 2][0:CAP, 0:1], axis=0),
                                 in_=ys[q % 4][0:CAP, :], in_offset=None, compute_op=ALU.add).then_inc(added, 16)

        AHEAD = 3

        def step(e, q):
            gather(e, q)
            if not (isinstance(e, int) and e < AHEAD):
                scatter(e - AHEAD, (q - AHEAD) % SLOTS)

        pool.wait_ge(rows_ready, 1)
        over_experts(pool, step)
        for e in range(NE - AHEAD, NE):
            scatter(e, e % SLOTS)

        for r in range(ZR):
            for q in range(ZQ):
                n = ZQ * r + q
                pool.wait_ge(z_norm, n + 1)
                pool.wait_ge(r_in, 16)
                g.tensor_tensor(a_in[q][:, r, 1, :], a_in[q][:, r, 1, :], r_all[:, 2 * n + 1, :], ALU.add).then_inc(z_second, 1)

    @block.tensor
    def _(pe):
        te = nc.tensor
        masks = route_m[:, :, :, :].rearrange("p b t e -> p (b t e)")
        te.matmul(ps_p[:, :], before[:, :], masks, start=True, stop=False, skip_group_check=True)
        for n in range(1, NT):
            m = te.matmul(ps_p[:, n * NE:], ones[:, :], masks[:, 0:(NT - n) * NE], start=False, stop=(n == NT - 1), skip_group_check=True)
        m.then_inc(counted, 1)
        pe.wait_ge(facts_ready, 1)
        pe.wait_ge(tile_facts, 1)
        pe.wait_ge(token_facts, 1)
        for t in range(NT):
            if t % QT == 0:
                pe.wait_ge(slots_ready, t // QT + 1)
            for k in range(TOPK):
                m = te.matmul(ps_t[0:CAP, 0:FACTS * NE], at_slot[:, t, k, :], fact[:, t, k, :, :].rearrange("p f e -> p (f e)"),
                              start=(t == 0 and k == 0), stop=(t == NT - 1 and k == TOPK - 1))
        m.then_inc(table_done, 1)

        def turn(e, q):
            x = xg[q % 4][0:CAP, :].rearrange("c (p k) -> c k p", k=KT)
            pe.wait_ge(gathered[q % 4], 16 * (e // 4 + 1) if isinstance(e, int) else 4 * (e - q % 4) + 16)
            since(pe, xgT_ready, e, e - 1)
            for k in range(KT):
                m = te.transpose(ps_x[q % 2][:, k * P:k * P + CAP], x[:, k, :], ident[0:CAP, 0:CAP])
            m.then_inc(turned, 1)

        def gate_up(e, q):
            pe.wait_ge(w_in[q], 48 * (e // SLOTS + 1) if isinstance(e, int) else 6 * (e - q) + 48)
            pe.wait_ge(xgT_ready, e + 1)
            since(pe, hid_ready, e, e - 1)
            for a, w in enumerate((w_gate[q], w_up[q])):
                for i in range(2):
                    for k in range(KT):
                        m = te.matmul(ps_g[q % 2][:, (2 * a + i) * P:(2 * a + i + 1) * P], w[:, k, i * P:(i + 1) * P], xgT[q % 2][:, k, :],
                                      start=(k == 0), stop=(k == KT - 1))
            m.then_inc(gu_done, 1)

        def down(e, q):
            pe.wait_ge(hid_ready, e + 1)
            since(pe, ys_ready, e, e - 1)
            for i in range(2):
                m = te.matmul(ps_y[q % 2][0:CAP, :], hid[q % 2][:, i, :], w_down[q][:, i, :], start=(i == 0), stop=(i == 1))
            m.then_inc(y_done, 1)

        def step(e, q):
            turn(e, q)
            if not (isinstance(e, int) and e < 2):
                down(e - 2, (q - 2) % SLOTS)
            gate_up(e, q)

        over_experts(pe, step)
        down(NE - 2, SLOTS - 2)
        down(NE - 1, SLOTS - 1)

    @block.scalar
    def _(act):
        sc_e = nc.scalar

        def rows(e, q):
            act.wait_ge(turned, e + 1)
            since(act, gu_done, e, e - 1)
            sc_e.activation(xgT[q % 2][:, :, 0:CAP], ps_x[q % 2][:, :].rearrange("p (k c) -> p k c", k=KT)[:, :, 0:CAP], ACT.Copy).then_inc(xgT_ready, 1)

        def gate(e, q):
            act.wait_ge(gu_done, e + 1)
            s = sg[q % 2][:, :, :]
            sc_e.activation(s, ps_g[q % 2][:, 0:2 * P].rearrange("p (i c) -> p i c", i=2)[:, :, 0:CAP], ACT.Exp, scale=-1.0).then_inc(act_chain, 1)
            act.wait_ge(act_chain, 1)
            sc_e.activation(s, s, ACT.Ln, bias=1.0).then_inc(act_chain, 1)
            act.wait_ge(act_chain, 2)
            act.sem_clear(act_chain)
            sc_e.activation(s, s, ACT.Exp, scale=-1.0).then_inc(sg_ready, 1)

        def step(e, q):
            rows(e, q)
            if not (isinstance(e, int) and e < 1):
                gate(e - 1, (q - 1) % SLOTS)

        sc_e.preload_act_table_set("natural_log_exp_and_others")
        act.wait_ge(picks_ready, 1)
        sc_e.activation(fact[:, :, :, 4, :], pick_of[:, :, :, :], ACT.Copy, scale=token[:, 0:1]).then_inc(token_facts, 1)
        act.wait_ge(padded, 1)
        over_experts(act, step)
        gate(NE - 1, SLOTS - 1)

        def z_inverse(r, q):
            act.wait_ge(z_stats, ZQ * r + q + 1)
            sc_e.activation(z_rs[q][:, :], z_mv[q][:, :, 1], ACT.Ln, bias=eps[:, 0:1]).then_inc(act_chain, 1)
            act.wait_ge(act_chain, 1)
            act.sem_clear(act_chain)
            sc_e.activation(z_rs[q][:, :], z_rs[q][:, :], ACT.Exp, scale=-0.5).then_inc(z_rstd, 1)

        def z_scale(r, q):
            act.wait_ge(z_shifts, ZQ * r + q + 1)
            for b in range(B):
                last = sc_e.activation(a_in[q][:, r, b, :], a_in[q][:, r, b, :], ACT.Identity, bias=z_shift[q][:, b:b + 1], scale=z_rs[q][:, b:b + 1])
            last.then_inc(z_norm, 1)

        for n in range(STEPS):
            z_inverse(n // ZQ, n % ZQ)
            if n > 0:
                z_scale((n - 1) // ZQ, (n - 1) % ZQ)
        z_scale(ZR - 1, ZQ - 1)

    @block.vector
    def _(dve):
        v = nc.vector

        class Steps:
            count = 0

        def link(ins):
            Steps.count += 1
            ins.then_inc(dve_chain, 1)
            dve.wait_ge(dve_chain, Steps.count)

        def end_steps():
            dve.sem_clear(dve_chain)
            Steps.count = 0

        w32 = route_w[:, :, :, :].rearrange("p b t e -> p (b t) e")
        picks = route_k[:, :, :, :].rearrange("p b t k -> p (b t) k")

        def over_picks(ap):
            return ap.rearrange("p t (o e) -> p t o e", o=1).to_broadcast([P, NT, TOPK, NE])

        v.tensor_tensor(pick_of[:, :, :, :], picks.rearrange("p t (k o) -> p t k o", o=1).to_broadcast([P, NT, TOPK, NE]),
                        iota_e[:, :].rearrange("p (a b e) -> p a b e", a=1, b=1).to_broadcast([P, NT, TOPK, NE]), ALU.is_equal).then_inc(picks_ready, 1)
        link(v.tensor_copy(w_part[:, 0], w32))
        link(v.tensor_tensor(rest[:, :, :], w32, w_part[:, 0], ALU.subtract))
        link(v.tensor_copy(w_part[:, 1], rest[:, :, :]))
        link(v.tensor_tensor(rest[:, :, :], rest[:, :, :], w_part[:, 1], ALU.subtract))
        link(v.tensor_copy(w_part[:, 2], rest[:, :, :]))
        dve.wait_ge(counted, 1)
        link(v.tensor_scalar(place[:, :, :], ps_p[:, :].rearrange("p (t e) -> p t e", e=NE), float(P - 1), None, ALU.min))
        link(v.tensor_tensor(chosen[:, :, :, :], pick_of[:, :, :, :], over_picks(place[:, :, :]), ALU.mult))
        link(v.tensor_reduce(slot[:, :, :], chosen[:, :, :, :], AX_X, ALU.add))
        for n in range(3):
            last = v.tensor_tensor(fact[:, :, :, n, :], pick_of[:, :, :, :], over_picks(w_part[:, n]), ALU.mult)
        last.then_inc(facts_ready, 1)
        for n in range(NT // QT):
            part = slice(n * QT, (n + 1) * QT)
            v.tensor_tensor(at_slot[:, part, :, :], slot[:, part, :].rearrange("p t (k o) -> p t k o", o=1).to_broadcast([P, QT, TOPK, CAP]),
                            slots_i[:, :].rearrange("p (a b c) -> p a b c", a=1, b=1).to_broadcast([P, QT, TOPK, CAP]), ALU.is_equal).then_inc(slots_ready, 1)
        dve.wait_ge(table_done, 1)
        link(v.tensor_copy(table[0:CAP, :, :], ps_t[0:CAP, 0:FACTS * NE].rearrange("p (f e) -> p f e", e=NE)))
        t_ = table[0:CAP, :, :]
        link(v.scalar_tensor_tensor(out=row_f[0:CAP, :], in0=t_[:, 3, :], scalar=float(P), in1=t_[:, 4, :], op0=ALU.mult, op1=ALU.add))
        link(v.tensor_scalar(tmp_f[0:CAP, :], t_[:, 3, :], 0.0, None, ALU.is_equal))
        link(v.scalar_tensor_tensor(out=row_f[0:CAP, :], in0=tmp_f[0:CAP, :], scalar=spare[0:CAP, 0:1], in1=row_f[0:CAP, :], op0=ALU.mult, op1=ALU.add))
        v.tensor_scalar(row_i[0:CAP, :], row_f[0:CAP, :], float(-P), None, ALU.add).then_inc(rows_ready, 1)
        link(v.tensor_tensor(slot_w[0:CAP, :], t_[:, 1, :], t_[:, 2, :], ALU.add))
        link(v.tensor_tensor(slot_w[0:CAP, :], slot_w[0:CAP, :], t_[:, 0, :], ALU.add))
        end_steps()

        def gate(e, q):
            dve.wait_ge(sg_ready, e + 1)
            since(dve, y_done, e, e - 1)
            gates = ps_g[q % 2][:, :].rearrange("p (a i c) -> p a i c", a=2, i=2)[:, :, :, 0:CAP]
            v.tensor_tensor(hid[q % 2][:, :, :], gates[:, 0], sg[q % 2][:, :, :], ALU.mult).then_inc(gated, 1)
            dve.wait_ge(gated, e + 1)
            v.tensor_tensor(hid[q % 2][:, :, :], gates[:, 1], hid[q % 2][:, :, :], ALU.mult).then_inc(hid_ready, 1)

        def weigh(e, q):
            dve.wait_ge(y_done, e + 1)
            since(dve, added, e, e - 3, 16)
            v.tensor_scalar(ys[q % 4][0:CAP, :], ps_y[q % 2][0:CAP, :], slot_w[0:CAP, bass.ds(e, 1)], None, ALU.mult).then_inc(ys_ready, 1)

        def step(e, q):
            if not (isinstance(e, int) and e < 1):
                gate(e - 1, (q - 1) % SLOTS)
            if not (isinstance(e, int) and e < 2):
                weigh(e - 2, (q - 2) % SLOTS)

        over_experts(dve, step)
        gate(NE - 1, SLOTS - 1)
        weigh(NE - 2, SLOTS - 2)
        weigh(NE - 1, SLOTS - 1)

        def z_moments(r, q):
            dve.wait_ge(z_in[q], 16 * (r + 1))
            for b in range(B):
                last = v.bn_stats(z_st[q][:, b, :], a_in[q][:, r, b, :])
            link(last)
            for b in range(B):
                last = v.bn_aggr(z_mv[q][:, b, :], z_st[q][:, b, :])
            last.then_inc(z_stats, 1)

        def z_bias(r, q):
            dve.wait_ge(z_rstd, ZQ * r + q + 1)
            v.scalar_tensor_tensor(out=z_shift[q][:, :], in0=z_mv[q][:, :, 0], scalar=-1.0, in1=z_rs[q][:, :], op0=ALU.mult, op1=ALU.mult).then_inc(z_shifts, 1)

        def z_add(r, q):
            n = ZQ * r + q
            dve.wait_ge(z_norm, n + 1)
            dve.wait_ge(r_in, 16)
            v.tensor_tensor(a_in[q][:, r, 0, :], a_in[q][:, r, 0, :], r_all[:, 2 * n, :], ALU.add).then_inc(z_first, 1)

        for n in range(STEPS + 3):
            if n < STEPS:
                z_moments(n // ZQ, n % ZQ)
            if 1 <= n <= STEPS:
                z_bias((n - 1) // ZQ, (n - 1) % ZQ)
            if n >= 3:
                z_add((n - 3) // ZQ, (n - 3) % ZQ)


def delta_moe_layer(nc, x, Wq, Wk, Wv, Wb, Wo, conv_q, conv_k, conv_v, onorm_w, router_w, e_bias,
                    W_gate, W_up, W_down, s_gate, s_up, s_down, out):
    x2_d = nc.dram_tensor("x2_rows", [NTOK, D], F32, kind="Internal").ap()
    h_d = nc.dram_tensor("h_rows", [NTOK + CAP, D], F32, kind="Internal").ap()
    acc_d = nc.dram_tensor("moe_rows", [NTOK + CAP, D], F32, kind="Internal").ap()
    with ExitStack() as both:
        def sb(name, shape, dt=F32):
            return both.enter_context(nc.sbuf_tensor(name, shape, dt))

        shared = dict(
            wring=sb("wring", [P, 2 * 3 * 1024]),
            route_m=sb("route_m", [P, B, STEPS, NE], BF16),
            route_w=sb("route_w", [P, B, STEPS, NE]),
            route_k=sb("route_k", [P, B, STEPS, TOPK]),
            ident=sb("ident", [P, P]),
            eps_ln=sb("eps_ln", [P, 1]),
            iota_e=sb("iota_e", [P, NE]),
            before=sb("before", [P, P], BF16),
            ones=sb("ones", [P, P], BF16),
            slots_i=sb("slots_i", [P, CAP]),
            spare=sb("spare", [P, 1]),
            tile_1=sb("tile_1", [P, NT]),
            token=sb("token", [P, 1]))
        with ExitStack() as ctx:
            step_part(nc, ctx, (x, Wq, Wk, Wv, Wb, Wo, conv_q, conv_k, conv_v, onorm_w, router_w, e_bias,
                                s_gate, s_up, s_down, x2_d, h_d, acc_d), shared)
        with ExitStack() as ctx:
            expert_part(nc, ctx, (W_gate, W_up, W_down, x2_d, h_d, acc_d, out), shared)


_INS = ["attn_x", "attn_Wq", "attn_Wk", "attn_Wv", "attn_Wb", "attn_Wo", "attn_conv_q", "attn_conv_k", "attn_conv_v",
        "attn_onorm_w", "ffn_router_w", "ffn_e_bias", "ffn_W_gate", "ffn_W_up", "ffn_W_down",
        "ffn_shared_gate", "ffn_shared_up", "ffn_shared_down"]
_TURNED = {"ffn_router_w", "ffn_shared_gate", "ffn_shared_up", "ffn_shared_down"}


def kernel(**inputs):
    import numpy as _np
    import concourse.bacc as _bacc
    from concourse import mybir as _mybir
    from concourse.bass_utils import run_bass_kernel_spmd as _run

    nc = _bacc.Bacc("TRN2", target_bir_lowering=False, num_devices=1)
    arrays, args = {}, []
    for name in _INS:
        a = _np.asarray(inputs["L0_" + name])
        a = _np.ascontiguousarray(a.T if name in _TURNED else a)
        arrays[f"in_{name}"] = a
        args.append(nc.dram_tensor(f"in_{name}", a.shape, _mybir.dt.from_np(a.dtype), kind="ExternalInput").ap())
    out = nc.dram_tensor("out_0", (B, SEQ, D), _mybir.dt.from_np(_np.dtype("float32")), kind="ExternalOutput").ap()
    delta_moe_layer(nc, *args, out)
    r = _run(nc, [arrays], core_ids=[0])
    return r.results[0]["out_0"]
```
